# Optimizing a Trainium2 kernel written in Bass

```python
import numpy as np
import jax
import jax.numpy as jnp

def _softmax(x, axis=-1):
    return jax.nn.softmax(x, axis=axis)

def _gelu(x):
    return jax.nn.gelu(x, approximate=True)

def _silu(x):
    return jax.nn.silu(x)

def _sigmoid(x):
    return jax.nn.sigmoid(x)

def _layernorm(x, axis=-1, eps=1e-05):
    m = jnp.mean(x, axis=axis, keepdims=True)
    v = jnp.var(x, axis=axis, keepdims=True)
    return (x - m) / jnp.sqrt(v + eps)

def _scatter_add(tgt, idx, src, axis=0):
    return tgt.at[idx].add(src)

def _segment_sum(src, seg, n):
    return jax.ops.segment_sum(src, seg, n)
kernel_name = 'mk_hybrid_d2_jaxref_r8_5ebb2f'

def setup_inputs(seed: int=0):
    np.random.seed(seed)
    _w = jnp.asarray

    def _L0_attn_a_setup():
        import jax, jax.numpy as jnp
        import numpy as np
        D_MODEL = 128
        N_HEADS = 16
        D_HEAD = D_MODEL // N_HEADS
        RPE_HIDDEN = 32

        def _rpe_bias(T, w1, b1, w2, b2):
            pos = jnp.arange(T, dtype=jnp.float32)
            rel = pos[:, None] - pos[None, :]
            rel = jnp.sign(rel) * jnp.log1p(jnp.abs(rel))
            h = jax.nn.relu(rel[..., None] * w1[0] + b1)
            bias = h @ w2 + b2
            return jnp.transpose(bias, (2, 0, 1))
        key = jax.random.key(seed)
        ks = jax.random.split(key, 8)
        B, T = (2, 256)
        s = lambda fan_in: 1.0 / np.sqrt(fan_in)
        return {'x': jax.random.normal(ks[0], (B, T, D_MODEL), dtype=jnp.float32), 'w_qkv': jax.random.uniform(ks[1], (D_MODEL, 3 * D_MODEL), jnp.float32, -s(D_MODEL), s(D_MODEL)), 'b_qkv': jnp.zeros((3 * D_MODEL,), jnp.float32), 'w_out': jax.random.uniform(ks[2], (D_MODEL, D_MODEL), jnp.float32, -s(D_MODEL), s(D_MODEL)), 'b_out': jnp.zeros((D_MODEL,), jnp.float32), 'w1_rpe': jax.random.uniform(ks[3], (1, RPE_HIDDEN), jnp.float32, -1.0, 1.0), 'b1_rpe': jax.random.uniform(ks[4], (RPE_HIDDEN,), jnp.float32, -1.0, 1.0), 'w2_rpe': jax.random.uniform(ks[5], (RPE_HIDDEN, N_HEADS), jnp.float32, -s(RPE_HIDDEN), s(RPE_HIDDEN)), 'b2_rpe': jnp.zeros((N_HEADS,), jnp.float32)}
    _L0_attn_a_in = _L0_attn_a_setup()

    def _L0_attn_b_setup():
        import jax, jax.numpy as jnp
        import numpy as np
        B, L, D = (8, 512, 128)
        LN_EPS = 1e-05

        def _linear_attn(q, k, v):
            d = q.shape[-1]
            q = jax.nn.softmax(q, axis=-1) * d ** (-0.5)
            k = jax.nn.softmax(k, axis=-2)
            context = jnp.einsum('bld,ble->bde', k, v)
            return jnp.einsum('bld,bde->ble', q, context)

        def _layernorm(x, gamma, beta):
            mu = jnp.mean(x, axis=-1, keepdims=True)
            var = jnp.var(x, axis=-1, keepdims=True)
            return (x - mu) * jax.lax.rsqrt(var + LN_EPS) * gamma + beta
        key = jax.random.key(seed)
        ks = jax.random.split(key, 5)
        scale = 1.0 / np.sqrt(D)
        return {'x': jax.random.normal(ks[0], (B, L, D), dtype=jnp.float32), 'Wq': jax.random.normal(ks[1], (D, D), dtype=jnp.float32) * scale, 'Wk': jax.random.normal(ks[2], (D, D), dtype=jnp.float32) * scale, 'Wv': jax.random.normal(ks[3], (D, D), dtype=jnp.float32) * scale, 'Wo': jax.random.normal(ks[4], (D, D), dtype=jnp.float32) * scale, 'bo': jnp.zeros((D,), dtype=jnp.float32), 'gamma': jnp.ones((D,), dtype=jnp.float32), 'beta': jnp.zeros((D,), dtype=jnp.float32)}
    _L0_attn_b_in = _L0_attn_b_setup()

    def _L0_ffn_setup():
        import jax, jax.numpy as jnp
        import numpy as np
        NUM_EXPERTS = 8
        EXPERT_CAPACITY = 2.0
        DIM = 128
        HIDDEN_DIM = 512
        key = jax.random.key(seed)
        k_x, k_g, k_w1, k_w2 = jax.random.split(key, 4)
        n, t, d, f, e = (8, 128, DIM, HIDDEN_DIM, NUM_EXPERTS)
        x = jax.random.normal(k_x, (n, t, d), dtype=jnp.float32)
        gate_w = jax.random.normal(k_g, (e, d), dtype=jnp.float32) * 0.02
        w1 = jax.random.normal(k_w1, (e, d, f), dtype=jnp.float32) * 0.02
        w2 = jax.random.normal(k_w2, (e, f, d), dtype=jnp.float32) * 0.02
        return {'x': x, 'gate_w': gate_w, 'w1': w1, 'w2': w2}
    _L0_ffn_in = _L0_ffn_setup()

    def _L1_attn_a_setup():
        import jax, jax.numpy as jnp
        import numpy as np
        LN_EPS = 1e-05

        def _silu(x):
            return x * jax.nn.sigmoid(x)
        key = jax.random.key(seed)
        ks = jax.random.split(key, 12)
        B, L, d_model = (2, 256, 128)
        d_inner, d_state, d_conv = (256, 16, 4)
        s = lambda fan: 1.0 / np.sqrt(fan)
        A = jnp.arange(1, d_state + 1, dtype=jnp.float32)[None, :] * jnp.ones((d_inner, 1), jnp.float32)
        return {'x': jax.random.normal(ks[0], (B, L, d_model), jnp.float32), 'w_in': jax.random.normal(ks[1], (d_model, 2 * d_inner), jnp.float32) * s(d_model), 'conv_w': jax.random.normal(ks[2], (d_inner, 1, d_conv), jnp.float32) * s(d_conv), 'conv_b': jax.random.normal(ks[3], (d_inner,), jnp.float32) * 0.02, 'w_xproj': jax.random.normal(ks[4], (d_inner, 2 * d_state), jnp.float32) * s(d_inner), 'w_dt': jax.random.normal(ks[5], (d_inner, d_inner), jnp.float32) * s(d_inner), 'b_dt': jax.random.normal(ks[6], (d_inner,), jnp.float32) * 0.02, 'A_log': jnp.log(A), 'D': jnp.ones((d_inner,), jnp.float32), 'w_out': jax.random.normal(ks[7], (d_inner, d_model), jnp.float32) * s(d_inner), 'ln_g': jnp.ones((d_model,), jnp.float32), 'ln_b': jnp.zeros((d_model,), jnp.float32)}
    _L1_attn_a_in = _L1_attn_a_setup()

    def _L1_attn_b_setup():
        import jax, jax.numpy as jnp
        import numpy as np
        HID = 128
        NH = 4
        HD = HID // NH
        KS = 4
        C = 64
        EPS = 1e-05
        B = 4
        L = 512

        def _causal_dwconv(x, w):
            xc = jnp.moveaxis(x, 1, 2)
            y = jax.lax.conv_general_dilated(xc, w, window_strides=(1,), padding=[(w.shape[-1] - 1, 0)], dimension_numbers=('NCH', 'OIH', 'NCH'), feature_group_count=w.shape[0])
            return jnp.moveaxis(jax.nn.silu(y), 1, 2)

        def _forward(x, Wq, Wk, Wv, Wb, conv_q, conv_k, conv_v, g, Wo):
            Bx, Lx, _ = x.shape
            N = Lx // C
            q = _causal_dwconv(x @ Wq, conv_q).reshape(Bx, Lx, NH, HD)
            k = _causal_dwconv(x @ Wk, conv_k).reshape(Bx, Lx, NH, HD)
            v = _causal_dwconv(x @ Wv, conv_v).reshape(Bx, Lx, NH, HD)
            q = q / jnp.linalg.norm(q, axis=-1, keepdims=True)
            k = k / jnp.linalg.norm(k, axis=-1, keepdims=True)
            beta = jax.nn.sigmoid(x @ Wb)
            Q = q.reshape(Bx, N, C, NH, HD)
            K = k.reshape(Bx, N, C, NH, HD)
            V = v.reshape(Bx, N, C, NH, HD)
            bta = beta.reshape(Bx, N, C, NH, 1)
            Kb = K * bta
            Vb = V * bta
            A = jnp.einsum('bnihd,bnjhd->bnij', Kb, K)
            T0 = jnp.eye(C, dtype=x.dtype) - jnp.tril(A, -1)
            col = jnp.arange(C)

            def body(i, T):
                row = jax.lax.dynamic_slice_in_dim(T, i, 1, axis=2)[:, :, 0]
                acc = jnp.einsum('bnj,bnjc->bnc', row, T)
                new_row = jnp.where(col < i, row + acc, row)
                return jax.lax.dynamic_update_slice_in_dim(T, new_row[:, :, None, :], i, axis=2)
            T = jax.lax.fori_loop(1, C, body, T0)
            W = jnp.einsum('bnij,bnjhd->bnihd', T, Kb)
            U = jnp.einsum('bnij,bnjhd->bnihd', T, Vb)

            def chunk_step(S, inp):
                q_i, k_i, w_i, u0 = inp
                Sd = jnp.diagonal(S, axis1=-2, axis2=-1)
                u_i = u0 - w_i * Sd[:, None]
                o_inter = q_i * Sd[:, None]
                A_i = jnp.tril(jnp.einsum('bchd,bchd->bc', q_i, k_i))
                o_intra = A_i[:, :, None, None] * u_i
                S = S + jnp.einsum('bchd,bche->bhde', k_i, u_i)
                return (S, o_inter + o_intra)
            xs = tuple((jnp.moveaxis(a, 1, 0) for a in (Q, K, W, U)))
            S0 = jnp.zeros((Bx, NH, HD, HD), x.dtype)
            S, O = jax.lax.scan(chunk_step, S0, xs)
            o = jnp.moveaxis(O, 0, 1).reshape(Bx, Lx, NH, HD)
            o = o * jax.lax.rsqrt(jnp.mean(o * o, axis=-1, keepdims=True) + EPS) * g
            out = o.reshape(Bx, Lx, NH * HD) @ Wo
            return (out, S)

        def _reference_tuple_inner(x, Wq, Wk, Wv, Wb, conv_q, conv_k, conv_v, g, Wo):
            return _forward(x, Wq, Wk, Wv, Wb, conv_q, conv_k, conv_v, g, Wo)
        key = jax.random.key(seed)
        ks = jax.random.split(key, 9)
        return {'x': jax.random.normal(ks[0], (B, L, HID), jnp.float32), 'Wq': jax.random.normal(ks[1], (HID, HID), jnp.float32) * 0.02, 'Wk': jax.random.normal(ks[2], (HID, HID), jnp.float32) * 0.02, 'Wv': jax.random.normal(ks[3], (HID, HID), jnp.float32) * 0.02, 'Wb': jax.random.normal(ks[4], (HID, NH), jnp.float32) * 0.02, 'conv_q': jax.random.normal(ks[5], (HID, 1, KS), jnp.float32) * 0.5, 'conv_k': jax.random.normal(ks[6], (HID, 1, KS), jnp.float32) * 0.5, 'conv_v': jax.random.normal(ks[7], (HID, 1, KS), jnp.float32) * 0.5, 'g': jnp.ones((HD,), jnp.float32), 'Wo': jax.random.normal(ks[8], (HID, HID), jnp.float32) * 0.02}
    _L1_attn_b_in = _L1_attn_b_setup()

    def _L1_ffn_setup():
        import jax, jax.numpy as jnp
        import numpy as np
        HIDDEN = 128
        N_EXPERTS = 32
        MOE_I = 64
        N_GROUP = 4
        TOPK_GROUP = 2
        TOP_K = 6
        N_LOCAL_GROUPS = 16
        ANCHOR_I = 32
        SHARED_I = 64
        ROUTED_SCALE = 0.2
        ANCHOR_ALPHA = 0.1
        BATCH, SEQ = (1, 128)

        def _moe_forward(hidden_states, gate_weight, gate_bias, w_gate, w_up, w_down, shared_w_gate, shared_w_up, shared_w_down, anchor_w_gate, anchor_w_up, anchor_w_down):
            B, S, H = hidden_states.shape
            x = hidden_states.reshape(-1, H)
            T = x.shape[0]
            E = gate_weight.shape[0]
            L = anchor_w_gate.shape[0]
            logits = x @ gate_weight.T
            scores = jax.nn.sigmoid(logits)
            sc = scores + gate_bias
            grp = sc.reshape(T, N_GROUP, E // N_GROUP)
            group_scores = jax.lax.top_k(grp, 2)[0].sum(-1)
            _, gidx = jax.lax.top_k(group_scores, TOPK_GROUP)
            gmask = jax.nn.one_hot(gidx, N_GROUP, dtype=sc.dtype).sum(1)
            emask = jnp.repeat(gmask, E // N_GROUP, axis=1)
            masked = jnp.where(emask > 0, sc, -jnp.inf)
            _, topidx = jax.lax.top_k(masked, TOP_K)
            tw = jnp.take_along_axis(scores, topidx, axis=-1)
            tw = tw / (tw.sum(-1, keepdims=True) + 1e-20) * ROUTED_SCALE
            g = jnp.einsum('th,ehi->tei', x, w_gate)
            u = jnp.einsum('th,ehi->tei', x, w_up)
            eo = jnp.einsum('tei,eih->teh', jax.nn.silu(g) * u, w_down)
            cw = (jax.nn.one_hot(topidx, E, dtype=x.dtype) * tw[..., None]).sum(1)
            routed = jnp.einsum('te,teh->th', cw, eo)
            shared = jax.nn.silu(x @ shared_w_gate) * (x @ shared_w_up) @ shared_w_down
            lg = topidx[:, 0] // (E // L)
            ag = jnp.einsum('th,lhi->tli', x, anchor_w_gate)
            au = jnp.einsum('th,lhi->tli', x, anchor_w_up)
            ao = jnp.einsum('tli,lih->tlh', jax.nn.silu(ag) * au, anchor_w_down)
            acw = jax.nn.one_hot(lg, L, dtype=x.dtype)
            anchor = jnp.einsum('tl,tlh->th', acw, ao)
            out = routed + shared + ANCHOR_ALPHA * anchor
            return out.reshape(B, S, H)
        key = jax.random.key(seed)
        ks = jax.random.split(key, 13)
        s = 0.02
        return {'hidden_states': jax.random.normal(ks[0], (BATCH, SEQ, HIDDEN), jnp.float32), 'gate_weight': s * jax.random.normal(ks[1], (N_EXPERTS, HIDDEN), jnp.float32), 'gate_bias': s * jax.random.normal(ks[2], (N_EXPERTS,), jnp.float32), 'w_gate': s * jax.random.normal(ks[3], (N_EXPERTS, HIDDEN, MOE_I), jnp.float32), 'w_up': s * jax.random.normal(ks[4], (N_EXPERTS, HIDDEN, MOE_I), jnp.float32), 'w_down': s * jax.random.normal(ks[5], (N_EXPERTS, MOE_I, HIDDEN), jnp.float32), 'shared_w_gate': s * jax.random.normal(ks[6], (HIDDEN, SHARED_I), jnp.float32), 'shared_w_up': s * jax.random.normal(ks[7], (HIDDEN, SHARED_I), jnp.float32), 'shared_w_down': s * jax.random.normal(ks[8], (SHARED_I, HIDDEN), jnp.float32), 'anchor_w_gate': s * jax.random.normal(ks[9], (N_LOCAL_GROUPS, HIDDEN, ANCHOR_I), jnp.float32), 'anchor_w_up': s * jax.random.normal(ks[10], (N_LOCAL_GROUPS, HIDDEN, ANCHOR_I), jnp.float32), 'anchor_w_down': s * jax.random.normal(ks[11], (N_LOCAL_GROUPS, ANCHOR_I, HIDDEN), jnp.float32)}
    _L1_ffn_in = _L1_ffn_setup()
    _d = {'L0_attn_a_x': _L0_attn_a_in['x'], 'L0_attn_a_w_qkv': _L0_attn_a_in['w_qkv'], 'L0_attn_a_b_qkv': _L0_attn_a_in['b_qkv'], 'L0_attn_a_w_out': _L0_attn_a_in['w_out'], 'L0_attn_a_b_out': _L0_attn_a_in['b_out'], 'L0_attn_a_w1_rpe': _L0_attn_a_in['w1_rpe'], 'L0_attn_a_b1_rpe': _L0_attn_a_in['b1_rpe'], 'L0_attn_a_w2_rpe': _L0_attn_a_in['w2_rpe'], 'L0_attn_a_b2_rpe': _L0_attn_a_in['b2_rpe'], 'L0_attn_b_Wq': _L0_attn_b_in['Wq'], 'L0_attn_b_Wk': _L0_attn_b_in['Wk'], 'L0_attn_b_Wv': _L0_attn_b_in['Wv'], 'L0_attn_b_Wo': _L0_attn_b_in['Wo'], 'L0_attn_b_bo': _L0_attn_b_in['bo'], 'L0_attn_b_gamma': _L0_attn_b_in['gamma'], 'L0_attn_b_beta': _L0_attn_b_in['beta'], 'L0_ffn_gate_w': _L0_ffn_in['gate_w'], 'L0_ffn_w1': _L0_ffn_in['w1'], 'L0_ffn_w2': _L0_ffn_in['w2'], 'L1_attn_a_w_in': _L1_attn_a_in['w_in'], 'L1_attn_a_conv_w': _L1_attn_a_in['conv_w'], 'L1_attn_a_conv_b': _L1_attn_a_in['conv_b'], 'L1_attn_a_w_xproj': _L1_attn_a_in['w_xproj'], 'L1_attn_a_w_dt': _L1_attn_a_in['w_dt'], 'L1_attn_a_b_dt': _L1_attn_a_in['b_dt'], 'L1_attn_a_A_log': _L1_attn_a_in['A_log'], 'L1_attn_a_D': _L1_attn_a_in['D'], 'L1_attn_a_w_out': _L1_attn_a_in['w_out'], 'L1_attn_a_ln_g': _L1_attn_a_in['ln_g'], 'L1_attn_a_ln_b': _L1_attn_a_in['ln_b'], 'L1_attn_b_Wq': _L1_attn_b_in['Wq'], 'L1_attn_b_Wk': _L1_attn_b_in['Wk'], 'L1_attn_b_Wv': _L1_attn_b_in['Wv'], 'L1_attn_b_Wb': _L1_attn_b_in['Wb'], 'L1_attn_b_conv_q': _L1_attn_b_in['conv_q'], 'L1_attn_b_conv_k': _L1_attn_b_in['conv_k'], 'L1_attn_b_conv_v': _L1_attn_b_in['conv_v'], 'L1_attn_b_g': _L1_attn_b_in['g'], 'L1_attn_b_Wo': _L1_attn_b_in['Wo'], 'L1_ffn_gate_weight': _L1_ffn_in['gate_weight'], 'L1_ffn_gate_bias': _L1_ffn_in['gate_bias'], 'L1_ffn_w_gate': _L1_ffn_in['w_gate'], 'L1_ffn_w_up': _L1_ffn_in['w_up'], 'L1_ffn_w_down': _L1_ffn_in['w_down'], 'L1_ffn_shared_w_gate': _L1_ffn_in['shared_w_gate'], 'L1_ffn_shared_w_up': _L1_ffn_in['shared_w_up'], 'L1_ffn_shared_w_down': _L1_ffn_in['shared_w_down'], 'L1_ffn_anchor_w_gate': _L1_ffn_in['anchor_w_gate'], 'L1_ffn_anchor_w_up': _L1_ffn_in['anchor_w_up'], 'L1_ffn_anchor_w_down': _L1_ffn_in['anchor_w_down']}
    _x0 = _d['L0_attn_a_x']
    _d['L0_attn_a_x'] = jax.random.normal(jax.random.fold_in(jax.random.key(seed), 1), (4, 512, 128), dtype=_x0.dtype)
    del _x0
    return _d

def reference(L0_attn_a_x, L0_attn_a_w_qkv, L0_attn_a_b_qkv, L0_attn_a_w_out, L0_attn_a_b_out, L0_attn_a_w1_rpe, L0_attn_a_b1_rpe, L0_attn_a_w2_rpe, L0_attn_a_b2_rpe, L0_attn_b_Wq, L0_attn_b_Wk, L0_attn_b_Wv, L0_attn_b_Wo, L0_attn_b_bo, L0_attn_b_gamma, L0_attn_b_beta, L0_ffn_gate_w, L0_ffn_w1, L0_ffn_w2, L1_attn_a_w_in, L1_attn_a_conv_w, L1_attn_a_conv_b, L1_attn_a_w_xproj, L1_attn_a_w_dt, L1_attn_a_b_dt, L1_attn_a_A_log, L1_attn_a_D, L1_attn_a_w_out, L1_attn_a_ln_g, L1_attn_a_ln_b, L1_attn_b_Wq, L1_attn_b_Wk, L1_attn_b_Wv, L1_attn_b_Wb, L1_attn_b_conv_q, L1_attn_b_conv_k, L1_attn_b_conv_v, L1_attn_b_g, L1_attn_b_Wo, L1_ffn_gate_weight, L1_ffn_gate_bias, L1_ffn_w_gate, L1_ffn_w_up, L1_ffn_w_down, L1_ffn_shared_w_gate, L1_ffn_shared_w_up, L1_ffn_shared_w_down, L1_ffn_anchor_w_gate, L1_ffn_anchor_w_up, L1_ffn_anchor_w_down):

    def _L0_attn_a_ref(x, w_qkv, b_qkv, w_out, b_out, w1_rpe, b1_rpe, w2_rpe, b2_rpe):
        import jax, jax.numpy as jnp
        import numpy as np
        D_MODEL = 128
        N_HEADS = 16
        D_HEAD = D_MODEL // N_HEADS
        RPE_HIDDEN = 32

        def _rpe_bias(T, w1, b1, w2, b2):
            pos = jnp.arange(T, dtype=jnp.float32)
            rel = pos[:, None] - pos[None, :]
            rel = jnp.sign(rel) * jnp.log1p(jnp.abs(rel))
            h = jax.nn.relu(rel[..., None] * w1[0] + b1)
            bias = h @ w2 + b2
            return jnp.transpose(bias, (2, 0, 1))
        B, T, C = x.shape
        qkv = x @ w_qkv + b_qkv
        q, k, v = jnp.split(qkv, 3, axis=-1)

        def heads(t):
            return jnp.transpose(t.reshape(B, T, N_HEADS, D_HEAD), (0, 2, 1, 3))
        q, k, v = (heads(q), heads(k), heads(v))
        scores = jnp.einsum('bhtd,bhsd->bhts', q, k) / np.sqrt(D_HEAD)
        scores = scores + _rpe_bias(T, w1_rpe, b1_rpe, w2_rpe, b2_rpe)[None]
        attn = jax.nn.softmax(scores, axis=-1)
        out = jnp.einsum('bhts,bhsd->bhtd', attn, v)
        out = jnp.transpose(out, (0, 2, 1, 3)).reshape(B, T, C)
        return out @ w_out + b_out

    def _L0_attn_b_ref(x, Wq, Wk, Wv, Wo, bo, gamma, beta):
        import jax, jax.numpy as jnp
        import numpy as np
        B, L, D = (8, 512, 128)
        LN_EPS = 1e-05

        def _linear_attn(q, k, v):
            d = q.shape[-1]
            q = jax.nn.softmax(q, axis=-1) * d ** (-0.5)
            k = jax.nn.softmax(k, axis=-2)
            context = jnp.einsum('bld,ble->bde', k, v)
            return jnp.einsum('bld,bde->ble', q, context)

        def _layernorm(x, gamma, beta):
            mu = jnp.mean(x, axis=-1, keepdims=True)
            var = jnp.var(x, axis=-1, keepdims=True)
            return (x - mu) * jax.lax.rsqrt(var + LN_EPS) * gamma + beta
        q = jnp.einsum('bld,de->ble', x, Wq)
        k = jnp.einsum('bld,de->ble', x, Wk)
        v = jnp.einsum('bld,de->ble', x, Wv)
        attn = _linear_attn(q, k, v)
        out = jnp.einsum('ble,ed->bld', attn, Wo) + bo
        return _layernorm(x + out, gamma, beta)

    def _L0_ffn_ref(x, gate_w, w1, w2):
        import jax, jax.numpy as jnp
        import numpy as np
        NUM_EXPERTS = 8
        EXPERT_CAPACITY = 2.0
        DIM = 128
        HIDDEN_DIM = 512
        n, t, d = x.shape
        e = gate_w.shape[0]
        k = int(EXPERT_CAPACITY * t / e)
        scores = jnp.einsum('ntd,ed->nte', x, gate_w)
        probs = jax.nn.softmax(scores, axis=-1)
        g, m = jax.lax.top_k(probs.transpose(0, 2, 1), k)
        batch_idx = jnp.arange(n)[:, None, None]
        xin = x[batch_idx, m]
        h = jnp.einsum('nekd,edf->nekf', xin, w1)
        h = jax.nn.gelu(h, approximate=False)
        h = jnp.einsum('nekf,efd->nekd', h, w2)
        out_tok = g[..., None] * h
        out = jnp.zeros((n, t, d), dtype=x.dtype).at[batch_idx, m].add(out_tok)
        return out

    def _L1_attn_a_ref(x, w_in, conv_w, conv_b, w_xproj, w_dt, b_dt, A_log, D, w_out, ln_g, ln_b):
        import jax, jax.numpy as jnp
        import numpy as np
        LN_EPS = 1e-05

        def _silu(x):
            return x * jax.nn.sigmoid(x)
        B, L, d_model = x.shape
        d_inner = conv_w.shape[0]
        d_state = A_log.shape[1]
        d_conv = conv_w.shape[2]
        residual = x
        mu = x.mean(-1, keepdims=True)
        var = ((x - mu) ** 2).mean(-1, keepdims=True)
        xn = (x - mu) * jax.lax.rsqrt(var + LN_EPS) * ln_g + ln_b
        xz = xn @ w_in
        x_b, z = jnp.split(xz, 2, axis=-1)
        xc = jnp.transpose(x_b, (0, 2, 1))
        xc = jax.lax.conv_general_dilated(xc, conv_w, window_strides=(1,), padding=[(d_conv - 1, 0)], dimension_numbers=('NCH', 'OIH', 'NCH'), feature_group_count=d_inner)
        xc = xc + conv_b[None, :, None]
        x_b = _silu(jnp.transpose(xc, (0, 2, 1)))
        A = -jnp.exp(A_log)
        x_dbl = x_b @ w_xproj
        B_mat, C_mat = jnp.split(x_dbl, 2, axis=-1)
        dt = jax.nn.softplus(x_b @ w_dt + b_dt)

        def step(h, ins):
            dt_t, B_t, C_t, x_t = ins
            A_bar = jnp.exp(dt_t[:, :, None] * A[None])
            B_bar = dt_t[:, :, None] * B_t[:, None, :]
            h = A_bar * h + B_bar * x_t[:, :, None]
            y_t = jnp.einsum('bdn,bn->bd', h, C_t)
            return (h, y_t)
        tm = lambda a: jnp.transpose(a, (1, 0, 2))
        h0 = jnp.zeros((B, d_inner, d_state), x.dtype)
        _, y = jax.lax.scan(step, h0, (tm(dt), tm(B_mat), tm(C_mat), tm(x_b)))
        y = jnp.transpose(y, (1, 0, 2)) + D * x_b
        y = y * _silu(z)
        return y @ w_out + residual

    def _L1_attn_b_ref(x, Wq, Wk, Wv, Wb, conv_q, conv_k, conv_v, g, Wo):
        import jax, jax.numpy as jnp
        import numpy as np
        HID = 128
        NH = 4
        HD = HID // NH
        KS = 4
        C = 64
        EPS = 1e-05
        B = 4
        L = 512

        def _causal_dwconv(x, w):
            xc = jnp.moveaxis(x, 1, 2)
            y = jax.lax.conv_general_dilated(xc, w, window_strides=(1,), padding=[(w.shape[-1] - 1, 0)], dimension_numbers=('NCH', 'OIH', 'NCH'), feature_group_count=w.shape[0])
            return jnp.moveaxis(jax.nn.silu(y), 1, 2)

        def _forward(x, Wq, Wk, Wv, Wb, conv_q, conv_k, conv_v, g, Wo):
            Bx, Lx, _ = x.shape
            N = Lx // C
            q = _causal_dwconv(x @ Wq, conv_q).reshape(Bx, Lx, NH, HD)
            k = _causal_dwconv(x @ Wk, conv_k).reshape(Bx, Lx, NH, HD)
            v = _causal_dwconv(x @ Wv, conv_v).reshape(Bx, Lx, NH, HD)
            q = q / jnp.linalg.norm(q, axis=-1, keepdims=True)
            k = k / jnp.linalg.norm(k, axis=-1, keepdims=True)
            beta = jax.nn.sigmoid(x @ Wb)
            Q = q.reshape(Bx, N, C, NH, HD)
            K = k.reshape(Bx, N, C, NH, HD)
            V = v.reshape(Bx, N, C, NH, HD)
            bta = beta.reshape(Bx, N, C, NH, 1)
            Kb = K * bta
            Vb = V * bta
            A = jnp.einsum('bnihd,bnjhd->bnij', Kb, K)
            T0 = jnp.eye(C, dtype=x.dtype) - jnp.tril(A, -1)
            col = jnp.arange(C)

            def body(i, T):
                row = jax.lax.dynamic_slice_in_dim(T, i, 1, axis=2)[:, :, 0]
                acc = jnp.einsum('bnj,bnjc->bnc', row, T)
                new_row = jnp.where(col < i, row + acc, row)
                return jax.lax.dynamic_update_slice_in_dim(T, new_row[:, :, None, :], i, axis=2)
            T = jax.lax.fori_loop(1, C, body, T0)
            W = jnp.einsum('bnij,bnjhd->bnihd', T, Kb)
            U = jnp.einsum('bnij,bnjhd->bnihd', T, Vb)

            def chunk_step(S, inp):
                q_i, k_i, w_i, u0 = inp
                Sd = jnp.diagonal(S, axis1=-2, axis2=-1)
                u_i = u0 - w_i * Sd[:, None]
                o_inter = q_i * Sd[:, None]
                A_i = jnp.tril(jnp.einsum('bchd,bchd->bc', q_i, k_i))
                o_intra = A_i[:, :, None, None] * u_i
                S = S + jnp.einsum('bchd,bche->bhde', k_i, u_i)
                return (S, o_inter + o_intra)
            xs = tuple((jnp.moveaxis(a, 1, 0) for a in (Q, K, W, U)))
            S0 = jnp.zeros((Bx, NH, HD, HD), x.dtype)
            S, O = jax.lax.scan(chunk_step, S0, xs)
            o = jnp.moveaxis(O, 0, 1).reshape(Bx, Lx, NH, HD)
            o = o * jax.lax.rsqrt(jnp.mean(o * o, axis=-1, keepdims=True) + EPS) * g
            out = o.reshape(Bx, Lx, NH * HD) @ Wo
            return (out, S)

        def _reference_tuple_inner(x, Wq, Wk, Wv, Wb, conv_q, conv_k, conv_v, g, Wo):
            return _forward(x, Wq, Wk, Wv, Wb, conv_q, conv_k, conv_v, g, Wo)
        return _reference_tuple_inner(x, Wq, Wk, Wv, Wb, conv_q, conv_k, conv_v, g, Wo)[0]

    def _L1_ffn_ref(hidden_states, gate_weight, gate_bias, w_gate, w_up, w_down, shared_w_gate, shared_w_up, shared_w_down, anchor_w_gate, anchor_w_up, anchor_w_down):
        import jax, jax.numpy as jnp
        import numpy as np
        HIDDEN = 128
        N_EXPERTS = 32
        MOE_I = 64
        N_GROUP = 4
        TOPK_GROUP = 2
        TOP_K = 6
        N_LOCAL_GROUPS = 16
        ANCHOR_I = 32
        SHARED_I = 64
        ROUTED_SCALE = 0.2
        ANCHOR_ALPHA = 0.1
        BATCH, SEQ = (1, 128)

        def _moe_forward(hidden_states, gate_weight, gate_bias, w_gate, w_up, w_down, shared_w_gate, shared_w_up, shared_w_down, anchor_w_gate, anchor_w_up, anchor_w_down):
            B, S, H = hidden_states.shape
            x = hidden_states.reshape(-1, H)
            T = x.shape[0]
            E = gate_weight.shape[0]
            L = anchor_w_gate.shape[0]
            logits = x @ gate_weight.T
            scores = jax.nn.sigmoid(logits)
            sc = scores + gate_bias
            grp = sc.reshape(T, N_GROUP, E // N_GROUP)
            group_scores = jax.lax.top_k(grp, 2)[0].sum(-1)
            _, gidx = jax.lax.top_k(group_scores, TOPK_GROUP)
            gmask = jax.nn.one_hot(gidx, N_GROUP, dtype=sc.dtype).sum(1)
            emask = jnp.repeat(gmask, E // N_GROUP, axis=1)
            masked = jnp.where(emask > 0, sc, -jnp.inf)
            _, topidx = jax.lax.top_k(masked, TOP_K)
            tw = jnp.take_along_axis(scores, topidx, axis=-1)
            tw = tw / (tw.sum(-1, keepdims=True) + 1e-20) * ROUTED_SCALE
            g = jnp.einsum('th,ehi->tei', x, w_gate)
            u = jnp.einsum('th,ehi->tei', x, w_up)
            eo = jnp.einsum('tei,eih->teh', jax.nn.silu(g) * u, w_down)
            cw = (jax.nn.one_hot(topidx, E, dtype=x.dtype) * tw[..., None]).sum(1)
            routed = jnp.einsum('te,teh->th', cw, eo)
            shared = jax.nn.silu(x @ shared_w_gate) * (x @ shared_w_up) @ shared_w_down
            lg = topidx[:, 0] // (E // L)
            ag = jnp.einsum('th,lhi->tli', x, anchor_w_gate)
            au = jnp.einsum('th,lhi->tli', x, anchor_w_up)
            ao = jnp.einsum('tli,lih->tlh', jax.nn.silu(ag) * au, anchor_w_down)
            acw = jax.nn.one_hot(lg, L, dtype=x.dtype)
            anchor = jnp.einsum('tl,tlh->th', acw, ao)
            out = routed + shared + ANCHOR_ALPHA * anchor
            return out.reshape(B, S, H)
        return _moe_forward(hidden_states, gate_weight, gate_bias, w_gate, w_up, w_down, shared_w_gate, shared_w_up, shared_w_down, anchor_w_gate, anchor_w_up, anchor_w_down)
    x = L0_attn_a_x
    x = x + _L0_attn_a_ref(_layernorm(x, axis=-1), L0_attn_a_w_qkv, L0_attn_a_b_qkv, L0_attn_a_w_out, L0_attn_a_b_out, L0_attn_a_w1_rpe, L0_attn_a_b1_rpe, L0_attn_a_w2_rpe, L0_attn_a_b2_rpe)
    x = x + _L0_ffn_ref(_layernorm(x, axis=-1), L0_ffn_gate_w, L0_ffn_w1, L0_ffn_w2)
    x = x + _L0_attn_b_ref(_layernorm(x, axis=-1), L0_attn_b_Wq, L0_attn_b_Wk, L0_attn_b_Wv, L0_attn_b_Wo, L0_attn_b_bo, L0_attn_b_gamma, L0_attn_b_beta)
    x = x + _L0_ffn_ref(_layernorm(x, axis=-1), L0_ffn_gate_w, L0_ffn_w1, L0_ffn_w2)
    x = x + _L1_attn_a_ref(_layernorm(x, axis=-1), L1_attn_a_w_in, L1_attn_a_conv_w, L1_attn_a_conv_b, L1_attn_a_w_xproj, L1_attn_a_w_dt, L1_attn_a_b_dt, L1_attn_a_A_log, L1_attn_a_D, L1_attn_a_w_out, L1_attn_a_ln_g, L1_attn_a_ln_b)
    x = x + _L1_ffn_ref(_layernorm(x, axis=-1), L1_ffn_gate_weight, L1_ffn_gate_bias, L1_ffn_w_gate, L1_ffn_w_up, L1_ffn_w_down, L1_ffn_shared_w_gate, L1_ffn_shared_w_up, L1_ffn_shared_w_down, L1_ffn_anchor_w_gate, L1_ffn_anchor_w_up, L1_ffn_anchor_w_down)
    x = x + _L1_attn_b_ref(_layernorm(x, axis=-1), L1_attn_b_Wq, L1_attn_b_Wk, L1_attn_b_Wv, L1_attn_b_Wb, L1_attn_b_conv_q, L1_attn_b_conv_k, L1_attn_b_conv_v, L1_attn_b_g, L1_attn_b_Wo)
    x = x + _L1_ffn_ref(_layernorm(x, axis=-1), L1_ffn_gate_weight, L1_ffn_gate_bias, L1_ffn_w_gate, L1_ffn_w_up, L1_ffn_w_down, L1_ffn_shared_w_gate, L1_ffn_shared_w_up, L1_ffn_shared_w_down, L1_ffn_anchor_w_gate, L1_ffn_anchor_w_up, L1_ffn_anchor_w_down)
    return x

_drawn_inputs = setup_inputs


def setup_inputs(seed=0):
    import zlib

    import numpy as np

    out = dict(_drawn_inputs(seed))
    spreads = {'L0_attn_a_b_qkv': (0.0, 0.1),
     'L0_attn_a_b_out': (0.0, 0.1),
     'L0_attn_a_b2_rpe': (0.0, 0.8),
     'L0_attn_b_bo': (0.0, 0.1),
     'L0_attn_b_gamma': (1.0, 0.2),
     'L0_attn_b_beta': (0.0, 0.1),
     'L1_attn_a_D': (1.0, 0.543),
     'L1_attn_a_ln_g': (1.0, 0.2),
     'L1_attn_a_ln_b': (0.0, 0.1),
     'L1_attn_b_g': (1.0, 0.6)}
    factors = {'L0_attn_a_w1_rpe': 4.892,
     'L0_attn_a_b1_rpe': 8.0,
     'L0_attn_a_w2_rpe': 5.539,
     'L0_attn_b_Wq': 8.0,
     'L0_attn_b_Wk': 8.0,
     'L0_attn_b_Wv': 7.727,
     'L0_attn_b_Wo': 7.385,
     'L0_ffn_gate_w': 3.208,
     'L0_ffn_w1': 2.832,
     'L0_ffn_w2': 2.791,
     'L1_attn_a_conv_b': 8.0,
     'L1_attn_a_b_dt': 8.0,
     'L1_attn_b_Wb': 4.469,
     'L1_ffn_gate_weight': 8.0,
     'L1_ffn_gate_bias': 8.0,
     'L1_ffn_w_gate': 8.0,
     'L1_ffn_w_up': 8.0,
     'L1_ffn_w_down': 8.0,
     'L1_ffn_shared_w_gate': 8.0,
     'L1_ffn_shared_w_up': 8.0,
     'L1_ffn_shared_w_down': 8.0,
     'L1_ffn_anchor_w_gate': 8.0,
     'L1_ffn_anchor_w_up': 8.0,
     'L1_ffn_anchor_w_down': 8.0}
    for name, (base, spread) in spreads.items():
        noise = np.random.default_rng([zlib.crc32(name.encode()), seed]).standard_normal(out[name].shape)
        drawn = base * np.exp(spread * noise) if base else spread * noise
        out[name] = jnp.asarray(drawn.astype(out[name].dtype))
    for name, factor in factors.items():
        out[name] = (out[name] * factor).astype(out[name].dtype)
    return out
```

```python
from contextlib import ExitStack

import concourse.bass as bass
from concourse import mybir

F32 = mybir.dt.float32
BF16 = mybir.dt.bfloat16
I32 = mybir.dt.int32
ALU = mybir.AluOpType
ACT = mybir.ActivationFunctionType
AX_X = mybir.AxisListType.X

P = 128
B, T, D = 4, 512, 128
NT = B * T // P
TPB = T // P
LN_EPS = 1e-5
PHASES = [0, 1, 2, 3, 4, 5, 6, 7]


class Core:

    def __init__(self, nc, ctx):
        self.nc, self.ctx = nc, ctx
        self.past, self.own = [], []
        self.x = self.sb("x", [P, NT, D])
        self.xn = self.sb("xn", [P, NT, D])
        self.xnT = self.sb("xnT", [D, B * T])
        self.ident = self.sb("ident", [P, P])
        self.ident16 = self.sb("ident16", [P, P], BF16)
        self.eps = self.sb("eps", [P, 1])
        self.bank = [ctx.enter_context(nc.psum_tensor(f"bank{i}", [P, 512], F32)) for i in range(8)]

    def sb(self, name, shape, dt=F32, ctx=None):
        return (ctx or self.ctx).enter_context(self.nc.sbuf_tensor(name, shape, dt))

    def sem(self, name):
        s = self.nc.alloc_semaphore(name=name)
        self.own.append(s)
        return s

    def next_layer(self):
        self.past, self.own = self.own, []

    def clear_past(self):
        self.nc.clear_and_free_semaphores(self.past)


class Link:

    def __init__(self, eng, sem, waited=None):
        self.eng, self.sem, self.n, self.base, self.waited = eng, sem, 0, 0, waited

    def __call__(self, ins):
        ins.then_inc(self.sem, 1)
        self.n += 1
        self.eng.wait_ge(self.sem, self.base + self.n)
        if self.waited is not None:
            self.eng.sem_inc(self.waited, 1)

    def start(self, i, per):
        self.first, self.n, self.base = self.n, 0, self.n + i * per

    def end(self, per, passes):
        assert self.n == per, (self.n, per)
        self.n, self.base = self.first + per * passes, 0


def bcast(ap, *dims):
    return bass.AP(ap.tensor, ap.offset, [ap.ap[0], *dims])



class Norm:
    def __init__(self, k, tag, ctx, scratch=None):
        self.k = k
        self.stats = k.sb(f"{tag}_stats", [P, NT, 6], ctx=ctx)
        self.mv = k.sb(f"{tag}_mv", [P, NT, 2], ctx=ctx)
        self.vare = k.sb(f"{tag}_vare", [P, NT], ctx=ctx)
        self.std = k.sb(f"{tag}_std", [P, NT], ctx=ctx)
        self.rstd = k.sb(f"{tag}_rstd", [P, NT], ctx=ctx)
        self.var_ready = k.sem(f"{tag}_var_ready")
        self.std_ready = k.sem(f"{tag}_std_ready")
        self.xn_ready = k.sem(f"{tag}_xn_ready")
        self.turned = k.sem(f"{tag}_turned")
        self.xnT_ready = k.sem(f"{tag}_xnT_ready")

    def statistics(self, dve, link, src):
        for j in range(NT):
            last = dve.bn_stats(self.stats[:, j, :], src[:, j, :])
        link(last)
        for j in range(NT):
            last = dve.bn_aggr(self.mv[:, j, :], self.stats[:, j, :])
        link(last)
        dve.tensor_scalar(self.vare[:], self.mv[:, :, 1], LN_EPS, None, ALU.add).then_inc(self.var_ready, 1)

    def scalar_sqrt(self, act, n=1):
        act.wait_ge(self.var_ready, n)
        act.activation(self.std[:], self.vare[:], ACT.Sqrt).then_inc(self.std_ready, 1)

    def vector(self, dve, link):
        k = self.k
        self.statistics(dve, link, k.x)
        self.normalise(dve, link)

    def normalise(self, dve, link):
        k = self.k
        dve.wait_ge(self.std_ready, 1)
        link(dve.reciprocal(self.rstd[:], self.std[:]))
        for j in range(NT):
            dve.tensor_scalar(k.xn[:, j, :], k.x[:, j, :], self.mv[:, j, 0:1], self.rstd[:, j:j + 1],
                              ALU.subtract, ALU.mult).then_inc(self.xn_ready, 1)

    def tensor(self, pe, src=None, ready=None):
        k = self.k
        src = k.xn if src is None else src
        ready = self.xn_ready if ready is None else ready
        for g in range(B):
            pe.wait_ge(ready, 4 * (g + 1))
            for j in range(4):
                last = pe.transpose(k.bank[g][:, j * P:(j + 1) * P], src[:, 4 * g + j, :], k.ident[:])
            last.then_inc(self.turned, 1)

    def scalar_copy(self, act):
        k = self.k
        for g in range(B):
            act.wait_ge(self.turned, g + 1)
            act.activation(k.xnT[:, g * T:(g + 1) * T], k.bank[g][:], ACT.Copy).then_inc(self.xnT_ready, 1)



def layer_attention(k, tag, w_qkv, b_qkv, w_out, b_out, w1_rpe, b1_rpe, w2_rpe, b2_rpe):
    nc = k.nc
    HID, H = w2_rpe.shape
    HD = D // H
    HP = H // 2
    PARTS = 8
    SCALE = float(HD) ** -0.5
    SPAN = 2 * T
    WIDE = 2 * T - P
    U = H * TPB
    PRODUCTS = [(0, 0), (0, 1), (1, 0), (1, 1), (0, 2), (2, 0)]
    with ExitStack() as ctx:
        def sb(name, shape, dt=F32):
            return k.sb(f"{tag}_{name}", shape, dt, ctx)

        def sem(name):
            return k.sem(f"{tag}_{name}")

        norm = Norm(k, tag, ctx)
        wqkv = sb("wqkv", [D, 3 * D])
        wout = sb("wout", [D, D])
        bqkv = sb("bqkv", [P, 3 * D])
        bout = sb("bout", [P, D])
        w1c = sb("w1c", [HID, 1])
        b1c = sb("b1c", [HID, 1])
        w2 = sb("w2", [HID, H])
        b2c = sb("b2c", [H, 1])
        rel = sb("rel", [HID, SPAN])
        mag = sb("mag", [HID, SPAN])
        side = sb("side", [HID, SPAN])
        curve = sb("curve", [H, SPAN])
        bias = sb("bias", [P, H, WIDE])
        scratch = nc.dram_tensor(f"{tag}_scratch", [H, SPAN], F32)
        qk = sb("qk", [P, NT, 2, D])
        v1 = sb("v1", [P, NT, H, HD + 1])
        rest = sb("rest", [P, 2, TPB, D])
        part = sb("part", [P, 3, TPB, D], BF16)
        stack = sb("stack", [P, 2, TPB, H, PARTS, HD], BF16)
        qkT = sb("qkT", [P, HP, 2, T], BF16)
        neg = sb("neg", [P, 2, T])
        nmax = sb("nmax", [P, 2, 1])
        prob = sb("prob", [P, 2, T])
        probT = sb("probT", [P, 2, T])
        rsum = sb("rsum", [P, U // 2])
        o = sb("o", [P, TPB, D])
        oT = sb("oT", [D, T])

        loaded_w, loaded_r, loaded_bias = sem("loaded_w"), sem("loaded_r"), sem("loaded_bias")
        waited, order, pool_order, act_order = sem("waited"), sem("order"), sem("pool_order"), sem("act_order")
        rel_ready, curve_turned, curve_ready, curve_stored = sem("rel_ready"), sem("curve_turned"), sem("curve_ready"), sem("curve_stored")
        side_ready, logd = sem("side_ready"), sem("logd")
        qkv_done, qkv_ready = sem("qkv_done"), sem("qkv_ready")
        stacked, parts_turned, parts_ready = sem("stacked"), sem("parts_turned"), sem("parts_ready")
        scored, biased, exped, prob_turned = sem("scored"), sem("biased"), sem("exped"), sem("prob_turned")
        probT_ready = [sem("probT_by_act"), sem("probT_by_dve")]
        mixed, o_ready, o_turned, oT_ready, projected, added = (
            sem("mixed"), sem("o_ready"), sem("o_turned"), sem("oT_ready"), sem("projected"), sem("added"))

        block = ctx.enter_context(nc.Block())

        @block.sync
        def _(sp):
            sp.dma_start(w1c[:], w1_rpe.rearrange("a h -> h a"), allow_slow_non_contiguous=True).then_inc(loaded_r, 16)
            sp.dma_start(b1c[:], b1_rpe.rearrange("(h a) -> h a", a=1)).then_inc(loaded_r, 16)
            sp.dma_start(w2[:], w2_rpe).then_inc(loaded_r, 16)
            sp.dma_start(b2c[:], b2_rpe.rearrange("(h a) -> h a", a=1)).then_inc(loaded_r, 16)
            sp.dma_start(wqkv[:], w_qkv).then_inc(loaded_w, 16)
            sp.dma_start(bqkv[:], b_qkv.partition_broadcast(P)).then_inc(loaded_w, 16)
            sp.dma_start(wout[:], w_out).then_inc(loaded_w, 16)
            sp.dma_start(bout[:], b_out.partition_broadcast(P)).then_inc(loaded_w, 16)
            sp.wait_ge(curve_ready, 2)
            sp.dma_start(scratch[:, :], curve[:]).then_inc(curve_stored, 16)
            sp.wait_ge(curve_stored, 16)
            for h in range(0, H, 4):
                src = bass.AP(scratch, h * SPAN, [[1, P], [SPAN, 4], [1, WIDE]])
                sp.dma_start(bias[:, h:h + 4, :], src).then_inc(loaded_bias, 16)
                sp.wait_ge(loaded_bias, 4 * h + 16)

        @block.gpsimd
        def _(pool):
            k.clear_past()
            link = Link(pool, pool_order, waited)
            pool.iota(rel[:], [[1, SPAN]], base=1 - T, channel_multiplier=0, allow_small_or_imprecise_dtypes=True).then_inc(rel_ready, 1)
            link(pool.memset(stack[:], 0.0))
            link(pool.memset(v1[:], 1.0))
            pool.wait_ge(qkv_ready, NT)
            pool.sem_inc(parts_turned, HP)
            with pool.Fori(0, B) as b:
                link.start(b, 10)
                pool.wait_ge(parts_turned, b * HP + HP)
                pool.sem_inc(waited, 1)
                for s in range(2):
                    src = qk[:, bass.ds(b * TPB, TPB), s, :]
                    link(pool.tensor_copy(rest[:, 0, :, :], src))
                    link(pool.tensor_copy(part[:, 0, :, :], rest[:, 0, :, :]))
                    link(pool.tensor_tensor(rest[:, 1, :, :], rest[:, 0, :, :], part[:, 0, :, :], ALU.subtract))
                    link(pool.tensor_copy(part[:, 1, :, :], rest[:, 1, :, :]))
                    link(pool.tensor_tensor(part[:, 2, :, :], rest[:, 1, :, :], part[:, 1, :, :], ALU.subtract))
                    for r, pair in enumerate(PRODUCTS):
                        for j in range(TPB):
                            last = pool.tensor_copy(stack[:, s, j, :, r, :], part[:, pair[s], j, :].rearrange("p (h d) -> p h d", d=HD))
                    last.then_inc(stacked, 1)

        @block.scalar
        def _(act):
            link = Link(act, act_order)
            norm.scalar_sqrt(act)
            act.wait_ge(side_ready, 1)
            act.activation(mag[:], mag[:], ACT.Ln, bias=1.0).then_inc(logd, 1)
            act.wait_ge(side_ready, 2)
            act.wait_ge(loaded_r, 64)
            link(act.activation(mag[:], mag[:], ACT.Relu, bias=b1c[:, 0:1], scale=w1c[:, 0:1]))
            norm.scalar_copy(act)
            for i in range(2):
                act.wait_ge(curve_turned, i + 1)
                act.activation(curve[:, i * T:(i + 1) * T], k.bank[4 + i][0:H, :], ACT.Identity, bias=b2c[:, 0:1]).then_inc(curve_ready, 1)
            with act.Fori(0, B) as b:
                def copy_parts(hp):
                    act.wait_ge(parts_turned, b * HP + hp + 1 + HP)
                    if hp == 0:
                        act.wait_ge(scored, b * U + 1)
                    act.activation(qkT[:, hp, :, :].rearrange("p s t -> p (s t)"), k.bank[6 + hp % 2][:].bitcast(BF16), ACT.Copy).then_inc(parts_ready, 1)

                copy_parts(0)
                copy_parts(1)
                for step in range(U + 2):
                    if step % 8 == 0 and 0 < step and step // 8 + 1 < HP:
                        copy_parts(step // 8 + 1)
                    if step < U:
                        u = step
                        act.wait_ge(biased, b * U + u + 3)
                        act.wait_ge(prob_turned, b * U + u + 1)
                        act.activation(prob[:, u % 2, :], neg[:, u % 2, :], ACT.Exp, bias=nmax[:, u % 2, :], scale=-1.0).then_inc(exped, 1)
                    if step >= 2 and step % 2 == 0:
                        u = step - 2
                        act.wait_ge(prob_turned, b * U + u + 3)
                        act.wait_ge(mixed, b * U + u + 1)
                        act.activation(probT[:, u % 2, :], k.bank[2 + u % 2][:], ACT.Copy).then_inc(probT_ready[0], 1)
                act.wait_ge(o_turned, b + 1)
                act.activation(oT[:], k.bank[6][:], ACT.Copy).then_inc(oT_ready, 1)

        @block.vector
        def _(dve):
            link = Link(dve, order)
            for s, n in ((biased, 2), (exped, 2), (prob_turned, 2), (mixed, 2), (probT_ready[0], 1), (probT_ready[1], 1),
                         (o_ready, 2), (added, 1), (scored, 1)):
                dve.sem_inc(s, n)
            norm.statistics(dve, link, k.x)
            dve.wait_ge(rel_ready, 1)
            dve.scalar_tensor_tensor(mag[:], rel[:], -1.0, rel[:], ALU.mult, ALU.max).then_inc(side_ready, 1)
            link(dve.tensor_scalar(side[:], rel[:], 0.0, 2.0, ALU.is_ge, ALU.mult))
            link(dve.tensor_scalar(side[:], side[:], -1.0, None, ALU.add))
            dve.wait_ge(logd, 1)
            dve.tensor_tensor(mag[:], mag[:], side[:], ALU.mult).then_inc(side_ready, 1)
            norm.normalise(dve, link)
            dve.wait_ge(pool_order, 2)
            dve.wait_ge(loaded_w, 64)
            for t in range(NT):
                dve.wait_ge(qkv_done, t + 1)
                ps = k.bank[4 + t % 4]
                dve.tensor_tensor(v1[:, t, :, 0:HD], ps[:, 2 * D:3 * D].rearrange("p (h d) -> p h d", d=HD),
                                  bqkv[:, 2 * D:3 * D].rearrange("p (h d) -> p h d", d=HD), ALU.add)
                if t == 0:
                    link(dve.tensor_scalar(bqkv[:, 0:D], bqkv[:, 0:D], SCALE, None, ALU.mult))
                dve.scalar_tensor_tensor(qk[:, t, 0, :], ps[:, 0:D], SCALE, bqkv[:, 0:D], ALU.mult, ALU.add)
                dve.tensor_tensor(qk[:, t, 1, :], ps[:, D:2 * D], bqkv[:, D:2 * D], ALU.add).then_inc(qkv_ready, 1)
            with dve.Fori(0, B) as b:
                link.start(b, 2)
                for step in range(U + 2):
                    if step < U:
                        u = step
                        h, j = u // TPB, u % TPB
                        if j == 0 and h % 4 == 0:
                            dve.wait_ge(loaded_bias, 4 * h + 16)
                        dve.wait_ge(scored, b * U + u + 2)
                        dve.wait_ge(exped, b * U + u + 1)
                        dve.sem_inc(waited, 1)
                        key0 = bias[:, h, T - 1 + j * P:T + j * P]
                        keys_back = bcast(key0, (-1, T))
                        dve.tensor_tensor_reduce(out=neg[:, u % 2, :], in0=k.bank[u % 2][:], in1=keys_back,
                                                 scale=-1.0, scalar=3e38, op0=ALU.add, op1=ALU.min, accum_out=nmax[:, u % 2, :]).then_inc(biased, 1)
                    if step >= 2 and step % 2 == 1:
                        u = step - 2
                        dve.wait_ge(prob_turned, b * U + u + 3)
                        dve.wait_ge(mixed, b * U + u + 1)
                        dve.tensor_copy(probT[:, u % 2, :], k.bank[2 + u % 2][:]).then_inc(probT_ready[1], 1)
                    if step in (U // 2 + 4, U + 1):
                        half = step // U
                        if half:
                            dve.wait_ge(mixed, b * U + U + 2)
                        else:
                            dve.wait_ge(mixed, b * U + U // 2 + 2)
                        ov = k.bank[4 + half][:, 0:(U // 2) * (HD + 1)].rearrange("p (h j d) -> p h j d", j=TPB, d=HD + 1)
                        link(dve.reciprocal(rsum[:].rearrange("p (h j) -> p h j", j=TPB), ov[:, :, :, HD]))
                        dst = o[:].rearrange("p j (h d) -> p h j d", d=HD)[:, half * H // 2:(half + 1) * H // 2]
                        dve.tensor_tensor(dst, ov[:, :, :, 0:HD], rsum[:].rearrange("p (h j) -> p h j", j=TPB).unsqueeze(3).to_broadcast([P, H // 2, TPB, HD]),
                                          ALU.mult).then_inc(o_ready, 1)
                dve.wait_ge(projected, b + 1)
                xb = k.x[:, bass.ds(b * TPB, TPB), :]
                dve.tensor_tensor(xb, xb, k.bank[7][:].rearrange("p (j d) -> p j d", d=D), ALU.add).then_inc(added, 1)
                dve.wait_ge(added, b * 2 + 2)
                dve.tensor_tensor(xb, xb, bcast(bout[:, 0:1], (0, TPB), (1, D)), ALU.add).then_inc(added, 1)
                link.end(2, B)

        @block.tensor
        def _(pe):
            pe.wait_ge(act_order, 1)
            for i in range(2):
                pe.matmul(k.bank[4 + i][0:H, :], w2[:], mag[:, i * T:(i + 1) * T], start=True, stop=True).then_inc(curve_turned, 1)
            norm.tensor(pe)
            pe.wait_ge(loaded_w, 64)
            pe.wait_ge(curve_ready, 2)
            for t in range(NT):
                pe.wait_ge(norm.xnT_ready, t // TPB + 1)
                if t >= 4:
                    pe.wait_ge(qkv_ready, t - 3)
                pe.matmul(k.bank[4 + t % 4][:, 0:3 * D], k.xnT[:, t * P:(t + 1) * P], wqkv[:], start=True, stop=True).then_inc(qkv_done, 1)
            pe.wait_ge(qkv_ready, NT)
            with pe.Fori(0, B) as b:
                def turn_parts(hp):
                    if hp == 1:
                        pe.wait_ge(added, b * 2 + 1)
                    if hp >= 2:
                        pe.wait_ge(parts_ready, b * HP + hp - 1)
                    bank = k.bank[6 + hp % 2][:].bitcast(BF16)
                    for s in range(2):
                        for j in range(TPB):
                            last = pe.transpose(bank[:, s * T + j * P:s * T + (j + 1) * P],
                                                stack[:, s, j, 2 * hp:2 * hp + 2, :, :].rearrange("p h r d -> p (h r d)"), k.ident16[:])
                    last.then_inc(parts_turned, 1)

                pe.wait_ge(stacked, b * 2 + 2)
                turn_parts(0)
                turn_parts(1)
                for step in range(U + 3):
                    if step % 8 == 0 and 0 < step and step // 8 + 1 < HP:
                        turn_parts(step // 8 + 1)
                    if step < U:
                        u = step
                        h, j = u // TPB, u % TPB
                        if j == 0:
                            pe.wait_ge(parts_ready, b * HP + h // 2 + 1)
                        pe.wait_ge(biased, b * U + u + 1)
                        r = slice(64 * (h % 2), 64 * (h % 2) + 64)
                        pe.matmul(k.bank[u % 2][:], qkT[r, h // 2, 0, j * P:(j + 1) * P], qkT[r, h // 2, 1, :], start=True, stop=True).then_inc(scored, 1)
                    if 2 <= step < U + 2:
                        u = step - 2
                        pe.wait_ge(exped, b * U + u + 3)
                        pe.wait_ge(probT_ready[u % 2], b * (U // 2) + u // 2 + 1)
                        for c in range(TPB):
                            last = pe.transpose(k.bank[2 + u % 2][:, c * P:(c + 1) * P], prob[:, u % 2, c * P:(c + 1) * P], k.ident[:])
                        last.then_inc(prob_turned, 1)
                    if step >= 3:
                        u = step - 3
                        h, j = u // TPB, u % TPB
                        if u % (U // 2) == 0:
                            pe.wait_ge(o_ready, b * 2 + u // (U // 2) + 1)
                        pe.wait_ge(probT_ready[u % 2], b * (U // 2) + u // 2 + 2)
                        c0 = (u % (U // 2)) * (HD + 1)
                        for c in range(TPB):
                            vals = v1[:, bass.ds(b * TPB + c, 1), h, :].rearrange("p t d -> p (t d)")
                            last = pe.matmul(k.bank[4 + h // (H // 2)][:, c0:c0 + HD + 1], probT[:, u % 2, c * P:(c + 1) * P], vals,
                                             start=(c == 0), stop=(c == TPB - 1))
                        last.then_inc(mixed, 1)
                pe.wait_ge(o_ready, b * 2 + 4)
                for j in range(TPB):
                    last = pe.transpose(k.bank[6][:, j * P:(j + 1) * P], o[:, j, :], k.ident[:])
                last.then_inc(o_turned, 1)
                pe.wait_ge(oT_ready, b + 1)
                for j in range(TPB):
                    last = pe.matmul(k.bank[7][:, j * D:(j + 1) * D], oT[:, j * P:(j + 1) * P], wout[:], start=True, stop=True)
                last.then_inc(projected, 1)



def layer_moe_experts(k, tag, gate_w, w1, w2):
    nc = k.nc
    E, F = w1.shape[0], w1.shape[2]
    CAP = int(2.0 * T / E)
    FT = F // P
    R = B * E
    assert CAP == P and CAP % 8 == 0 and E % 2 == 0
    with ExitStack() as ctx:
        def sb(name, shape, dt=F32):
            return k.sb(f"{tag}_{name}", shape, dt, ctx)

        def sem(name):
            return k.sem(f"{tag}_{name}")

        norm = Norm(k, tag, ctx)
        gw = sb("gw", [E, D])
        gwT = sb("gwT", [D, E])
        w1s = sb("w1s", [D, 2, F])
        w2s = sb("w2s", [P, 2, FT, D])
        lmax = sb("lmax", [P, NT])
        probs = sb("probs", [P, NT, E])
        psum_e = sb("psum_e", [P, NT])
        prec = sb("prec", [P, NT])
        rows = sb("rows", [R, 2, T])
        best = sb("best", [R, 8])
        ones = sb("ones", [R, T])
        chosen = sb("chosen", [R, T])
        count = sb("count", [R, T])
        slot = sb("slot", [R, T])
        slots = sb("slots", [P, E, NT])
        gates = sb("gates", [P, E, NT])
        number = sb("number", [P, P])
        pick = sb("pick", [P, 2, NT, P])
        own = sb("own", [P, 2, NT])
        place = sb("place", [P, B, T])
        xin = sb("xin", [D, T])
        hid = sb("hid", [P, FT, T])
        gate = sb("gate", [P, B])
        y = sb("y", [P, B, D])

        loaded_gw = sem("loaded_gw")
        loaded_w = [sem("loaded_w0"), sem("loaded_w1")]
        order, pool_order, number_made = sem("order"), sem("pool_order"), sem("number_made")
        gwT_turned, gwT_ready, logits_ready = sem("gwT_turned"), sem("gwT_ready"), sem("logits_ready")
        shifted, exped, probs_ready = sem("shifted"), sem("exped"), sem("probs_ready")
        rows_turned, slot_ready, slot_turned, slots_ready = sem("rows_turned"), sem("slot_ready"), sem("slot_turned"), sem("slots_ready")
        own_ready, own_seen, pick_ready, pick_used = sem("own_ready"), sem("own_seen"), sem("pick_ready"), sem("pick_used")
        xin_ready, xin_copied, h_ready, gelu_done = sem("xin_ready"), sem("xin_copied"), sem("h_ready"), sem("gelu_done")
        turned, place_ready, gate_ready, gate_copied = sem("pturned"), sem("place_ready"), sem("gate_ready"), sem("gate_copied")
        y_done, y_ready, out_ready, out_added, w_used = sem("y_done"), sem("y_ready"), sem("out_ready"), sem("out_added"), sem("w_used")

        block = ctx.enter_context(nc.Block())

        @block.sync
        def _(sp):
            sp.dma_start(gw[:], gate_w).then_inc(loaded_gw, 16)
            sp.sem_inc(w_used, 2)
            with sp.Fori(0, E // 2) as i:
                for s in range(2):
                    sp.wait_ge(w_used, i * 2 + s + 1)
                    sp.dma_start(w1s[:, s, :], w1[bass.ds(i * 2 + s, 1), :, :].rearrange("e d f -> d (e f)")).then_inc(loaded_w[s], 16)
                    sp.dma_start(w2s[:, s, :, :], w2[bass.ds(i * 2 + s, 1), :, :].rearrange("e (t p) d -> p (e t) d", p=P))\
                        .then_inc(loaded_w[s], 16)

        @block.gpsimd
        def _(pool):
            k.clear_past()
            pool.iota(number[:], [[1, P]], base=0, channel_multiplier=0, allow_small_or_imprecise_dtypes=True).then_inc(number_made, 1)
            pool.memset(ones[:], 1.0).then_inc(number_made, 1)
            pool.wait_ge(number_made, 2)
            pool.sem_inc(pick_used, 2)
            pool.wait_ge(slots_ready, 1)
            with pool.Fori(0, E // 2) as i:
                for s in range(2):
                    pool.wait_ge(pick_used, i * 2 + s + 1)
                    pool.tensor_copy(own[:, s, :], slots[:, bass.ds(i * 2 + s, 1), :].rearrange("p e j -> p (e j)")).then_inc(own_ready, 1)
                    pool.wait_ge(own_ready, i * 2 + s + 1)
                    pool.sem_inc(own_seen, 1)
                    for j in range(NT):
                        last = pool.tensor_scalar(pick[:, s, j, :], number[:], own[:, s, j:j + 1], None, ALU.is_equal)
                    last.then_inc(pick_ready, 1)

        @block.scalar
        def _(act):
            norm.scalar_sqrt(act)
            norm.scalar_copy(act)
            act.wait_ge(shifted, 1)
            act.activation(probs[:], probs[:], ACT.Exp).then_inc(exped, 1)
            with act.Fori(0, E // 2) as i:
                for s in range(2):
                    e = i * 2 + s
                    act.wait_ge(xin_ready, e + 1)
                    act.activation(xin[:], k.bank[0][:], ACT.Copy).then_inc(xin_copied, 1)
                    for f in range(FT):
                        act.wait_ge(h_ready, e * FT + f + 1)
                        act.activation(hid[:, f, :], k.bank[1 + f % 2][:], ACT.Gelu).then_inc(gelu_done, 1)
                    act.wait_ge(y_done, e + 1)

        @block.vector
        def _(dve):
            link = Link(dve, order)
            dve.sem_inc(gelu_done, 2)
            dve.sem_inc(out_added, 2)
            norm.vector(dve, link)
            dve.wait_ge(gwT_turned, 1)
            dve.tensor_copy(gwT[:], k.bank[4][:, 0:E]).then_inc(gwT_ready, 1)
            dve.wait_ge(logits_ready, 1)
            logits = k.bank[5][:, 0:NT * E].rearrange("p (j e) -> p j e", e=E)
            link(dve.tensor_reduce(lmax[:], logits, AX_X, ALU.max))
            dve.tensor_tensor(probs[:], logits, bcast(lmax[:, 0:1], (1, NT), (0, E)), ALU.subtract).then_inc(shifted, 1)
            dve.wait_ge(exped, 1)
            link(dve.tensor_reduce(psum_e[:], probs[:], AX_X, ALU.add))
            link(dve.reciprocal(prec[:], psum_e[:]))
            link(dve.tensor_tensor(probs[:], probs[:], bcast(prec[:, 0:1], (1, NT), (0, E)), ALU.mult))
            dve.tensor_copy(gates[:].rearrange("p e (n j) -> p j n e", j=TPB), probs[:].rearrange("p (j n) e -> p j n e", j=TPB))\
                .then_inc(probs_ready, 1)
            dve.wait_ge(rows_turned, 1)
            link(dve.tensor_copy(rows[:, 0, :], k.bank[6][0:R, :]))
            for r in range(CAP // 8):
                link(dve.max(best[:], rows[:, r % 2, :]))
                link(dve.match_replace(rows[:, 1 - r % 2, :], best[:], rows[:, r % 2, :], -1.0))
            link(dve.tensor_scalar(chosen[:], rows[:, (CAP // 8) % 2, :], 0.0, None, ALU.is_lt))
            dve.wait_ge(number_made, 2)
            link(dve.tensor_tensor_scan(count[:], ones[:], chosen[:], 0.0, ALU.mult, ALU.add))
            link(dve.tensor_tensor(slot[:], count[:], chosen[:], ALU.mult))
            dve.tensor_scalar(slot[:], slot[:], -1.0, None, ALU.add).then_inc(slot_ready, 1)
            dve.wait_ge(slot_turned, 1)
            dve.tensor_copy(slots[:].rearrange("p e (n j) -> p j n e", j=TPB),
                            k.bank[7][:, 0:TPB * R].rearrange("p (j n e) -> p j n e", j=TPB, n=B)).then_inc(slots_ready, 1)
            with dve.Fori(0, E // 2) as i:
                for s in range(2):
                    e = i * 2 + s
                    for n in range(B):
                        dve.wait_ge(turned, e * B + n + 1)
                        dve.tensor_copy(place[:, n, :], k.bank[3][:]).then_inc(place_ready, 1)
                    dve.wait_ge(gate_ready, e + 1)
                    dve.tensor_copy(gate[:], k.bank[4][:, 0:B]).then_inc(gate_copied, 1)
                    dve.wait_ge(gate_copied, e + 1)
                    dve.wait_ge(y_done, e + 1)
                    dve.tensor_tensor(y[:], k.bank[5][:].rearrange("p (n d) -> p n d", d=D), bcast(gate[:, 0:1], (1, B), (0, D)), ALU.mult)\
                        .then_inc(y_ready, 1)
                    for n in range(B):
                        dve.wait_ge(out_ready, e * B + n + 1)
                        xb = k.x[:, n * TPB:(n + 1) * TPB, :].rearrange("p j d -> p (j d)")
                        dve.tensor_tensor(xb, xb, k.bank[6 + n % 2][:], ALU.add).then_inc(out_added, 1)
                    dve.wait_ge(out_added, e * B + B + 2)

        @block.tensor
        def _(pe):
            norm.tensor(pe)
            pe.wait_ge(loaded_gw, 16)
            pe.transpose(k.bank[4][:, 0:E], gw[:], k.ident[0:E, 0:E]).then_inc(gwT_turned, 1)
            pe.wait_ge(gwT_ready, 1)
            pe.wait_ge(norm.xnT_ready, B)
            for j in range(TPB):
                for n in range(B):
                    o = (j * B + n) * E
                    t = n * TPB + j
                    last = pe.matmul(k.bank[5][:, o:o + E], k.xnT[:, t * P:(t + 1) * P], gwT[:], start=True, stop=True)
            last.then_inc(logits_ready, 1)
            pe.wait_ge(probs_ready, 1)
            for j in range(TPB):
                last = pe.transpose(k.bank[6][0:R, j * P:(j + 1) * P], probs[:, j * B:(j + 1) * B, :].rearrange("p n e -> p (n e)"), k.ident[:])
            last.then_inc(rows_turned, 1)
            pe.wait_ge(slot_ready, 1)
            for j in range(TPB):
                last = pe.transpose(k.bank[7][:, j * R:(j + 1) * R], slot[:, j * P:(j + 1) * P], k.ident[0:R, 0:R])
            last.then_inc(slot_turned, 1)
            pe.wait_ge(slots_ready, 1)
            with pe.Fori(0, E // 2) as i:
                for s in range(2):
                    e = i * 2 + s

                    def turn(n):
                        if n:
                            pe.wait_ge(place_ready, e * B + n)
                        for j in range(TPB):
                            last = pe.transpose(k.bank[3][:, j * P:(j + 1) * P], pick[:, s, n * TPB + j, :], k.ident[:])
                        last.then_inc(turned, 1)

                    pe.wait_ge(pick_ready, e + 1)
                    for n in range(B):
                        for j in range(TPB):
                            t = n * TPB + j
                            last = pe.matmul(k.bank[0][:, n * CAP:(n + 1) * CAP], k.xn[:, t, :], pick[:, s, t, :],
                                             start=(j == 0), stop=(j == TPB - 1))
                    last.then_inc(xin_ready, 1)
                    turn(0)
                    for n in range(B):
                        for j in range(TPB):
                            t = n * TPB + j
                            g = gates[:, bass.ds(e, 1), t:t + 1].rearrange("p e j -> p (e j)")
                            last = pe.matmul(k.bank[4][:, n:n + 1], pick[:, s, t, :], g, start=(j == 0), stop=(j == TPB - 1))
                    last.then_inc(gate_ready, 1)
                    pe.wait_ge(xin_copied, e + 1)
                    pe.wait_ge(loaded_w[s], i * 32 + 32)
                    for f in range(FT):
                        pe.wait_ge(gelu_done, e * FT + f + 1)
                        pe.matmul(k.bank[1 + f % 2][:], w1s[:, s, f * P:(f + 1) * P], xin[:], start=True, stop=True).then_inc(h_ready, 1)
                        if f < B - 1:
                            turn(f + 1)
                    pe.wait_ge(gelu_done, e * FT + FT + 2)
                    for n in range(B):
                        for f in range(FT):
                            last = pe.matmul(k.bank[5][:, n * D:(n + 1) * D], hid[:, f, n * CAP:(n + 1) * CAP], w2s[:, s, f, :],
                                             start=(f == 0), stop=(f == FT - 1))
                    last.then_inc(y_done, 1)
                    pe.wait_ge(turned, e * B + B)
                    pe.sem_inc(pick_used, 1)
                    pe.wait_ge(y_done, e + 1)
                    pe.sem_inc(w_used, 1)
                    pe.wait_ge(y_ready, e + 1)
                    pe.wait_ge(place_ready, e * B + B)
                    for n in range(B):
                        pe.wait_ge(out_added, e * B + n + 1)
                        for j in range(TPB):
                            last = pe.matmul(k.bank[6 + n % 2][:, j * D:(j + 1) * D], place[:, n, j * P:(j + 1) * P], y[:, n, :],
                                             start=True, stop=True)
                        last.then_inc(out_ready, 1)



def layer_linear_attention(k, tag, Wq, Wk, Wv, Wo, bo, gamma, beta):
    nc = k.nc
    with ExitStack() as ctx:
        def sb(name, shape, dt=F32):
            return k.sb(f"{tag}_{name}", shape, dt, ctx)

        def sem(name):
            return k.sem(f"{tag}_{name}")

        norm = Norm(k, tag, ctx)
        norm2 = Norm(k, f"{tag}2", ctx)
        wqv = sb("wqv", [D, 2 * D])
        wk = sb("wk", [D, D])
        wo = sb("wo", [D, D])
        bov = sb("bov", [P, D])
        gam = sb("gam", [P, D])
        bet = sb("bet", [P, D])
        nqmax = sb("nqmax", [P, NT])
        qsum = sb("qsum", [P, NT])
        rq = sb("rq", [P, NT])
        qe = sb("qe", [P, NT, D])
        v = sb("v", [P, NT, D])
        nkmax = sb("nkmax", [D, B])
        ksum = sb("ksum", [D, B])
        rk = sb("rk", [D, B])
        keT = sb("keT", [D, B, T])
        ke = sb("ke", [P, NT, D])
        qeT = sb("qeT", [D, B, T])
        ctxT = sb("ctxT", [D, B, D])
        cw = sb("cw", [D, B, D])
        xb = sb("xb", [P, NT, D])
        r = sb("r", [P, NT, D])

        loaded_w = sem("loaded_w")
        order, pool_order = sem("order"), sem("pool_order")
        qv_done, qmax_ready, v_ready, qe_ready = sem("qv_done"), sem("qmax_ready"), sem("v_ready"), sem("qe_ready")
        k_done, kmax_ready, ke_ready, ke_turned, ke_copied = sem("k_done"), sem("kmax_ready"), sem("ke_ready"), sem("ke_turned"), sem("ke_copied")
        q_turned, qT_copied = sem("q_turned"), sem("qT_copied")
        ctx_done, ctx_copied, cw_done, cw_ready, out_done, out_added = (
            sem("ctx_done"), sem("ctx_copied"), sem("cw_done"), sem("cw_ready"), sem("out_done"), sem("out_added"))

        block = ctx.enter_context(nc.Block())

        @block.sync
        def _(sp):
            for dst, src in ((wqv[:, 0:D], Wq), (wqv[:, D:2 * D], Wv), (wk[:], Wk), (wo[:], Wo)):
                sp.dma_start(dst, src).then_inc(loaded_w, 16)
            for dst, src in ((bov, bo), (gam, gamma), (bet, beta)):
                sp.dma_start(dst[:], src.partition_broadcast(P)).then_inc(loaded_w, 16)

        @block.gpsimd
        def _(pool):
            k.clear_past()
            pool.wait_ge(loaded_w, 112)
            pool.wait_ge(norm.xn_ready, NT)
            pool.tensor_tensor(xb[:], k.xn[:], bcast(bov[:, 0:1], (0, NT), (1, D)), ALU.add).then_inc(pool_order, 1)
            pool.tensor_tensor(k.x[:], k.x[:], bcast(bet[:, 0:1], (0, NT), (1, D)), ALU.add).then_inc(pool_order, 1)

        @block.scalar
        def _(act):
            norm.scalar_sqrt(act)
            norm.scalar_copy(act)
            for t in range(NT):
                act.wait_ge(qmax_ready, t + 1)
                act.wait_ge(v_ready, t + 1)
                act.activation(qe[:, t, :], k.bank[4 + t % 2][:, 0:D], ACT.Exp, bias=nqmax[:, t:t + 1], accum_out=qsum[:, t:t + 1]).then_inc(qe_ready, 1)
            for b in range(B):
                act.wait_ge(kmax_ready, b + 1)
                act.activation(keT[:, b, :], k.bank[6 + b % 2][:], ACT.Exp, bias=nkmax[:, b:b + 1], accum_out=ksum[:, b:b + 1]).then_inc(ke_ready, 1)
            for b in range(B):
                act.wait_ge(q_turned, b + 1)
                act.activation(qeT[:, b, :], k.bank[2 + b % 2][:], ACT.Copy).then_inc(qT_copied, 1)
            norm2.scalar_sqrt(act)

        @block.vector
        def _(dve):
            link = Link(dve, order)
            norm.vector(dve, link)
            for t in range(NT):
                bank = k.bank[4 + t % 2]
                dve.wait_ge(qv_done, t + 1)
                dve.tensor_reduce(nqmax[:, t:t + 1], bank[:, 0:D], AX_X, ALU.max, negate=True).then_inc(qmax_ready, 1)
                dve.tensor_copy(v[:, t, :], bank[:, D:2 * D]).then_inc(v_ready, 1)
            for b in range(B):
                dve.wait_ge(k_done, b + 1)
                dve.tensor_reduce(nkmax[:, b:b + 1], k.bank[6 + b % 2][:], AX_X, ALU.max, negate=True).then_inc(kmax_ready, 1)
            for b in range(B):
                dve.wait_ge(ke_turned, b + 1)
                dve.tensor_copy(ke[:, b * TPB:(b + 1) * TPB, :].rearrange("p j d -> p (j d)"), k.bank[b % 2][:]).then_inc(ke_copied, 1)
            dve.wait_ge(qe_ready, NT)
            dve.reciprocal(rq[:], qsum[:])
            dve.wait_ge(ke_ready, B)
            link(dve.reciprocal(rk[:], ksum[:]))
            dve.wait_ge(ctx_done, 1)
            dve.tensor_copy(ctxT[:].rearrange("p b d -> p (b d)"), k.bank[4][:]).then_inc(ctx_copied, 1)
            dve.wait_ge(cw_done, 1)
            for b in range(B):
                dve.tensor_scalar(cw[:, b, :], k.bank[5][:, b * D:(b + 1) * D], rk[:, b:b + 1], float(D) ** -0.5, ALU.mult, ALU.mult)\
                    .then_inc(cw_ready, 1)
            dve.wait_ge(pool_order, 2)
            for t in range(NT):
                dve.wait_ge(out_done, t // TPB + 1)
                last = dve.scalar_tensor_tensor(r[:, t, :], k.bank[6 + (t // TPB) % 2][:, (t % TPB) * D:(t % TPB + 1) * D], rq[:, t:t + 1], xb[:, t, :],
                                                ALU.mult, ALU.add)
                if t % TPB == TPB - 1:
                    last.then_inc(out_added, 1)
            dve.wait_ge(out_added, B)
            norm2.statistics(dve, link, r)
            dve.wait_ge(norm2.std_ready, 1)
            link(dve.reciprocal(norm2.rstd[:], norm2.std[:]))
            for t in range(NT):
                last = dve.tensor_scalar(r[:, t, :], r[:, t, :], norm2.mv[:, t, 0:1], norm2.rstd[:, t:t + 1], ALU.subtract, ALU.mult)
            link(last)
            link(dve.tensor_tensor(r[:], r[:], bcast(gam[:, 0:1], (0, NT), (1, D)), ALU.mult))
            dve.tensor_tensor(k.x[:], k.x[:], r[:], ALU.add)

        @block.tensor
        def _(pe):
            norm.tensor(pe)
            pe.wait_ge(loaded_w, 112)
            for t in range(NT):
                pe.wait_ge(norm.xnT_ready, t // TPB + 1)
                if t >= 2:
                    pe.wait_ge(qe_ready, t - 1)
                    pe.wait_ge(v_ready, t - 1)
                pe.matmul(k.bank[4 + t % 2][:, 0:2 * D], k.xnT[:, t * P:(t + 1) * P], wqv[:], start=True, stop=True).then_inc(qv_done, 1)
            for b in range(B):
                if b >= 2:
                    pe.wait_ge(ke_ready, b - 1)
                pe.matmul(k.bank[6 + b % 2][:], wk[:], k.xnT[:, b * T:(b + 1) * T], start=True, stop=True).then_inc(k_done, 1)
            for b in range(B):
                pe.wait_ge(qe_ready, (b + 1) * TPB)
                if b >= 2:
                    pe.wait_ge(qT_copied, b - 1)
                for j in range(TPB):
                    last = pe.transpose(k.bank[2 + b % 2][:, j * P:(j + 1) * P], qe[:, b * TPB + j, :], k.ident[:])
                last.then_inc(q_turned, 1)
            for b in range(B):
                pe.wait_ge(ke_ready, b + 1)
                if b >= 2:
                    pe.wait_ge(ke_copied, b - 1)
                for j in range(TPB):
                    last = pe.transpose(k.bank[b % 2][:, j * P:(j + 1) * P], keT[:, b, j * P:(j + 1) * P], k.ident[:])
                last.then_inc(ke_turned, 1)
            for b in range(B):
                pe.wait_ge(ke_copied, b + 1)
                pe.wait_ge(v_ready, NT)
                for j in range(TPB):
                    last = pe.matmul(k.bank[4][:, b * D:(b + 1) * D], v[:, b * TPB + j, :], ke[:, b * TPB + j, :], start=(j == 0), stop=(j == TPB - 1))
            last.then_inc(ctx_done, 1)
            pe.wait_ge(ctx_copied, 1)
            for b in range(B):
                last = pe.matmul(k.bank[5][:, b * D:(b + 1) * D], ctxT[:, b, :], wo[:], start=True, stop=True)
            last.then_inc(cw_done, 1)
            for b in range(B):
                pe.wait_ge(cw_ready, b + 1)
                pe.wait_ge(qT_copied, b + 1)
                if b >= 2:
                    pe.wait_ge(out_added, b - 1)
                for j in range(TPB):
                    last = pe.matmul(k.bank[6 + b % 2][:, j * D:(j + 1) * D], qeT[:, b, j * P:(j + 1) * P], cw[:, b, :], start=True, stop=True)
                last.then_inc(out_done, 1)



def layer_scan(k, tag, w_in, conv_w, conv_b, w_xproj, w_dt, b_dt, A_log, Dskip, w_out, ln_g, ln_b):
    nc = k.nc
    DI, N = A_log.shape
    TAPS = conv_w.shape[2]
    C = DI // P
    Q = N * B
    with ExitStack() as ctx:
        def sb(name, shape, dt=F32):
            return k.sb(f"{tag}_{name}", shape, dt, ctx)

        def sem(name):
            return k.sem(f"{tag}_{name}")

        norm = Norm(k, tag, ctx)
        norm2 = Norm(k, f"{tag}2", ctx)
        win = sb("win", [D, 2 * DI])
        cw = sb("cw", [P, C, TAPS])
        cols = sb("cols", [P, 3, C])
        lngb = sb("lngb", [D, 2])
        wx3 = sb("wx3", [P, C, 3, 2 * N])
        wdt = sb("wdt", [P, C, DI])
        wout = sb("wout", [P, C, D])
        A = sb("A", [P, C, N])
        z2 = sb("z2", [P, NT, D])
        xp = sb("xp", [P, C, B, TAPS - 1 + T])
        xc = sb("xc", [P, C, B, T])
        zs = sb("zs", [P, C, B, T])
        dt_ = sb("dt", [P, C, B, T])
        dtx = sb("dtx", [P, C, B, T])
        t1 = sb("t1", [3 * 2 * N, T], BF16)
        t2 = sb("t2", [3 * 2 * N, T], BF16)
        r1 = sb("r1", [3 * 2 * N, T])
        r2 = sb("r2", [3 * 2 * N, T])
        bc = sb("bc", [3 * 2 * N, B, T], BF16)
        spread = sb("spread", [3 * 2 * N, 2 * N, P], BF16)
        keep = sb("keep", [P, B, T])
        bsb = sb("bsb", [P, B, T])
        push = sb("push", [P, B, T])
        h = sb("h", [P, B, T])
        hc = sb("hc", [P, B, T])

        loaded_w = sem("loaded_w")
        order, pool_order, act_order, waited = sem("order"), sem("pool_order"), sem("act_order"), sem("waited")
        z2_ready, xz_done, xz_copied, conv_ready, xc_ready = sem("z2_ready"), sem("xz_done"), sem("xz_copied"), sem("conv_ready"), sem("xc_ready")
        bc_done, bc_ready, dt_done, dt_ready, soft_ready = sem("bc_done"), sem("bc_ready"), sem("dt_done"), sem("dt_ready"), sem("soft_ready")
        dtx_ready, skip_ready = sem("dtx_ready"), sem("skip_ready")
        b_done, b_copied, c_done, push_ready, keep_ready = sem("b_done"), sem("b_copied"), sem("c_done"), sem("push_ready"), sem("keep_ready")
        scanned, hc_ready, summed, gated = sem("scanned"), sem("hc_ready"), sem("summed"), sem("gated")
        out_done, added, x_ready = sem("out_done"), sem("added"), sem("x_ready")
        NW = 12

        block = ctx.enter_context(nc.Block())

        @block.sync
        def _(sp):
            sp.dma_start(win[:], w_in).then_inc(loaded_w, 16)
            sp.dma_start(cw[:], conv_w.rearrange("(c p) a k -> p c (a k)", p=P)).then_inc(loaded_w, 16)
            for i, v in enumerate((conv_b, b_dt, Dskip)):
                sp.dma_start(cols[:, i, :], v.rearrange("(c p) -> p c", p=P), allow_slow_non_contiguous=True).then_inc(loaded_w, 16)
            sp.dma_start(A[:], A_log.rearrange("(c p) n -> p c n", p=P)).then_inc(loaded_w, 16)
            for r in range(3):
                sp.dma_start(wx3[:, :, r, :], w_xproj.rearrange("(c p) n -> p c n", p=P)).then_inc(loaded_w, 16)
            sp.dma_start(wdt[:], w_dt.rearrange("(c p) n -> p c n", p=P)).then_inc(loaded_w, 16)
            sp.dma_start(wout[:], w_out.rearrange("(c p) n -> p c n", p=P)).then_inc(loaded_w, 16)
            sp.dma_start(lngb[:, 0:1], ln_g.rearrange("(d a) -> d a", a=1)).then_inc(loaded_w, 16)
            sp.dma_start(lngb[:, 1:2], ln_b.rearrange("(d a) -> d a", a=1)).then_inc(loaded_w, 16)

        @block.gpsimd
        def _(pool):
            k.clear_past()
            link = Link(pool, pool_order)
            link(pool.memset(xp[:, :, :, 0:TAPS - 1], 0.0))
            link(pool.memset(spread[:], 0.0))
            for part in range(3):
                link(pool.affine_select(out=spread[:], in_=spread[:], compare_op=ALU.not_equal, fill=1.0, base=-2 * N * part,
                                        pattern=[[-1, 2 * N], [0, P]], channel_multiplier=1))
            pool.wait_ge(norm.xn_ready, NT)
            pool.tensor_tensor(k.x[:], k.x[:], k.xn[:], ALU.add).then_inc(x_ready, 1)
            for c in range(C):
                pool.wait_ge(dtx_ready, c + 1)
                with pool.Fori(0, N) as n:
                    for b in range(B):
                        q = c * Q + n * B + b
                        pool.wait_ge(b_copied, q + 3)
                        pool.wait_ge(scanned, q + 1)
                        pool.tensor_tensor(push[:, b, :], dtx[:, c, b, :], bsb[:, b, :], ALU.mult).then_inc(push_ready, 1)

        @block.scalar
        def _(act):
            link = Link(act, act_order)
            norm.scalar_sqrt(act)
            norm2.scalar_sqrt(act)
            act.wait_ge(loaded_w, 16 * (NW + 1))
            for g in range(B):
                act.wait_ge(norm2.turned, g + 1)
                act.activation(k.xnT[:, g * T:(g + 1) * T], k.bank[g][:], ACT.Identity, bias=lngb[:, 1:2], scale=lngb[:, 0:1])\
                   .then_inc(norm2.xnT_ready, 1)
            act.wait_ge(pool_order, 1)
            for b in range(B):
                for m in range(2 * C):
                    i = b * 2 * C + m
                    act.wait_ge(xz_done, i + 1)
                    bank = k.bank[4 + i % 4]
                    if m < C:
                        act.activation(xp[:, m, b, TAPS - 1:], bank[:], ACT.Copy).then_inc(xz_copied, 1)
                    else:
                        act.activation(zs[:, m - C, b, :], bank[:], ACT.Silu).then_inc(xz_copied, 1)
            for c in range(C):
                act.wait_ge(conv_ready, c + 1)
                act.activation(xc[:, c, :, :], xc[:, c, :, :], ACT.Silu).then_inc(xc_ready, 1)
            for c in range(C):
                for b in range(B):
                    i = c * B + b
                    act.wait_ge(dt_done, i + 1)
                    link(act.activation(dtx[:, c, b, :], k.bank[i % 4][:], ACT.Abs, bias=cols[:, 1, c:c + 1]))
                    act.activation(dtx[:, c, b, :], dtx[:, c, b, :], ACT.Exp, scale=-1.0).then_inc(dt_ready, 1)
            act.wait_ge(dt_ready, C * B)
            link(act.activation(A[:].rearrange("p c n -> p (c n)"), A[:].rearrange("p c n -> p (c n)"), ACT.Exp))
            link(act.activation(A[:].rearrange("p c n -> p (c n)"), A[:].rearrange("p c n -> p (c n)"), ACT.Copy, scale=-1.0))
            for c in range(C):
                act.activation(dtx[:, c, :, :], dtx[:, c, :, :], ACT.Ln, bias=1.0).then_inc(soft_ready, 1)
            for c in range(C):
                act.wait_ge(dtx_ready, c + 1)
                with act.Fori(0, N) as n:
                    for b in range(B):
                        q = c * Q + n * B + b
                        act.wait_ge(b_done, q + 1)
                        act.wait_ge(push_ready, q + 1)
                        act.activation(bsb[:, b, :], k.bank[4 + b % 2][:], ACT.Copy).then_inc(b_copied, 1)
                        act.wait_ge(scanned, q + 1)
                        act.sem_inc(waited, 1)
                        act.activation(keep[:, b, :], dt_[:, c, b, :], ACT.Exp, scale=A[:, c, bass.ds(n, 1)]).then_inc(keep_ready, 1)

        @block.vector
        def _(dve):
            link = Link(dve, order)
            for s, m in ((scanned, 4), (summed, 4), (b_copied, 2), (hc_ready, 4), (push_ready, 4)):
                dve.sem_inc(s, m)
            norm.vector(dve, link)
            dve.wait_ge(norm.xn_ready, NT)
            norm2.statistics(dve, link, k.xn)
            dve.wait_ge(norm2.std_ready, 1)
            link(dve.reciprocal(norm2.rstd[:], norm2.std[:]))
            for t in range(NT):
                dve.tensor_scalar(z2[:, t, :], k.xn[:, t, :], norm2.mv[:, t, 0:1], norm2.rstd[:, t:t + 1],
                                  ALU.subtract, ALU.mult).then_inc(z2_ready, 1)
            dve.wait_ge(loaded_w, 16 * (NW + 1))
            dve.wait_ge(pool_order, 1)
            dve.wait_ge(xz_copied, 2 * C * B)
            for c in range(C):
                link(dve.tensor_scalar(xc[:, c, :, :], xp[:, c, :, 0:T], cw[:, c, 0:1], cols[:, 0, c:c + 1], ALU.mult, ALU.add))
                for j in range(1, TAPS):
                    last = dve.scalar_tensor_tensor(xc[:, c, :, :], xp[:, c, :, j:j + T], cw[:, c, j:j + 1], xc[:, c, :, :], ALU.mult, ALU.add)
                    if j < TAPS - 1:
                        link(last)
                last.then_inc(conv_ready, 1)
            for b in range(B):
                dve.wait_ge(bc_done, b + 1)
                if b:
                    dve.wait_ge(bc_ready, b)
                ps = k.bank[4 + b][0:3 * 2 * N, :]
                G = 2 * N
                link(dve.tensor_copy(t1[:], ps))
                link(dve.tensor_tensor(r1[:], ps, t1[:], ALU.subtract))
                link(dve.tensor_copy(t2[:], r1[:]))
                link(dve.tensor_tensor(r2[:], r1[:], t2[:], ALU.subtract))
                dve.tensor_copy(bc[0:G, b, :], t1[0:G, :])
                dve.tensor_copy(bc[G:2 * G, b, :], t2[G:2 * G, :])
                dve.tensor_copy(bc[2 * G:3 * G, b, :], r2[2 * G:3 * G, :]).then_inc(bc_ready, 1)
            for c in range(C):
                for b in range(B):
                    i = c * B + b
                    dve.wait_ge(dt_done, i + 1)
                    dve.wait_ge(dt_ready, i + 1)
                    dve.tensor_scalar(dt_[:, c, b, :], k.bank[i % 4][:], cols[:, 1, c:c + 1], 0.0, ALU.add, ALU.max).then_inc(gated, 1)
            dve.wait_ge(gated, C * B)
            for c in range(C):
                dve.wait_ge(soft_ready, c + 1)
                link(dve.tensor_tensor(dt_[:, c, :, :], dt_[:, c, :, :], dtx[:, c, :, :], ALU.add))
                dve.tensor_tensor(dtx[:, c, :, :], dt_[:, c, :, :], xc[:, c, :, :], ALU.mult).then_inc(dtx_ready, 1)
            dve.wait_ge(dtx_ready, C)
            for c in range(C):
                dve.tensor_scalar(xc[:, c, :, :], xc[:, c, :, :], cols[:, 2, c:c + 1], None, ALU.mult).then_inc(skip_ready, 1)
            for c in range(C):
                with dve.Fori(0, N) as n:
                    def scan(b):
                        q = c * Q + n * B + b
                        dve.wait_ge(keep_ready, q + 1)
                        dve.wait_ge(push_ready, q + 5)
                        dve.wait_ge(hc_ready, q + 1)
                        dve.tensor_tensor_scan(h[:, b, :], keep[:, b, :], push[:, b, :], 0.0, ALU.mult, ALU.add).then_inc(scanned, 1)

                    def weigh(b):
                        q = c * Q + n * B + b
                        dve.wait_ge(scanned, q + 5)
                        dve.wait_ge(c_done, q + 1)
                        dve.wait_ge(summed, q + 1)
                        dve.tensor_tensor(hc[:, b, :], h[:, b, :], k.bank[6 + b % 2][:], ALU.mult).then_inc(hc_ready, 1)

                    scan(0)
                    for b in range(1, B):
                        scan(b)
                        weigh(b - 1)
                    weigh(B - 1)
                dve.wait_ge(summed, (c + 1) * Q + 4)
                for b in range(B):
                    dve.tensor_tensor(zs[:, c, b, :], zs[:, c, b, :], k.bank[b][:], ALU.mult).then_inc(gated, 1)
            dve.wait_ge(x_ready, 1)
            for g in range(B):
                dve.wait_ge(out_done, g + 1)
                xv = k.x[:, g * TPB:(g + 1) * TPB, :].rearrange("p j d -> p (j d)")
                dve.tensor_tensor(xv, xv, k.bank[4 + g % 4][:], ALU.add).then_inc(added, 1)

        @block.tensor
        def _(pe):
            norm2.tensor(pe, z2, z2_ready)
            pe.wait_ge(loaded_w, 16 * (NW + 1))
            for b in range(B):
                pe.wait_ge(norm2.xnT_ready, b + 1)
                for m in range(2 * C):
                    i = b * 2 * C + m
                    if i >= 4:
                        pe.wait_ge(xz_copied, i - 3)
                    pe.matmul(k.bank[4 + i % 4][:], win[:, m * P:(m + 1) * P], k.xnT[:, b * T:(b + 1) * T], start=True, stop=True).then_inc(xz_done, 1)
            pe.wait_ge(xc_ready, C)
            pe.wait_ge(xz_copied, 2 * C * B)
            for b in range(B):
                for c in range(C):
                    last = pe.matmul(k.bank[4 + b][0:3 * 2 * N, :], wx3[:, c, :, :].rearrange("p r n -> p (r n)"), xc[:, c, b, :], start=(c == 0), stop=(c == C - 1))
                last.then_inc(bc_done, 1)
            for m in range(C):
                for b in range(B):
                    i = m * B + b
                    if i >= 4:
                        pe.wait_ge(gated, i - 3)
                    for c in range(C):
                        last = pe.matmul(k.bank[i % 4][:], wdt[:, c, m * P:(m + 1) * P], xc[:, c, b, :], start=(c == 0), stop=(c == C - 1))
                    last.then_inc(dt_done, 1)
            pe.wait_ge(pool_order, 5)
            pe.wait_ge(bc_ready, B)
            pe.wait_ge(skip_ready, C)
            for c in range(C):
                if c:
                    pe.wait_ge(gated, C * B + c * B)
                else:
                    pe.wait_ge(gated, C * B)
                for b in range(B):
                    pe.matmul(k.bank[b][:], k.ident[:], xc[:, c, b, :], start=True, stop=False, skip_group_check=True)
                with pe.Fori(0, N) as n:
                    def spread_bc(b):
                        q = c * Q + n * B + b
                        pe.wait_ge(b_copied, q + 1)
                        sel = spread[:, bass.ds(n, 1), :].rearrange("r n p -> r (n p)")
                        pe.matmul(k.bank[4 + b % 2][:], sel, bc[:, b, :], start=True, stop=True).then_inc(b_done, 1)
                        pe.wait_ge(hc_ready, q + 3)
                        sel = spread[:, bass.ds(n + N, 1), :].rearrange("r n p -> r (n p)")
                        pe.matmul(k.bank[6 + b % 2][:], sel, bc[:, b, :], start=True, stop=True).then_inc(c_done, 1)

                    spread_bc(0)
                    spread_bc(1)
                    for b in range(B):
                        pe.wait_ge(hc_ready, c * Q + n * B + b + 5)
                        pe.matmul(k.bank[b][:], k.ident[:], hc[:, b, :], start=False, stop=False, skip_group_check=True).then_inc(summed, 1)
                        if b + 2 < B:
                            spread_bc(b + 2)
            pe.wait_ge(gated, C * B + C * B)
            for g in range(B):
                for j in range(TPB):
                    t = g * TPB + j
                    for c in range(C):
                        last = pe.matmul(k.bank[4 + g % 4][:, j * D:(j + 1) * D], zs[:, c, g, j * P:(j + 1) * P], wout[:, c, :], start=(c == 0), stop=(c == C - 1))
                last.then_inc(out_done, 1)



def layer_moe_tokens(k, tag, gate_weight, gate_bias, w_gate, w_up, w_down, s_gate, s_up, s_down, a_gate, a_up, a_down):
    nc = k.nc
    E, I = w_gate.shape[0], w_gate.shape[2]
    L, AI = a_gate.shape[0], a_gate.shape[2]
    SI = s_gate.shape[1]
    NG, TOPK, SCALE, ALPHA = 4, 6, 0.2, 0.1
    GE = E // NG
    ET, AT = E * I // P, L * AI // P
    TILES = ET + AT + 1
    LOW, HIT = -1e30, 3e38
    STK = 3 * E + L
    with ExitStack() as ctx:
        def sb(name, shape, dt=F32):
            return k.sb(f"{tag}_{name}", shape, dt, ctx)

        def sem(name):
            return k.sem(f"{tag}_{name}")

        norm = Norm(k, tag, ctx)
        gw = sb("gw", [E, D])
        gwT = sb("gwT", [D, E])
        gb = sb("gb", [P, E])
        wg = sb("wg", [D, TILES * P])
        wu = sb("wu", [D, TILES * P])
        wd = sb("wd", [P, TILES, D])
        score = sb("score", [P, NT, E])
        sc = sb("sc", [P, NT, E])
        hi = sb("hi", [P, NT * NG, GE // 2])
        lo = sb("lo", [P, NT * NG, GE // 2])
        hi2 = sb("hi2", [P, NT * NG, GE // 4])
        lo2 = sb("lo2", [P, NT * NG, GE // 4])
        t2 = sb("t2", [P, NT * NG, GE // 4])
        top1 = sb("top1", [P, NT * NG])
        top2 = sb("top2", [P, NT * NG])
        gs = sb("gs", [P, NT, NG])
        wins = sb("wins", [P, NT, NG])
        duel = sb("duel", [P, 6, NT])
        gmask = sb("gmask", [P, NT, NG])
        masked = sb("masked", [P, NT, E])
        low = sb("low", [P, NT, E])
        best = sb("best", [P, NT, 8])
        only1 = sb("only1", [P, NT, 8])
        work = sb("work", [P, NT, E])
        work1 = sb("work1", [P, NT, E])
        total = sb("total", [P, NT])
        rtotal = sb("rtotal", [P, NT])
        cw = sb("cw", [P, NT, E])
        rest = sb("rest", [P, NT, E])
        stack = sb("stack", [P, NT, STK], BF16)
        stackT = sb("stackT", [STK, B * T], BF16)
        spread = sb("spread", [P, (ET + AT) * P], BF16)
        silu = sb("silu", [P, 2, T])
        gated = sb("gated", [P, 2, T])
        hidden = sb("hidden", [P, 2, T])

        loaded_gw, loaded_w = sem("loaded_gw"), sem("loaded_w")
        order, spread_made = sem("order"), sem("spread_made")
        gwT_turned, gwT_ready = sem("gwT_turned"), sem("gwT_ready")
        logits_ready, score_ready = sem("logits_ready"), sem("score_ready")
        stack_ready, stack_turned, stackT_ready = sem("stack_ready"), sem("stack_turned"), sem("stackT_ready")
        in_ready, silu_ready, hidden_ready = sem("in_ready"), sem("silu_ready"), sem("hidden_ready")
        down_done, acc_used = sem("down_done"), sem("acc_used")

        block = ctx.enter_context(nc.Block())
        NW = 9

        @block.sync
        def _(sp):
            sp.dma_start(gw[:], gate_weight).then_inc(loaded_gw, 16)
            sp.dma_start(gb[:], gate_bias.partition_broadcast(P)).then_inc(loaded_gw, 16)
            for dst, e, l, s in ((wg, w_gate, a_gate, s_gate), (wu, w_up, a_up, s_up)):
                sp.dma_start(dst[:, 0:E * I].rearrange("h (e i) -> h e i", i=I), e.rearrange("e h i -> h e i")).then_inc(loaded_w, 16)
                sp.dma_start(dst[:, E * I:E * I + L * AI].rearrange("h (e i) -> h e i", i=AI),
                             l.rearrange("e h i -> h e i")).then_inc(loaded_w, 16)
                sp.dma_start(dst[:, E * I + L * AI:E * I + L * AI + SI], s).then_inc(loaded_w, 16)
            sp.dma_start(wd[:, 0:ET, :], w_down.rearrange("(t e) i d -> (e i) t d", e=P // I)).then_inc(loaded_w, 16)
            sp.dma_start(wd[:, ET:ET + AT, :], a_down.rearrange("(t e) i d -> (e i) t d", e=P // AI)).then_inc(loaded_w, 16)
            sp.dma_start(wd[0:SI, ET + AT, :], s_down).then_inc(loaded_w, 16)

        @block.gpsimd
        def _(pool):
            k.clear_past()
            link = Link(pool, spread_made)
            link(pool.memset(wg[:, TILES * P - (P - SI):], 0.0))
            link(pool.memset(wu[:, TILES * P - (P - SI):], 0.0))
            link(pool.memset(wd[SI:P, TILES - 1, :], 0.0))
            link(pool.memset(spread[:], 0.0))
            for part in range(3):
                v = spread[:, 0:ET * P].rearrange("r (e i) -> r e i", i=I)
                link(pool.affine_select(out=v, in_=v, compare_op=ALU.not_equal, fill=1.0, base=-E * part,
                                        pattern=[[-1, E], [0, I]], channel_multiplier=1))
            v = spread[:, ET * P:].rearrange("r (e i) -> r e i", i=AI)
            link(pool.affine_select(out=v, in_=v, compare_op=ALU.not_equal, fill=1.0, base=-3 * E,
                                    pattern=[[-1, L], [0, AI]], channel_multiplier=1))

        @block.scalar
        def _(act):
            norm.scalar_sqrt(act)
            norm.scalar_copy(act)
            act.wait_ge(logits_ready, 1)
            act.activation(score[:].rearrange("p j e -> p (j e)"), k.bank[5][:], ACT.Sigmoid).then_inc(score_ready, 1)
            for g in range(2):
                act.wait_ge(stack_turned, g + 1)
                act.activation(stackT[:, g * 1024:(g + 1) * 1024], k.bank[6 + g][0:STK, :].bitcast(BF16), ACT.Copy)\
                   .then_inc(stackT_ready, 1)
            with act.Fori(0, B) as c:
                for t in range(TILES):
                    act.wait_ge(in_ready, c * TILES + t + 1)
                    act.wait_ge(hidden_ready, c * TILES + t + (1 if t else 2))
                    act.activation(silu[:, t % 2, :], k.bank[t % 2][:, :], ACT.Silu).then_inc(silu_ready, 1)

        @block.vector
        def _(dve):
            link = Link(dve, order)
            dve.sem_inc(hidden_ready, 2)
            dve.sem_inc(down_done, 2)
            dve.sem_inc(acc_used, 1)
            norm.vector(dve, link)
            dve.wait_ge(gwT_turned, 1)
            dve.tensor_copy(gwT[:], k.bank[4][:, 0:E]).then_inc(gwT_ready, 1)
            dve.wait_ge(loaded_gw, 32)
            dve.wait_ge(score_ready, 1)
            link(dve.tensor_tensor(sc[:], score[:], bcast(gb[:, 0:1], (0, NT), (1, E)), ALU.add))
            g8 = sc[:].rearrange("p j (g e) -> p (j g) e", e=GE)
            h = GE // 2
            dve.tensor_tensor(hi[:], g8[:, :, 0:h], g8[:, :, h:GE], ALU.max)
            link(dve.tensor_tensor(lo[:], g8[:, :, 0:h], g8[:, :, h:GE], ALU.min))
            q = h // 2
            dve.tensor_tensor(t2[:], hi[:, :, 0:q], hi[:, :, q:h], ALU.min)
            dve.tensor_tensor(lo2[:], lo[:, :, 0:q], lo[:, :, q:h], ALU.max)
            link(dve.tensor_tensor(hi2[:], hi[:, :, 0:q], hi[:, :, q:h], ALU.max))
            link(dve.tensor_tensor(lo2[:], lo2[:], t2[:], ALU.max))
            dve.tensor_tensor(top1[:], hi2[:, :, 0], hi2[:, :, 1], ALU.max)
            dve.tensor_tensor(t2[:, :, 0], hi2[:, :, 0], hi2[:, :, 1], ALU.min)
            link(dve.tensor_tensor(top2[:], lo2[:, :, 0], lo2[:, :, 1], ALU.max))
            link(dve.tensor_tensor(top2[:], top2[:], t2[:, :, 0], ALU.max))
            link(dve.tensor_tensor(gs[:].rearrange("p j g -> p (j g)"), top1[:], top2[:], ALU.add))
            pairs = [(a, b) for a in range(NG) for b in range(a + 1, NG)]
            dve.memset(wins[:], 0.0)
            for n, (a, b) in enumerate(pairs):
                last = dve.tensor_tensor(duel[:, n, :], gs[:, :, a], gs[:, :, b], ALU.is_ge)
            link(last)
            for n, (a, b) in enumerate(pairs):
                link(dve.tensor_tensor(wins[:, :, a], wins[:, :, a], duel[:, n, :], ALU.add))
                link(dve.scalar_tensor_tensor(wins[:, :, b], duel[:, n, :], -1.0, wins[:, :, b], ALU.mult, ALU.add))
            for g in range(NG):
                last = dve.tensor_scalar(gmask[:, :, g], wins[:, :, g], float(g), 2.0, ALU.add, ALU.is_ge)
            link(last)
            emask = bcast(gmask[:, 0, 0:1], (1, NT * NG), (0, GE))
            link(dve.tensor_scalar(low[:].rearrange("p j (g e) -> p (j g) e", e=GE), emask, -LOW, LOW, ALU.mult, ALU.add))
            link(dve.tensor_tensor(masked[:].rearrange("p j (g e) -> p (j g) e", e=GE), g8, emask, ALU.mult))
            link(dve.tensor_tensor(masked[:], masked[:], low[:], ALU.add))
            for j in range(NT):
                last = dve.max(best[:, j, :], masked[:, j, :])
            link(last)
            dve.memset(only1[:, :, 1:8], LOW)
            dve.tensor_copy(only1[:, :, 0], best[:, :, 0])
            link(dve.memset(best[:, :, TOPK:8], LOW))
            for j in range(NT):
                dve.match_replace(work[:, j, :], best[:, j, :], masked[:, j, :], HIT)
                last = dve.match_replace(work1[:, j, :], only1[:, j, :], masked[:, j, :], HIT)
            link(last)
            w8 = work[:].rearrange("p j (g e) -> p (j g) e", e=GE)
            w18 = work1[:].rearrange("p j (g e) -> p (j g) e", e=GE)
            dve.scalar_tensor_tensor(w8, w8, HIT, emask, ALU.is_equal, ALU.mult)
            link(dve.scalar_tensor_tensor(w18, w18, HIT, emask, ALU.is_equal, ALU.mult))
            dve.tensor_tensor(stack[:, :, 3 * E:], work1[:, :, 0::2], work1[:, :, 1::2], ALU.add)
            link(dve.tensor_tensor(cw[:], work[:], score[:], ALU.mult))
            link(dve.tensor_reduce(total[:], cw[:], AX_X, ALU.add))
            link(dve.tensor_scalar(total[:], total[:], 1e-20, None, ALU.add))
            link(dve.reciprocal(rtotal[:], total[:]))
            link(dve.scalar_tensor_tensor(cw[:], cw[:], SCALE, bcast(rtotal[:, 0:1], (1, NT), (0, E)), ALU.mult, ALU.mult))
            link(dve.tensor_copy(stack[:, :, 0:E], cw[:]))
            link(dve.tensor_tensor(rest[:], cw[:], stack[:, :, 0:E], ALU.subtract))
            link(dve.tensor_copy(stack[:, :, E:2 * E], rest[:]))
            link(dve.tensor_tensor(rest[:], rest[:], stack[:, :, E:2 * E], ALU.subtract))
            dve.tensor_copy(stack[:, :, 2 * E:3 * E], rest[:]).then_inc(stack_ready, 1)
            with dve.Fori(0, B) as c:
                link.start(c, TILES - 1)
                for t in range(TILES):
                    sl, up, wt = silu[:, t % 2, :], k.bank[2 + t % 2][:, :], k.bank[4 + t % 2][:, :]
                    dve.wait_ge(silu_ready, c * TILES + t + 1)
                    dve.wait_ge(down_done, c * TILES + t + (1 if t else 2))
                    if t == TILES - 1:
                        dve.tensor_tensor(hidden[:, t % 2, :], sl, up, ALU.mult).then_inc(hidden_ready, 1)
                        continue
                    link(dve.scalar_tensor_tensor(gated[:, t % 2, :], sl, 1.0 if t < ET else ALPHA, up, ALU.mult, ALU.mult))
                    dve.tensor_tensor(hidden[:, t % 2, :], gated[:, t % 2, :], wt, ALU.mult).then_inc(hidden_ready, 1)
                dve.wait_ge(down_done, (c + 1) * TILES + 2)
                xc = k.x[:].rearrange("p j d -> p (j d)")[:, bass.ds(c * T, T)]
                dve.tensor_tensor(xc, xc, k.bank[6][:], ALU.add).then_inc(acc_used, 1)
                link.end(TILES - 1, B)

        @block.tensor
        def _(pe):
            norm.tensor(pe)
            pe.wait_ge(loaded_gw, 32)
            pe.transpose(k.bank[4][:, 0:E], gw[:], k.ident[0:E, 0:E]).then_inc(gwT_turned, 1)
            pe.wait_ge(gwT_ready, 1)
            pe.wait_ge(norm.xnT_ready, B)
            for j in range(NT):
                last = pe.matmul(k.bank[5][:, j * E:(j + 1) * E], k.xnT[:, j * P:(j + 1) * P], gwT[:], start=True, stop=True)
            last.then_inc(logits_ready, 1)
            pe.wait_ge(stack_ready, 1)
            for j in range(NT):
                g, o = 6 + j // 8, j % 8
                last = pe.transpose(k.bank[g][0:STK, :].bitcast(BF16)[:, o * P:(o + 1) * P], stack[:, j, :], k.ident16[:])
                if o == 7:
                    last.then_inc(stack_turned, 1)
            pe.wait_ge(stackT_ready, 2)
            pe.wait_ge(loaded_w, 16 * NW)
            pe.wait_ge(spread_made, 8)
            with pe.Fori(0, B) as c:
                xc = k.xnT[:, bass.ds(c * T, T)]
                wc = stackT[:, bass.ds(c * T, T)]

                def products(t):
                    pe.wait_ge(hidden_ready, c * TILES + t + (1 if t else 2))
                    pe.matmul(k.bank[2 + t % 2][:, :], wu[:, t * P:(t + 1) * P], xc, start=True, stop=True)
                    if t < TILES - 1:
                        pe.matmul(k.bank[4 + t % 2][:], spread[0:STK, t * P:(t + 1) * P], wc, start=True, stop=True)
                    pe.matmul(k.bank[t % 2][:, :], wg[:, t * P:(t + 1) * P], xc, start=True, stop=True).then_inc(in_ready, 1)

                def down(t):
                    pe.wait_ge(hidden_ready, c * TILES + t + 3)
                    if t == 0:
                        pe.wait_ge(acc_used, c + 1)
                    for j in range(TPB):
                        last = pe.matmul(k.bank[6][:, j * D:(j + 1) * D], hidden[:, t % 2, j * P:(j + 1) * P],
                                         wd[:, t, :], start=(t == 0 and j == 0), stop=(t == TILES - 1), skip_group_check=True)
                    last.then_inc(down_done, 1)

                products(0)
                for t in range(TILES):
                    if t + 1 < TILES:
                        products(t + 1)
                    down(t)



def layer_delta(k, tag, Wq, Wk, Wv, Wb, conv_q, conv_k, conv_v, g, Wo):
    nc = k.nc
    H = Wb.shape[1]
    HD = D // H
    TAPS = conv_q.shape[2]
    CH = 64
    NCH = T // CH
    LEVELS = CH.bit_length() - 1
    with ExitStack() as ctx:
        def sb(name, shape, dt=F32):
            return k.sb(f"{tag}_{name}", shape, dt, ctx)

        def sem(name):
            return k.sem(f"{tag}_{name}")

        norm = Norm(k, tag, ctx)
        w3 = sb("w3", [D, 3, D])
        wb = sb("wb", [D, H])
        wbr = sb("wbr", [D, H, HD])
        wo = sb("wo", [D, D])
        cw = sb("cw", [P, 3, TAPS])
        gc = sb("gc", [P, 1])
        xp = sb("xp", [P, 3, B, TAPS - 1 + T])
        s3 = sb("s3", [P, 3, B, T])
        beta = sb("beta", [P, B, T])
        kb = sb("kb", [P, B, T])
        heads = sb("heads", [P, P])
        ones = sb("ones", [P, P])
        ident2 = sb("ident2", [P, P])
        masks = sb("masks", [P, LEVELS, P])
        kbn = sb("kbn", [P, NT, D])
        vbn = sb("vbn", [P, NT, D])
        aT = sb("aT", [P, B, T])
        cT = sb("cT", [P, B, T])
        m = sb("m", [P, B, T])
        mT = sb("mT", [P, B, T])
        xx = sb("xx", [P, B, T])
        wT = sb("wT", [P, B, T])
        prod = sb("prod", [P, T])
        ka = sb("ka", [P, B, NCH])
        kbv = sb("kbv", [P, B, NCH])
        sd = sb("sd", [P, B, NCH + 1])
        early = sb("early", [P, B, NCH, B])
        qk = sb("qk", [P, B, NCH, B])
        u0 = sb("u0", [P, B, NCH, B])
        sq = xx
        uT = beta
        o = cT

        loaded_w = sem("loaded_w")
        order, pool_order = sem("order"), sem("pool_order")
        in_done, in_copied, conv_ready, act_ready = sem("in_done"), sem("in_copied"), sem("conv_ready"), sem("act_ready")
        wbr_ready, beta_done, beta_ready = sem("wbr_ready"), sem("beta_done"), sem("beta_ready")
        sq_ready, norm_done, root_ready, unit_ready = sem("sq_ready"), sem("norm_done"), sem("root_ready"), sem("unit_ready")
        kb_ready, vb_ready, a_done, aT_ready = sem("kb_ready"), sem("vb_ready"), sem("a_done"), sem("aT_ready")
        n_turned, n_ready = sem("n_turned"), sem("n_ready")
        cT_ready, x_done, x_ready, y_done, yT_done, m_ready, mT_ready = (sem("cT_ready"), sem("x_done"), sem("x_ready"), sem("y_done"),
                                                                          sem("yT_done"), sem("m_ready"), sem("mT_ready"))
        t_ready, wu_done, w_copied, u_copied = sem("t_ready"), sem("wu_done"), sem("w_copied"), sem("u_copied")
        qk_ready, qk_done, o_ready, osq_ready, on_done, oroot_ready, on_ready, out_done = (
            sem("qk_ready"), sem("qk_done"), sem("o_ready"), sem("osq_ready"), sem("on_done"), sem("oroot_ready"), sem("on_ready"), sem("out_done"))
        NW = 5 + 3 + H

        block = ctx.enter_context(nc.Block())

        def flat(ap):
            return ap.rearrange("p b t -> p (b t)")

        @block.sync
        def _(sp):
            for i, w in enumerate((Wq, Wk, Wv)):
                sp.dma_start(w3[:, i, :], w).then_inc(loaded_w, 16)
            sp.dma_start(wb[:], Wb).then_inc(loaded_w, 16)
            sp.dma_start(wo[:], Wo).then_inc(loaded_w, 16)
            for i, w in enumerate((conv_q, conv_k, conv_v)):
                sp.dma_start(cw[:, i, :], w.rearrange("d a k -> d (a k)")).then_inc(loaded_w, 16)
            for h in range(H):
                sp.dma_start(gc[h * HD:(h + 1) * HD, :], g.rearrange("(d a) -> d a", a=1)).then_inc(loaded_w, 16)

        @block.gpsimd
        def _(pool):
            k.clear_past()
            link = Link(pool, pool_order)
            link(pool.memset(xp[:, :, :, 0:TAPS - 1], 0.0))
            link(pool.memset(ones[:], 1.0))
            hv = heads[:].rearrange("p (h d) -> p h d", d=HD)
            link(pool.memset(heads[:], 1.0))
            link(pool.affine_select(out=hv, in_=hv, compare_op=ALU.is_ge, fill=0.0, base=0, pattern=[[-HD, H], [0, HD]], channel_multiplier=1))
            link(pool.affine_select(out=hv, in_=hv, compare_op=ALU.is_ge, fill=0.0, base=HD - 1, pattern=[[HD, H], [0, HD]], channel_multiplier=-1))
            link(pool.memset(masks[:], 0.0))
            for l in range(LEVELS):
                s = 1 << l
                v = masks[:, l, :].rearrange("p (n a s) -> p n a s", a=2, s=s)[:, :, 1, :]
                link(pool.memset(v, 1.0))
                link(pool.affine_select(out=v, in_=v, compare_op=ALU.is_ge, fill=0.0, base=0, pattern=[[-2 * s, P // (2 * s)], [0, s]], channel_multiplier=1))
                link(pool.affine_select(out=v, in_=v, compare_op=ALU.is_ge, fill=0.0, base=s - 1, pattern=[[2 * s, P // (2 * s)], [0, s]], channel_multiplier=-1))
            link(pool.memset(sd[:, :, 0:1], 0.0))
            link(pool.memset(early[:], 1.0))
            link(pool.affine_select(out=early[:], in_=early[:], compare_op=ALU.is_ge, fill=0.0, base=0,
                                    pattern=[[1, B], [0, NCH], [-1, B]], channel_multiplier=0))
            link(pool.tensor_scalar(ident2[:], k.ident[:], 2.0, None, ALU.mult))
            for l in range(LEVELS):
                for b in range(B):
                    pool.wait_ge(aT_ready, b + 1)
                    if l:
                        pool.wait_ge(x_done, (l - 1) * B + b + 1)
                        if l == 1:
                            pool.wait_ge(mT_ready, b + 1)
                    pool.tensor_tensor(cT[:, b, :].rearrange("p (j i) -> p j i", i=P), aT[:, b, :].rearrange("p (j i) -> p j i", i=P),
                                       bcast(masks[:, l, 0:1], (0, TPB), (1, P)), ALU.mult).then_inc(cT_ready, 1)

        @block.scalar
        def _(act):
            norm.scalar_sqrt(act)
            norm.scalar_copy(act)
            act.wait_ge(pool_order, 1)
            for b in range(B):
                for i in range(3):
                    n = b * 3 + i
                    act.wait_ge(in_done, n + 1)
                    act.activation(xp[:, i, b, TAPS - 1:], k.bank[4 + n % 4][:], ACT.Copy).then_inc(in_copied, 1)
            for i in range(3):
                act.wait_ge(conv_ready, i + 1)
                act.activation(s3[:, i, :, :], s3[:, i, :, :], ACT.Silu).then_inc(act_ready, 1)
            for b in range(B):
                act.wait_ge(beta_done, b + 1)
                act.activation(beta[:, b, :], k.bank[b][:], ACT.Sigmoid).then_inc(beta_ready, 1)
            for n in range(2 * B):
                act.wait_ge(norm_done, n + 1)
                act.activation(xp[:, n // B, n % B, 0:T], k.bank[4 + n % 4][:], ACT.Sqrt).then_inc(root_ready, 1)
            for n in range(2 * B):
                act.wait_ge(n_turned, n + 1)
                dst = (kbn, vbn)[n // B]
                act.activation(dst[:, (n % B) * TPB:(n % B + 1) * TPB, :].rearrange("p j d -> p (j d)"), k.bank[n % 2][:], ACT.Copy).then_inc(n_ready, 1)
            for l in range(1, LEVELS):
                for b in range(B):
                    act.wait_ge(x_done, l * B + b + 1)
                    if l > 1:
                        act.wait_ge(yT_done, (l - 2) * B + b + 1)
                    act.activation(xx[:, b, :], k.bank[b % 2][:], ACT.Copy).then_inc(x_ready, 1)
            for b in range(B):
                act.wait_ge(wu_done, b + 1)
                act.activation(wT[:, b, :], k.bank[b % 2][:], ACT.Copy).then_inc(w_copied, 1)
            for b in range(B):
                act.wait_ge(o_ready, b + 1)
                act.activation(sq[:, b, :], o[:, b, :], ACT.Square).then_inc(osq_ready, 1)
            for b in range(B):
                act.wait_ge(on_done, b + 1)
                act.activation(wT[:, b, :], k.bank[4 + b][:], ACT.Sqrt, scale=1.0 / HD, bias=k.eps[:, 0:1]).then_inc(oroot_ready, 1)

        @block.vector
        def _(dve):
            link = Link(dve, order)
            norm.vector(dve, link)
            dve.wait_ge(loaded_w, 16 * NW)
            dve.tensor_copy(wbr[:], bcast(wb[:, 0:1], (1, H), (0, HD))).then_inc(wbr_ready, 1)
            dve.wait_ge(in_copied, 3 * B)
            for i in range(3):
                link(dve.tensor_scalar(s3[:, i, :, :], xp[:, i, :, 0:T], cw[:, i, 0:1], None, ALU.mult))
                for j in range(1, TAPS):
                    last = dve.scalar_tensor_tensor(s3[:, i, :, :], xp[:, i, :, j:j + T], cw[:, i, j:j + 1], s3[:, i, :, :], ALU.mult, ALU.add)
                    if j < TAPS - 1:
                        link(last)
                last.then_inc(conv_ready, 1)
            for i in range(2):
                dve.wait_ge(act_ready, i + 1)
                for b in range(B):
                    n = i * B + b
                    if i:
                        dve.wait_ge(norm_done, b + 1)
                    dve.tensor_tensor(sq[:, b, :], s3[:, i, b, :], s3[:, i, b, :], ALU.mult).then_inc(sq_ready, 1)
            for n in range(2 * B):
                i, b = n // B, n % B
                dve.wait_ge(root_ready, n + 1)
                link(dve.reciprocal(xp[:, i, b, 0:T], xp[:, i, b, 0:T]))
                last = dve.tensor_tensor(s3[:, i, b, :], s3[:, i, b, :], xp[:, i, b, 0:T], ALU.mult)
                last.then_inc(unit_ready, 1)
            dve.wait_ge(unit_ready, 2 * B)
            dve.wait_ge(act_ready, 3)
            for b in range(B):
                dve.wait_ge(beta_ready, b + 1)
                dve.tensor_tensor(kb[:, b, :], s3[:, 1, b, :], beta[:, b, :], ALU.mult).then_inc(kb_ready, 1)
            for b in range(B):
                dve.tensor_tensor(s3[:, 2, b, :], s3[:, 2, b, :], beta[:, b, :], ALU.mult).then_inc(vb_ready, 1)
            for b in range(B):
                dve.wait_ge(a_done, b + 1)
                dve.tensor_copy(aT[:, b, :], k.bank[4 + b % 2][:]).then_inc(aT_ready, 1)
            idb = bcast(k.ident[:, 0:1], (0, TPB), (1, P))
            for b in range(B):
                dve.wait_ge(x_done, b + 1)
                dve.wait_ge(cT_ready, b + 1)
                dve.tensor_tensor(m[:, b, :].rearrange("p (j i) -> p j i", i=P), idb, k.bank[b % 2][:].rearrange("p (j i) -> p j i", i=P), ALU.subtract)\
                    .then_inc(m_ready, 1)
                dve.tensor_tensor(mT[:, b, :].rearrange("p (j i) -> p j i", i=P), idb, cT[:, b, :].rearrange("p (j i) -> p j i", i=P), ALU.subtract)\
                    .then_inc(mT_ready, 1)
            for l in range(1, LEVELS):
                for b in range(B):
                    n = (l - 1) * B + b
                    dve.wait_ge(yT_done, n + 1)
                    dve.wait_ge(m_ready, l * B)
                    dve.wait_ge(mT_ready, l * B)
                    dve.tensor_tensor(m[:, b, :], m[:, b, :], k.bank[4 + b % 2][:], ALU.subtract).then_inc(m_ready, 1)
                    dve.tensor_tensor(mT[:, b, :], mT[:, b, :], k.bank[6 + b % 2][:], ALU.subtract).then_inc(mT_ready, 1)
            dve.wait_ge(mT_ready, LEVELS * B)
            id2 = bcast(ident2[:, 0:1], (0, TPB), (1, P))
            for b in range(B):
                mv = mT[:, b, :].rearrange("p (j i) -> p j i", i=P)
                dve.scalar_tensor_tensor(mv, mv, 3.0, id2, ALU.mult, ALU.subtract).then_inc(t_ready, 1)
            for b in range(B):
                dve.wait_ge(wu_done, b + 1)
                dve.tensor_copy(uT[:, b, :], k.bank[2 + b % 2][:]).then_inc(u_copied, 1)
            dve.wait_ge(u_copied, B)
            dve.wait_ge(w_copied, B)
            for src, dst in ((wT, ka), (uT, kbv)):
                for b in range(B):
                    link(dve.tensor_tensor(prod[:], s3[:, 1, b, :], src[:, b, :], ALU.mult))
                    link(dve.tensor_reduce(dst[:, b, :], prod[:].rearrange("p (n c) -> p n c", c=CH), AX_X, ALU.add))
            link(dve.tensor_scalar(ka[:], ka[:], -1.0, 1.0, ALU.mult, ALU.add))
            for b in range(B):
                last = dve.tensor_tensor_scan(sd[:, b, 1:NCH + 1], ka[:, b, :], kbv[:, b, :], 0.0, ALU.mult, ALU.add)
            link(last)
            def first(ap):
                return ap.rearrange("p b (n c) -> p b n c", c=CH)[:, :, :, 0:B]

            dve.tensor_tensor(qk[:], first(s3[:, 0, :, :]), first(s3[:, 1, :, :]), ALU.mult).then_inc(qk_ready, 1)
            for b in range(B):
                sdb = bcast(sd[:, b, 0:1], (1, NCH), (0, B))
                last = dve.tensor_tensor(u0[:, b, :, :], first(wT[:])[:, b], sdb, ALU.mult)
            link(last)
            link(dve.tensor_tensor(u0[:], first(uT[:]), u0[:], ALU.subtract))
            link(dve.tensor_tensor(u0[:], u0[:], early[:], ALU.mult))
            dve.wait_ge(qk_done, 1)
            link(dve.tensor_tensor(u0[:], u0[:], k.bank[4][:, 0:B * NCH * B].rearrange("p (b n c) -> p b n c", b=B, n=NCH), ALU.mult))
            for b in range(B):
                ov = o[:, b, :].rearrange("p (n c) -> p n c", c=CH)
                link(dve.tensor_tensor(ov, s3[:, 0, b, :].rearrange("p (n c) -> p n c", c=CH), bcast(sd[:, b, 0:1], (1, NCH), (0, CH)), ALU.mult))
                dve.tensor_tensor(ov[:, :, 0:B], ov[:, :, 0:B], u0[:, b, :, :], ALU.add).then_inc(o_ready, 1)
            dve.wait_ge(o_ready, B)
            for b in range(B):
                dve.wait_ge(oroot_ready, b + 1)
                link(dve.reciprocal(wT[:, b, :], wT[:, b, :]))
                dve.scalar_tensor_tensor(o[:, b, :], o[:, b, :], gc[:, 0:1], wT[:, b, :], ALU.mult, ALU.mult).then_inc(on_ready, 1)
            for b in range(B):
                dve.wait_ge(out_done, b + 1)
                xv = k.x[:, b * TPB:(b + 1) * TPB, :].rearrange("p j d -> p (j d)")
                dve.tensor_tensor(xv, xv, k.bank[b][:], ALU.add)

        @block.tensor
        def _(pe):
            norm.tensor(pe)
            pe.wait_ge(loaded_w, 16 * NW)
            for b in range(B):
                pe.wait_ge(norm.xnT_ready, b + 1)
                for i in range(3):
                    n = b * 3 + i
                    if n >= 4:
                        pe.wait_ge(in_copied, n - 3)
                    pe.matmul(k.bank[4 + n % 4][:], w3[:, i, :], k.xnT[:, b * T:(b + 1) * T], start=True, stop=True).then_inc(in_done, 1)
            pe.wait_ge(wbr_ready, 1)
            for b in range(B):
                pe.matmul(k.bank[b][:], wbr[:].rearrange("p h d -> p (h d)"), k.xnT[:, b * T:(b + 1) * T], start=True, stop=True).then_inc(beta_done, 1)
            pe.wait_ge(pool_order, 5)
            pe.wait_ge(in_copied, 3 * B)
            for n in range(2 * B):
                pe.wait_ge(sq_ready, n + 1)
                if n >= 4:
                    pe.wait_ge(root_ready, n - 3)
                pe.matmul(k.bank[4 + n % 4][:], heads[:], sq[:, n % B, :], start=True, stop=True).then_inc(norm_done, 1)
            pe.wait_ge(beta_ready, B)
            for n in range(2 * B):
                i, b = n // B, n % B
                pe.wait_ge((kb_ready, vb_ready)[i], b + 1)
                if n >= 2:
                    pe.wait_ge(n_ready, n - 1)
                for j in range(TPB):
                    src = (kb[:, b, j * P:(j + 1) * P], s3[:, 2, b, j * P:(j + 1) * P])[i]
                    last = pe.transpose(k.bank[n % 2][:, j * P:(j + 1) * P], src, k.ident[:])
                last.then_inc(n_turned, 1)
            pe.wait_ge(root_ready, 2 * B)
            for b in range(B):
                if b >= 2:
                    pe.wait_ge(aT_ready, b - 1)
                for j in range(TPB):
                    c = slice(j * P, (j + 1) * P)
                    last = pe.matmul(k.bank[4 + b % 2][:, c], s3[:, 1, b, c], kb[:, b, c], start=True, stop=True)
                last.then_inc(a_done, 1)
            pe.wait_ge(n_ready, 2 * B)
            pe.wait_ge(aT_ready, B)
            for b in range(B):
                pe.wait_ge(cT_ready, b + 1)
                if b >= 2:
                    pe.wait_ge(m_ready, b - 1)
                for j in range(TPB):
                    c = slice(j * P, (j + 1) * P)
                    last = pe.transpose(k.bank[b % 2][:, c], cT[:, b, c], k.ident[:])
                last.then_inc(x_done, 1)
            for l in range(1, LEVELS):
                def cross(b):
                    pe.wait_ge(cT_ready, l * B + b + 1)
                    pe.wait_ge(m_ready, l * B if l == 1 else (l - 1) * B + b + 1)
                    if (l - 1) * B + b >= 2:
                        pe.wait_ge(x_ready, (l - 1) * B + b - 1)
                    for j in range(TPB):
                        c = slice(j * P, (j + 1) * P)
                        last = pe.matmul(k.bank[b % 2][:, c], cT[:, b, c], m[:, b, c], start=True, stop=True)
                    last.then_inc(x_done, 1)

                def close(b):
                    n = (l - 1) * B + b
                    pe.wait_ge(x_ready, n + 1)
                    pe.wait_ge(mT_ready, B + n if n >= B else B)
                    if n >= 2:
                        pe.wait_ge(mT_ready, B + n - 1)
                    for j in range(TPB):
                        c = slice(j * P, (j + 1) * P)
                        pe.matmul(k.bank[4 + b % 2][:, c], mT[:, b, c], xx[:, b, c], start=True, stop=True)
                    for j in range(TPB):
                        c = slice(j * P, (j + 1) * P)
                        last = pe.matmul(k.bank[6 + b % 2][:, c], xx[:, b, c], mT[:, b, c], start=True, stop=True)
                    last.then_inc(yT_done, 1)

                cross(0)
                for b in range(B):
                    if b + 1 < B:
                        cross(b + 1)
                    close(b)
            pe.wait_ge(x_ready, (LEVELS - 1) * B)
            for b in range(B):
                pe.wait_ge(t_ready, b + 1)
                if b >= 2:
                    pe.wait_ge(w_copied, b - 1)
                    pe.wait_ge(u_copied, b - 1)
                for src, bank in ((kbn, k.bank[b % 2]), (vbn, k.bank[2 + b % 2])):
                    for j in range(TPB):
                        c = slice(j * P, (j + 1) * P)
                        last = pe.matmul(bank[:, c], src[:, b * TPB + j, :], mT[:, b, c], start=True, stop=True)
                last.then_inc(wu_done, 1)
            pe.wait_ge(qk_ready, 1)
            pe.matmul(k.bank[4][:, 0:B * NCH * B], ones[:], qk[:].rearrange("p b n c -> p (b n c)"), start=True, stop=True).then_inc(qk_done, 1)
            pe.wait_ge(o_ready, B)
            for b in range(B):
                pe.wait_ge(osq_ready, b + 1)
                pe.matmul(k.bank[4 + b][:], heads[:], sq[:, b, :], start=True, stop=True).then_inc(on_done, 1)
            for b in range(B):
                pe.wait_ge(on_ready, b + 1)
                for j in range(TPB):
                    c = slice(j * P, (j + 1) * P)
                    last = pe.matmul(k.bank[b][:, c], o[:, b, c], wo[:], start=True, stop=True)
                last.then_inc(out_done, 1)


def build(nc, a, out):
    with ExitStack() as ctx:
        k = Core(nc, ctx)
        x_loaded, made = k.sem("x_loaded"), k.sem("made")
        with nc.Block() as block:
            @block.sync
            def _(sp):
                sp.dma_start(k.x[:], a["L0_attn_a_x"].rearrange("b (j p) d -> p (b j) d", p=P)).then_inc(x_loaded, 16)
                sp.wait_ge(x_loaded, 16)

            @block.gpsimd
            def _(pool):
                link = Link(pool, made)
                link(pool.memset(k.eps[:], LN_EPS))
                pool.memset(k.ident16[:], 0.0)
                link(pool.memset(k.ident[:], 0.0))
                for m in (k.ident, k.ident16):
                    pool.affine_select(out=m[:], in_=m[:], compare_op=ALU.not_equal, fill=1.0,
                                       base=0, pattern=[[-1, P]], channel_multiplier=1)
        l0a = [a[f"L0_attn_a_{n}"] for n in ("w_qkv", "b_qkv", "w_out", "b_out", "w1_rpe", "b1_rpe", "w2_rpe", "b2_rpe")]
        l0f = [a[f"L0_ffn_{n}"] for n in ("gate_w", "w1", "w2")]
        l0b = [a[f"L0_attn_b_{n}"] for n in ("Wq", "Wk", "Wv", "Wo", "bo", "gamma", "beta")]
        l1a = [a[f"L1_attn_a_{n}"] for n in ("w_in", "conv_w", "conv_b", "w_xproj", "w_dt", "b_dt", "A_log", "D", "w_out",
                                             "ln_g", "ln_b")]
        l1b = [a[f"L1_attn_b_{n}"] for n in ("Wq", "Wk", "Wv", "Wb", "conv_q", "conv_k", "conv_v", "g", "Wo")]
        l1f = [a[f"L1_ffn_{n}"] for n in ("gate_weight", "gate_bias", "w_gate", "w_up", "w_down", "shared_w_gate", "shared_w_up",
                                          "shared_w_down", "anchor_w_gate", "anchor_w_up", "anchor_w_down")]
        layers = [("la", layer_attention, l0a), ("lb", layer_moe_experts, l0f), ("lc", layer_linear_attention, l0b),
                  ("ld", layer_moe_experts, l0f), ("le", layer_scan, l1a), ("lf", layer_moe_tokens, l1f),
                  ("lg", layer_delta, l1b), ("lh", layer_moe_tokens, l1f)]
        for n in PHASES:
            tag, layer, args = layers[n]
            k.next_layer()
            layer(k, tag, *args)
        k.next_layer()
        stored = k.sem("stored")
        with nc.Block() as block:
            @block.sync
            def _(sp):
                sp.dma_start(out.rearrange("b (j p) d -> p (b j) d", p=P), k.x[:]).then_inc(stored, 16)
                sp.wait_ge(stored, 16)


_INS = ['L0_attn_a_x', 'L0_attn_a_w_qkv', 'L0_attn_a_b_qkv', 'L0_attn_a_w_out', 'L0_attn_a_b_out', 'L0_attn_a_w1_rpe',
        'L0_attn_a_b1_rpe', 'L0_attn_a_w2_rpe', 'L0_attn_a_b2_rpe', 'L0_attn_b_Wq', 'L0_attn_b_Wk', 'L0_attn_b_Wv',
        'L0_attn_b_Wo', 'L0_attn_b_bo', 'L0_attn_b_gamma', 'L0_attn_b_beta', 'L0_ffn_gate_w', 'L0_ffn_w1', 'L0_ffn_w2',
        'L1_attn_a_w_in', 'L1_attn_a_conv_w', 'L1_attn_a_conv_b', 'L1_attn_a_w_xproj', 'L1_attn_a_w_dt', 'L1_attn_a_b_dt',
        'L1_attn_a_A_log', 'L1_attn_a_D', 'L1_attn_a_w_out', 'L1_attn_a_ln_g', 'L1_attn_a_ln_b', 'L1_attn_b_Wq',
        'L1_attn_b_Wk', 'L1_attn_b_Wv', 'L1_attn_b_Wb', 'L1_attn_b_conv_q', 'L1_attn_b_conv_k', 'L1_attn_b_conv_v',
        'L1_attn_b_g', 'L1_attn_b_Wo', 'L1_ffn_gate_weight', 'L1_ffn_gate_bias', 'L1_ffn_w_gate', 'L1_ffn_w_up',
        'L1_ffn_w_down', 'L1_ffn_shared_w_gate', 'L1_ffn_shared_w_up', 'L1_ffn_shared_w_down', 'L1_ffn_anchor_w_gate',
        'L1_ffn_anchor_w_up', 'L1_ffn_anchor_w_down']


def kernel(**inputs):
    import numpy as _np
    import concourse.bacc as _bacc
    from concourse import mybir as _mybir
    from concourse.bass_utils import run_bass_kernel_spmd as _run

    nc = _bacc.Bacc("TRN2", target_bir_lowering=False, num_devices=1)
    arrays, args = {}, {}
    for name in _INS:
        arr = _np.ascontiguousarray(inputs[name])
        arrays[f"in_{name}_dram"] = arr
        args[name] = nc.dram_tensor(f"in_{name}_dram", arr.shape, _mybir.dt.from_np(arr.dtype), kind="ExternalInput").ap()
    out = nc.dram_tensor("out_0_dram", (4, 512, 128), _mybir.dt.float32, kind="ExternalOutput").ap()
    build(nc, args, out)
    r = _run(nc, [arrays], core_ids=[0])
    return r.results[0]["out_0_dram"]
```

```python
from contextlib import ExitStack

import concourse.bass as bass
from concourse import mybir

F32 = mybir.dt.float32
BF16 = mybir.dt.bfloat16
I32 = mybir.dt.int32
ALU = mybir.AluOpType
ACT = mybir.ActivationFunctionType
AX_X = mybir.AxisListType.X

P = 128
B, T, D = 4, 512, 128
NT = B * T // P
TPB = T // P
LN_EPS = 1e-5
PHASES = [0, 1, 2, 3, 4, 5, 6, 7]


class Core:

    def __init__(self, nc, ctx):
        self.nc, self.ctx = nc, ctx
        self.past, self.own = [], []
        self.x = self.sb("x", [P, NT, D])
        self.xn = self.sb("xn", [P, NT, D])
        self.xnT = self.sb("xnT", [D, B * T])
        self.ident = self.sb("ident", [P, P])
        self.ident16 = self.sb("ident16", [P, P], BF16)
        self.eps = self.sb("eps", [P, 1])
        self.bank = [ctx.enter_context(nc.psum_tensor(f"bank{i}", [P, 512], F32)) for i in range(8)]

    def sb(self, name, shape, dt=F32, ctx=None):
        return (ctx or self.ctx).enter_context(self.nc.sbuf_tensor(name, shape, dt))

    def sem(self, name):
        s = self.nc.alloc_semaphore(name=name)
        self.own.append(s)
        return s

    def next_layer(self):
        self.past, self.own = self.own, []

    def clear_past(self):
        self.nc.clear_and_free_semaphores(self.past)


class Link:

    def __init__(self, eng, sem, waited=None):
        self.eng, self.sem, self.n, self.base, self.waited = eng, sem, 0, 0, waited

    def __call__(self, ins):
        ins.then_inc(self.sem, 1)
        self.n += 1
        self.eng.wait_ge(self.sem, self.base + self.n)
        if self.waited is not None:
            self.eng.sem_inc(self.waited, 1)

    def start(self, i, per):
        self.first, self.n, self.base = self.n, 0, self.n + i * per

    def end(self, per, passes):
        assert self.n == per, (self.n, per)
        self.n, self.base = self.first + per * passes, 0


def bcast(ap, *dims):
    return bass.AP(ap.tensor, ap.offset, [ap.ap[0], *dims])



class Norm:
    def __init__(self, k, tag, ctx, scratch=None):
        self.k = k
        self.stats = k.sb(f"{tag}_stats", [P, NT, 6], ctx=ctx)
        self.mv = k.sb(f"{tag}_mv", [P, NT, 2], ctx=ctx)
        self.vare = k.sb(f"{tag}_vare", [P, NT], ctx=ctx)
        self.std = k.sb(f"{tag}_std", [P, NT], ctx=ctx)
        self.rstd = k.sb(f"{tag}_rstd", [P, NT], ctx=ctx)
        self.var_ready = k.sem(f"{tag}_var_ready")
        self.std_ready = k.sem(f"{tag}_std_ready")
        self.xn_ready = k.sem(f"{tag}_xn_ready")
        self.turned = k.sem(f"{tag}_turned")
        self.xnT_ready = k.sem(f"{tag}_xnT_ready")

    def statistics(self, dve, link, src):
        for j in range(NT):
            last = dve.bn_stats(self.stats[:, j, :], src[:, j, :])
        link(last)
        for j in range(NT):
            last = dve.bn_aggr(self.mv[:, j, :], self.stats[:, j, :])
        link(last)
        dve.tensor_scalar(self.vare[:], self.mv[:, :, 1], LN_EPS, None, ALU.add).then_inc(self.var_ready, 1)

    def scalar_sqrt(self, act, n=1):
        act.wait_ge(self.var_ready, n)
        act.activation(self.std[:], self.vare[:], ACT.Sqrt).then_inc(self.std_ready, 1)

    def vector(self, dve, link):
        k = self.k
        self.statistics(dve, link, k.x)
        self.normalise(dve, link)

    def normalise(self, dve, link):
        k = self.k
        dve.wait_ge(self.std_ready, 1)
        link(dve.reciprocal(self.rstd[:], self.std[:]))
        for j in range(NT):
            dve.tensor_scalar(k.xn[:, j, :], k.x[:, j, :], self.mv[:, j, 0:1], self.rstd[:, j:j + 1],
                              ALU.subtract, ALU.mult).then_inc(self.xn_ready, 1)

    def tensor(self, pe, src=None, ready=None):
        k = self.k
        src = k.xn if src is None else src
        ready = self.xn_ready if ready is None else ready
        for g in range(B):
            pe.wait_ge(ready, 4 * (g + 1))
            for j in range(4):
                last = pe.transpose(k.bank[g][:, j * P:(j + 1) * P], src[:, 4 * g + j, :], k.ident[:])
            last.then_inc(self.turned, 1)

    def scalar_copy(self, act):
        k = self.k
        for g in range(B):
            act.wait_ge(self.turned, g + 1)
            act.activation(k.xnT[:, g * T:(g + 1) * T], k.bank[g][:], ACT.Copy).then_inc(self.xnT_ready, 1)



def layer_attention(k, tag, w_qkv, b_qkv, w_out, b_out, w1_rpe, b1_rpe, w2_rpe, b2_rpe):
    nc = k.nc
    HID, H = w2_rpe.shape
    HD = D // H
    HP = H // 2
    PARTS = 8
    SCALE = float(HD) ** -0.5
    SPAN = 2 * T
    WIDE = 2 * T - P
    U = H * TPB
    GH = 4
    NG = H // GH
    VW = 32
    NN, NR, NV = 4, 4, 12
    TURN, COPY = 2, 3
    MIX = COPY + TPB
    GROUP = GH * TPB
    LEAVE, BACK, SCALE_O = MIX + GROUP, MIX + GROUP + 1, MIX + GROUP + 3
    PRODUCTS = [(0, 0), (0, 1), (1, 0), (1, 1), (0, 2), (2, 0)]
    with ExitStack() as ctx:
        def sb(name, shape, dt=F32):
            return k.sb(f"{tag}_{name}", shape, dt, ctx)

        def sem(name):
            return k.sem(f"{tag}_{name}")

        norm = Norm(k, tag, ctx)
        wqkv = sb("wqkv", [D, 3 * D])
        wout = sb("wout", [D, D])
        bqkv = sb("bqkv", [P, 3 * D])
        bout = sb("bout", [P, D])
        w1c = sb("w1c", [HID, 1])
        b1c = sb("b1c", [HID, 1])
        w2 = sb("w2", [HID, H])
        b2c = sb("b2c", [H, 1])
        rel = sb("rel", [HID, SPAN])
        mag = sb("mag", [HID, SPAN])
        curve = rel[0:H]
        bias = sb("bias", [P, H, WIDE])
        scratch = nc.dram_tensor(f"{tag}_scratch", [H, SPAN], F32)
        qk = sb("qk", [P, NT, 2, D])
        v = k.xn
        v1 = sb("v1", [P, TPB, H, VW])
        rest = sb("rest", [P, 2, TPB, D])
        part = sb("part", [P, 2, 3, TPB, D], BF16)
        stack = sb("stack", [P, 2, TPB, H, PARTS, HD], BF16)
        qkT = sb("qkT", [P, HP, 2, T], BF16)
        neg = sb("neg", [P, NN, T])
        nmax = sb("nmax", [P, NN, 1])
        prob = sb("prob", [P, NR, T])
        side = prob[0:HID, 0:2, :].rearrange("p a t -> p (a t)")
        probT = sb("probT", [P, NV, T])
        mixT = sb("mixT", [P, 2, GH, P])
        rsum = sb("rsum", [P, GH, TPB])
        o, oT = k.xn, k.xnT

        loaded_w, loaded_r, loaded_bias = sem("loaded_w"), sem("loaded_r"), sem("loaded_bias")
        waited, order, pool_order, act_order = sem("waited"), sem("order"), sem("pool_order"), sem("act_order")
        rel_ready, curve_turned, curve_ready, curve_stored = sem("rel_ready"), sem("curve_turned"), sem("curve_ready"), sem("curve_stored")
        side_ready, logd = sem("side_ready"), sem("logd")
        qkv_done, qkv_ready = sem("qkv_done"), sem("qkv_ready")
        stacked, parts_turned, parts_ready = sem("stacked"), sem("parts_turned"), sem("parts_ready")
        scored, biased, exped, prob_turned = sem("scored"), sem("biased"), sem("exped"), sem("prob_turned")
        probT_ready = [sem("probT_by_act"), sem("probT_by_dve")]
        mixed, mixT_ready, mix_back, o_ready, v1_ready = sem("mixed"), sem("mixT_ready"), sem("mix_back"), sem("o_ready"), sem("v1_ready")
        o_turned, oT_ready, projected, added, x_ready = sem("o_turned"), sem("oT_ready"), sem("projected"), sem("added"), sem("x_ready")

        block = ctx.enter_context(nc.Block())

        @block.sync
        def _(sp):
            sp.dma_start(w1c[:], w1_rpe.rearrange("a h -> h a"), allow_slow_non_contiguous=True).then_inc(loaded_r, 16)
            sp.dma_start(b1c[:], b1_rpe.rearrange("(h a) -> h a", a=1)).then_inc(loaded_r, 16)
            sp.dma_start(w2[:], w2_rpe).then_inc(loaded_r, 16)
            sp.dma_start(b2c[:], b2_rpe.rearrange("(h a) -> h a", a=1)).then_inc(loaded_r, 16)
            sp.dma_start(wqkv[:], w_qkv).then_inc(loaded_w, 16)
            sp.dma_start(bqkv[:], b_qkv.partition_broadcast(P)).then_inc(loaded_w, 16)
            sp.dma_start(wout[:], w_out).then_inc(loaded_w, 16)
            sp.dma_start(bout[:], b_out.partition_broadcast(P)).then_inc(loaded_w, 16)
            sp.wait_ge(curve_ready, 2)
            sp.dma_start(scratch[:, :], curve).then_inc(curve_stored, 16)
            sp.wait_ge(curve_stored, 16)
            for h in range(0, H, 4):
                src = bass.AP(scratch, h * SPAN, [[1, P], [SPAN, 4], [1, WIDE]])
                sp.dma_start(bias[:, h:h + 4, :], src).then_inc(loaded_bias, 16)
                sp.wait_ge(loaded_bias, 4 * h + 16)

        @block.gpsimd
        def _(pool):
            k.clear_past()
            link = Link(pool, pool_order, waited)
            pool.iota(rel[:], [[1, SPAN]], base=1 - T, channel_multiplier=0, allow_small_or_imprecise_dtypes=True).then_inc(rel_ready, 1)
            link(pool.memset(stack[:], 0.0))
            link(pool.memset(v1[:], 0.0))
            link(pool.memset(v1[:, :, :, HD:HD + 1], 1.0))
            pool.wait_ge(loaded_w, 64)
            pool.wait_ge(norm.xn_ready, NT)
            pool.tensor_tensor(k.x[:], k.x[:], bcast(bout[:, 0:1], (0, NT), (1, D)), ALU.add).then_inc(x_ready, 1)
            pool.wait_ge(qkv_ready, NT)
            pool.tensor_copy(v1[:, :, :, 0:HD], v[:, 0:TPB, :].rearrange("p j (h d) -> p j h d", d=HD)).then_inc(v1_ready, 1)
            pool.wait_ge(stacked, 2)
            with pool.Fori(0, B - 1) as b:
                link.start(b, 2 * (2 * 3) + 1)
                for s in range(2):
                    whole, left = rest[:, 0, :, :], rest[:, 1, :, :]
                    link(pool.tensor_copy(whole, qk[:, bass.ds(b * TPB + TPB, TPB), s, :]))
                    for i in range(3):
                        link(pool.tensor_copy(part[:, s, i, :, :], whole if i == 0 else left))
                        if i < 2:
                            link(pool.tensor_tensor(left, whole if i == 0 else left, part[:, s, i, :, :], ALU.subtract))
                pool.wait_ge(parts_turned, b * HP + HP)
                pool.sem_inc(waited, 1)
                for s in range(2):
                    for r, pair in enumerate(PRODUCTS):
                        last = pool.tensor_copy(stack[:, s, :, :, r, :], part[:, s, pair[s], :, :].rearrange("p j (h d) -> p j h d", d=HD))
                    last.then_inc(stacked, 1)
                pool.wait_ge(mixed, b * H + H + NV // TPB)
                pool.sem_inc(waited, 1)
                link(pool.tensor_copy(v1[:, :, :, 0:HD], v[:, bass.ds(b * TPB + TPB, TPB), :].rearrange("p j (h d) -> p j h d", d=HD)))
                pool.sem_inc(v1_ready, 1)
                link.end(2 * (2 * 3) + 1, B - 1)

        @block.scalar
        def _(act):
            link = Link(act, act_order)
            norm.scalar_sqrt(act)
            act.wait_ge(side_ready, 1)
            act.activation(mag[:], mag[:], ACT.Ln, bias=1.0).then_inc(logd, 1)
            act.wait_ge(side_ready, 2)
            act.wait_ge(loaded_r, 64)
            link(act.activation(mag[:], mag[:], ACT.Relu, bias=b1c[:, 0:1], scale=w1c[:, 0:1]))
            norm.scalar_copy(act)
            for i in range(2):
                act.wait_ge(curve_turned, i + 1)
                act.activation(curve[:, i * T:(i + 1) * T], k.bank[4 + i][0:H, :], ACT.Identity, bias=b2c[:, 0:1]).then_inc(curve_ready, 1)
            with act.Fori(0, B) as b:
                def copy_parts(hp):
                    act.wait_ge(parts_turned, b * HP + hp + 1)
                    if hp == 0:
                        act.wait_ge(scored, b * U + 1)
                    act.activation(qkT[:, hp, :, :].rearrange("p s t -> p (s t)"), k.bank[6][:].bitcast(BF16), ACT.Copy).then_inc(parts_ready, 1)

                copy_parts(0)
                copy_parts(1)
                for step in range(U - GROUP + LEAVE + 1):
                    if step % TPB == 2 and step // TPB + 2 < HP:
                        copy_parts(step // TPB + 2)
                    u = step - COPY
                    if 0 <= u < U and u % 2 == 0:
                        act.wait_ge(prob_turned, b * U + u + 1 + NR)
                        act.wait_ge(mixed, b * H + u // TPB + 1)
                        act.activation(probT[:, u % NV, :], k.bank[2 + u % 2][:], ACT.Copy).then_inc(probT_ready[0], 1)
                    if step < U:
                        u = step
                        act.wait_ge(biased, b * U + u + 3)
                        act.wait_ge(prob_turned, b * U + u + 1)
                        act.activation(prob[:, u % NR, :], neg[:, u % NN, :], ACT.Exp, bias=nmax[:, u % NN, :], scale=-1.0).then_inc(exped, 1)
                    g = (step - LEAVE) // GROUP
                    if step >= LEAVE and (step - LEAVE) % GROUP == 0:
                        act.wait_ge(mixed, b * H + (g + 1) * GH + NV // TPB)
                        act.wait_ge(mix_back, b * NG + g + 1)
                        act.activation(mixT[:, g % 2, :, :].rearrange("p h t -> p (h t)"), k.bank[4 + g % 2][:], ACT.Copy).then_inc(mixT_ready, 1)
            for g in range(B):
                act.wait_ge(o_turned, g + 1)
                act.activation(oT[:, g * T:(g + 1) * T], k.bank[g][:], ACT.Copy).then_inc(oT_ready, 1)

        @block.vector
        def _(dve):
            link = Link(dve, order)
            for s, n in ((biased, 2), (exped, NN), (prob_turned, NR), (mixed, NV // TPB), (probT_ready[0], 1), (probT_ready[1], 1),
                         (mixT_ready, 2), (mix_back, 2), (o_ready, 1), (parts_ready, 1), (scored, 1)):
                dve.sem_inc(s, n)
            norm.statistics(dve, link, k.x)
            dve.wait_ge(rel_ready, 1)
            dve.scalar_tensor_tensor(mag[:], rel[:], -1.0, rel[:], ALU.mult, ALU.max).then_inc(side_ready, 1)
            link(dve.tensor_scalar(side, rel[:], 0.0, 2.0, ALU.is_ge, ALU.mult))
            link(dve.tensor_scalar(side, side, -1.0, None, ALU.add))
            dve.wait_ge(logd, 1)
            dve.tensor_tensor(mag[:], mag[:], side, ALU.mult).then_inc(side_ready, 1)
            norm.normalise(dve, link)
            dve.wait_ge(pool_order, 1)
            dve.wait_ge(loaded_w, 64)
            dve.wait_ge(norm.turned, B)
            for t in range(NT):
                dve.wait_ge(qkv_done, t + 1)
                ps = k.bank[4 + t % 4]
                dve.tensor_tensor(v[:, t, :], ps[:, 2 * D:3 * D], bqkv[:, 2 * D:3 * D], ALU.add)
                if t == 0:
                    link(dve.tensor_scalar(bqkv[:, 0:D], bqkv[:, 0:D], SCALE, None, ALU.mult))
                dve.scalar_tensor_tensor(qk[:, t, 0, :], ps[:, 0:D], SCALE, bqkv[:, 0:D], ALU.mult, ALU.add)
                dve.tensor_tensor(qk[:, t, 1, :], ps[:, D:2 * D], bqkv[:, D:2 * D], ALU.add).then_inc(qkv_ready, 1)
            dve.wait_ge(qkv_ready, NT)
            for s in range(2):
                left = rest[:, s, :, :]
                for i in range(3):
                    src = qk[:, 0:TPB, s, :] if i == 0 else left
                    link(dve.tensor_copy(part[:, s, i, :, :], src))
                    if i < 2:
                        link(dve.tensor_tensor(left, src, part[:, s, i, :, :], ALU.subtract))
                for r, pair in enumerate(PRODUCTS):
                    last = dve.tensor_copy(stack[:, s, :, :, r, :], part[:, s, pair[s], :, :].rearrange("p j (h d) -> p j h d", d=HD))
                last.then_inc(stacked, 1)
            with dve.Fori(0, B) as b:
                link.start(b, NG)
                for step in range(U - GROUP + SCALE_O + 1):
                    u = step - COPY
                    if 0 <= u < U and u % 2 == 1:
                        dve.wait_ge(prob_turned, b * U + u + 1 + NR)
                        dve.wait_ge(mixed, b * H + u // TPB + 1)
                        dve.tensor_copy(probT[:, u % NV, :], k.bank[2 + u % 2][:]).then_inc(probT_ready[1], 1)
                    if step < U:
                        u = step
                        h, j = u // TPB, u % TPB
                        if j == 0 and h % 4 == 0:
                            dve.wait_ge(loaded_bias, 4 * h + 16)
                        dve.wait_ge(scored, b * U + u + 2)
                        dve.wait_ge(exped, b * U + u + 1)
                        dve.sem_inc(waited, 1)
                        key0 = bias[:, h, T - 1 + j * P:T + j * P]
                        keys_back = bcast(key0, (-1, T))
                        dve.tensor_tensor_reduce(out=neg[:, u % NN, :], in0=k.bank[u % 2][:], in1=keys_back,
                                                 scale=-1.0, scalar=3e38, op0=ALU.add, op1=ALU.min, accum_out=nmax[:, u % NN, :]).then_inc(biased, 1)
                    if step >= SCALE_O and (step - SCALE_O) % GROUP == 0:
                        g = (step - SCALE_O) // GROUP
                        dve.wait_ge(mix_back, b * NG + g + 3)
                        dve.sem_inc(waited, 1)
                        ov = k.bank[7][:].rearrange("p (h j d) -> p h j d", j=TPB, d=VW)
                        link(dve.reciprocal(rsum[:], ov[:, :, :, HD]))
                        dst = o[:, bass.ds(b * TPB, TPB), g * GH * HD:(g + 1) * GH * HD].rearrange("p j (h d) -> p h j d", d=HD)
                        dve.tensor_tensor(dst, ov[:, :, :, 0:HD], rsum[:].unsqueeze(3).to_broadcast([P, GH, TPB, HD]), ALU.mult).then_inc(o_ready, 1)
                link.end(NG, B)
            dve.wait_ge(x_ready, 1)
            for g in range(B):
                dve.wait_ge(projected, g + 1)
                xb = k.x[:, g * TPB:(g + 1) * TPB, :].rearrange("p j d -> p (j d)")
                dve.tensor_tensor(xb, xb, k.bank[4 + g][:], ALU.add).then_inc(added, 1)

        @block.tensor
        def _(pe):
            pe.wait_ge(act_order, 1)
            for i in range(2):
                pe.matmul(k.bank[4 + i][0:H, :], w2[:], mag[:, i * T:(i + 1) * T], start=True, stop=True).then_inc(curve_turned, 1)
            norm.tensor(pe)
            pe.wait_ge(loaded_w, 64)
            pe.wait_ge(curve_ready, 2)
            for t in range(NT):
                pe.wait_ge(norm.xnT_ready, t // TPB + 1)
                if t >= 4:
                    pe.wait_ge(qkv_ready, t - 3)
                pe.matmul(k.bank[4 + t % 4][:, 0:3 * D], k.xnT[:, t * P:(t + 1) * P], wqkv[:], start=True, stop=True).then_inc(qkv_done, 1)
            pe.wait_ge(qkv_ready, NT)
            with pe.Fori(0, B) as b:
                def turn_parts(hp):
                    pe.wait_ge(parts_ready, b * HP + hp + 1)
                    bank = k.bank[6][:].bitcast(BF16)
                    for s in range(2):
                        for j in range(TPB):
                            last = pe.transpose(bank[:, s * T + j * P:s * T + (j + 1) * P],
                                                stack[:, s, j, 2 * hp:2 * hp + 2, :, :].rearrange("p h r d -> p (h r d)"), k.ident16[:])
                    last.then_inc(parts_turned, 1)

                pe.wait_ge(stacked, b * 2 + 2)
                turn_parts(0)
                turn_parts(1)
                for step in range(U - GROUP + BACK + 1):
                    if step % TPB == 1 and step // TPB + 2 < HP:
                        turn_parts(step // TPB + 2)
                    if step < U:
                        u = step
                        h, j = u // TPB, u % TPB
                        if j == 0:
                            pe.wait_ge(parts_ready, b * HP + h // 2 + 2)
                        pe.wait_ge(biased, b * U + u + 1)
                        r = slice(64 * (h % 2), 64 * (h % 2) + 64)
                        pe.matmul(k.bank[u % 2][:], qkT[r, h // 2, 0, j * P:(j + 1) * P], qkT[r, h // 2, 1, :], start=True, stop=True).then_inc(scored, 1)
                    u = step - MIX
                    if 0 <= u < U:
                        h, c = u // TPB, u % TPB
                        g = h // GH
                        if c == 0:
                            if h == 0:
                                pe.wait_ge(v1_ready, b + 1)
                            if h % GH == 0:
                                pe.wait_ge(mixT_ready, b * NG + g + 1)
                            for side_ready_ in probT_ready:
                                pe.wait_ge(side_ready_, b * (U // 2) + 2 * h + 3)
                        for j in range(TPB):
                            last = pe.matmul(k.bank[4 + g % 2][VW * j:VW * (j + 1), (h % GH) * P:(h % GH + 1) * P], v1[:, c, h, :],
                                             probT[:, (h * TPB + j) % NV, c * P:(c + 1) * P], start=(c == 0), stop=(c == TPB - 1),
                                             tile_position=(0, VW * j))
                        if c == TPB - 1:
                            last.then_inc(mixed, 1)
                    u = step - TURN
                    if 0 <= u < U:
                        pe.wait_ge(exped, b * U + u + 1 + NN)
                        pe.wait_ge(probT_ready[u % 2], b * (U // 2) + u // 2 + 1)
                        for c in range(TPB):
                            last = pe.transpose(k.bank[2 + u % 2][:, c * P:(c + 1) * P], prob[:, u % NR, c * P:(c + 1) * P], k.ident[:])
                        last.then_inc(prob_turned, 1)
                    if step >= BACK and (step - BACK) % GROUP == 0:
                        g = (step - BACK) // GROUP
                        pe.wait_ge(mixT_ready, b * NG + g + 3)
                        pe.wait_ge(o_ready, b * NG + g + 1)
                        for i in range(GH):
                            last = pe.transpose(k.bank[7][:, i * P:(i + 1) * P], mixT[:, g % 2, i, :], k.ident[:])
                        last.then_inc(mix_back, 1)
            norm_order = NG * B + 1
            pe.wait_ge(o_ready, norm_order)
            for g in range(B):
                for j in range(TPB):
                    last = pe.transpose(k.bank[g][:, j * P:(j + 1) * P], o[:, g * TPB + j, :], k.ident[:])
                last.then_inc(o_turned, 1)
            for g in range(B):
                pe.wait_ge(oT_ready, g + 1)
                for j in range(TPB):
                    last = pe.matmul(k.bank[4 + g][:, j * D:(j + 1) * D], oT[:, (g * TPB + j) * P:(g * TPB + j + 1) * P], wout[:], start=True, stop=True)
                last.then_inc(projected, 1)



def layer_moe_experts(k, tag, gate_w, w1, w2):
    nc = k.nc
    E, F = w1.shape[0], w1.shape[2]
    CAP = int(2.0 * T / E)
    FT = F // P
    R = B * E
    assert CAP == P and CAP % 8 == 0 and E % 2 == 0
    with ExitStack() as ctx:
        def sb(name, shape, dt=F32):
            return k.sb(f"{tag}_{name}", shape, dt, ctx)

        def sem(name):
            return k.sem(f"{tag}_{name}")

        norm = Norm(k, tag, ctx)
        gw = sb("gw", [E, D])
        gwT = sb("gwT", [D, E])
        w1s = sb("w1s", [D, 2, F])
        w2s = sb("w2s", [P, 2, FT, D])
        lmax = sb("lmax", [P, NT])
        probs = sb("probs", [P, NT, E])
        psum_e = sb("psum_e", [P, NT])
        prec = sb("prec", [P, NT])
        rows = sb("rows", [R, 2, T])
        best = sb("best", [R, 8])
        ones = sb("ones", [R, T])
        chosen = sb("chosen", [R, T])
        count = sb("count", [R, T])
        slot = sb("slot", [R, T])
        slots = sb("slots", [P, E, NT])
        gates = sb("gates", [P, E, NT])
        number = sb("number", [P, P])
        pick = sb("pick", [P, 2, NT, P])
        own = sb("own", [P, 2, NT])
        place = sb("place", [P, B, T])
        xin = sb("xin", [D, T])
        hid = sb("hid", [P, FT, T])
        gate = sb("gate", [P, B])
        y = sb("y", [P, B, D])

        loaded_gw = sem("loaded_gw")
        loaded_w = [sem("loaded_w0"), sem("loaded_w1")]
        order, pool_order, number_made = sem("order"), sem("pool_order"), sem("number_made")
        gwT_turned, gwT_ready, logits_ready = sem("gwT_turned"), sem("gwT_ready"), sem("logits_ready")
        shifted, exped, probs_ready = sem("shifted"), sem("exped"), sem("probs_ready")
        rows_turned, slot_ready, slot_turned, slots_ready = sem("rows_turned"), sem("slot_ready"), sem("slot_turned"), sem("slots_ready")
        own_ready, own_seen, pick_ready, pick_used = sem("own_ready"), sem("own_seen"), sem("pick_ready"), sem("pick_used")
        xin_ready, xin_copied, h_ready, gelu_done = sem("xin_ready"), sem("xin_copied"), sem("h_ready"), sem("gelu_done")
        turned, place_ready, gate_ready, gate_copied = sem("pturned"), sem("place_ready"), sem("gate_ready"), sem("gate_copied")
        y_done, y_ready, out_ready, out_added, w_used = sem("y_done"), sem("y_ready"), sem("out_ready"), sem("out_added"), sem("w_used")

        block = ctx.enter_context(nc.Block())

        @block.sync
        def _(sp):
            sp.dma_start(gw[:], gate_w).then_inc(loaded_gw, 16)
            sp.sem_inc(w_used, 2)
            with sp.Fori(0, E // 2) as i:
                for s in range(2):
                    sp.wait_ge(w_used, i * 2 + s + 1)
                    sp.dma_start(w1s[:, s, :], w1[bass.ds(i * 2 + s, 1), :, :].rearrange("e d f -> d (e f)")).then_inc(loaded_w[s], 16)
                    sp.dma_start(w2s[:, s, :, :], w2[bass.ds(i * 2 + s, 1), :, :].rearrange("e (t p) d -> p (e t) d", p=P))\
                        .then_inc(loaded_w[s], 16)

        @block.gpsimd
        def _(pool):
            k.clear_past()
            pool.iota(number[:], [[1, P]], base=0, channel_multiplier=0, allow_small_or_imprecise_dtypes=True).then_inc(number_made, 1)
            pool.memset(ones[:], 1.0).then_inc(number_made, 1)
            pool.wait_ge(number_made, 2)
            pool.sem_inc(pick_used, 2)
            pool.wait_ge(slots_ready, 1)
            with pool.Fori(0, E // 2) as i:
                for s in range(2):
                    pool.wait_ge(pick_used, i * 2 + s + 1)
                    pool.tensor_copy(own[:, s, :], slots[:, bass.ds(i * 2 + s, 1), :].rearrange("p e j -> p (e j)")).then_inc(own_ready, 1)
                    pool.wait_ge(own_ready, i * 2 + s + 1)
                    pool.sem_inc(own_seen, 1)
                    for j in range(NT):
                        last = pool.tensor_scalar(pick[:, s, j, :], number[:], own[:, s, j:j + 1], None, ALU.is_equal)
                    last.then_inc(pick_ready, 1)

        @block.scalar
        def _(act):
            norm.scalar_sqrt(act)
            norm.scalar_copy(act)
            act.wait_ge(shifted, 1)
            act.activation(probs[:], probs[:], ACT.Exp).then_inc(exped, 1)
            with act.Fori(0, E // 2) as i:
                for s in range(2):
                    e = i * 2 + s
                    act.wait_ge(xin_ready, e + 1)
                    act.activation(xin[:], k.bank[0][:], ACT.Copy).then_inc(xin_copied, 1)
                    for f in range(FT):
                        act.wait_ge(h_ready, e * FT + f + 1)
                        act.activation(hid[:, f, :], k.bank[1 + f % 2][:], ACT.Gelu).then_inc(gelu_done, 1)
                    act.wait_ge(y_done, e + 1)

        @block.vector
        def _(dve):
            link = Link(dve, order)
            dve.sem_inc(gelu_done, 2)
            dve.sem_inc(out_added, 2)
            norm.vector(dve, link)
            dve.wait_ge(gwT_turned, 1)
            dve.tensor_copy(gwT[:], k.bank[4][:, 0:E]).then_inc(gwT_ready, 1)
            dve.wait_ge(logits_ready, 1)
            logits = k.bank[5][:, 0:NT * E].rearrange("p (j e) -> p j e", e=E)
            link(dve.tensor_reduce(lmax[:], logits, AX_X, ALU.max))
            dve.tensor_tensor(probs[:], logits, bcast(lmax[:, 0:1], (1, NT), (0, E)), ALU.subtract).then_inc(shifted, 1)
            dve.wait_ge(exped, 1)
            link(dve.tensor_reduce(psum_e[:], probs[:], AX_X, ALU.add))
            link(dve.reciprocal(prec[:], psum_e[:]))
            link(dve.tensor_tensor(probs[:], probs[:], bcast(prec[:, 0:1], (1, NT), (0, E)), ALU.mult))
            dve.tensor_copy(gates[:].rearrange("p e (n j) -> p j n e", j=TPB), probs[:].rearrange("p (j n) e -> p j n e", j=TPB))\
                .then_inc(probs_ready, 1)
            dve.wait_ge(rows_turned, 1)
            link(dve.tensor_copy(rows[:, 0, :], k.bank[6][0:R, :]))
            for r in range(CAP // 8):
                link(dve.max(best[:], rows[:, r % 2, :]))
                link(dve.match_replace(rows[:, 1 - r % 2, :], best[:], rows[:, r % 2, :], -1.0))
            link(dve.tensor_scalar(chosen[:], rows[:, (CAP // 8) % 2, :], 0.0, None, ALU.is_lt))
            dve.wait_ge(number_made, 2)
            link(dve.tensor_tensor_scan(count[:], ones[:], chosen[:], 0.0, ALU.mult, ALU.add))
            link(dve.tensor_tensor(slot[:], count[:], chosen[:], ALU.mult))
            dve.tensor_scalar(slot[:], slot[:], -1.0, None, ALU.add).then_inc(slot_ready, 1)
            dve.wait_ge(slot_turned, 1)
            dve.tensor_copy(slots[:].rearrange("p e (n j) -> p j n e", j=TPB),
                            k.bank[7][:, 0:TPB * R].rearrange("p (j n e) -> p j n e", j=TPB, n=B)).then_inc(slots_ready, 1)
            with dve.Fori(0, E // 2) as i:
                for s in range(2):
                    e = i * 2 + s
                    for n in range(B):
                        dve.wait_ge(turned, e * B + n + 1)
                        dve.tensor_copy(place[:, n, :], k.bank[3][:]).then_inc(place_ready, 1)
                    dve.wait_ge(gate_ready, e + 1)
                    dve.tensor_copy(gate[:], k.bank[4][:, 0:B]).then_inc(gate_copied, 1)
                    dve.wait_ge(gate_copied, e + 1)
                    dve.wait_ge(y_done, e + 1)
                    dve.tensor_tensor(y[:], k.bank[5][:].rearrange("p (n d) -> p n d", d=D), bcast(gate[:, 0:1], (1, B), (0, D)), ALU.mult)\
                        .then_inc(y_ready, 1)
                    for n in range(B):
                        dve.wait_ge(out_ready, e * B + n + 1)
                        xb = k.x[:, n * TPB:(n + 1) * TPB, :].rearrange("p j d -> p (j d)")
                        dve.tensor_tensor(xb, xb, k.bank[6 + n % 2][:], ALU.add).then_inc(out_added, 1)
                    dve.wait_ge(out_added, e * B + B + 2)

        @block.tensor
        def _(pe):
            norm.tensor(pe)
            pe.wait_ge(loaded_gw, 16)
            pe.transpose(k.bank[4][:, 0:E], gw[:], k.ident[0:E, 0:E]).then_inc(gwT_turned, 1)
            pe.wait_ge(gwT_ready, 1)
            pe.wait_ge(norm.xnT_ready, B)
            for j in range(TPB):
                for n in range(B):
                    o = (j * B + n) * E
                    t = n * TPB + j
                    last = pe.matmul(k.bank[5][:, o:o + E], k.xnT[:, t * P:(t + 1) * P], gwT[:], start=True, stop=True)
            last.then_inc(logits_ready, 1)
            pe.wait_ge(probs_ready, 1)
            for j in range(TPB):
                last = pe.transpose(k.bank[6][0:R, j * P:(j + 1) * P], probs[:, j * B:(j + 1) * B, :].rearrange("p n e -> p (n e)"), k.ident[:])
            last.then_inc(rows_turned, 1)
            pe.wait_ge(slot_ready, 1)
            for j in range(TPB):
                last = pe.transpose(k.bank[7][:, j * R:(j + 1) * R], slot[:, j * P:(j + 1) * P], k.ident[0:R, 0:R])
            last.then_inc(slot_turned, 1)
            pe.wait_ge(slots_ready, 1)
            with pe.Fori(0, E // 2) as i:
                for s in range(2):
                    e = i * 2 + s

                    def turn(n):
                        if n:
                            pe.wait_ge(place_ready, e * B + n)
                        for j in range(TPB):
                            last = pe.transpose(k.bank[3][:, j * P:(j + 1) * P], pick[:, s, n * TPB + j, :], k.ident[:])
                        last.then_inc(turned, 1)

                    pe.wait_ge(pick_ready, e + 1)
                    for n in range(B):
                        for j in range(TPB):
                            t = n * TPB + j
                            last = pe.matmul(k.bank[0][:, n * CAP:(n + 1) * CAP], k.xn[:, t, :], pick[:, s, t, :],
                                             start=(j == 0), stop=(j == TPB - 1))
                    last.then_inc(xin_ready, 1)
                    turn(0)
                    for n in range(B):
                        for j in range(TPB):
                            t = n * TPB + j
                            g = gates[:, bass.ds(e, 1), t:t + 1].rearrange("p e j -> p (e j)")
                            last = pe.matmul(k.bank[4][:, n:n + 1], pick[:, s, t, :], g, start=(j == 0), stop=(j == TPB - 1))
                    last.then_inc(gate_ready, 1)
                    pe.wait_ge(xin_copied, e + 1)
                    pe.wait_ge(loaded_w[s], i * 32 + 32)
                    for f in range(FT):
                        pe.wait_ge(gelu_done, e * FT + f + 1)
                        pe.matmul(k.bank[1 + f % 2][:], w1s[:, s, f * P:(f + 1) * P], xin[:], start=True, stop=True).then_inc(h_ready, 1)
                        if f < B - 1:
                            turn(f + 1)
                    pe.wait_ge(gelu_done, e * FT + FT + 2)
                    for n in range(B):
                        for f in range(FT):
                            last = pe.matmul(k.bank[5][:, n * D:(n + 1) * D], hid[:, f, n * CAP:(n + 1) * CAP], w2s[:, s, f, :],
                                             start=(f == 0), stop=(f == FT - 1))
                    last.then_inc(y_done, 1)
                    pe.wait_ge(turned, e * B + B)
                    pe.sem_inc(pick_used, 1)
                    pe.wait_ge(y_done, e + 1)
                    pe.sem_inc(w_used, 1)
                    pe.wait_ge(y_ready, e + 1)
                    pe.wait_ge(place_ready, e * B + B)
                    for n in range(B):
                        pe.wait_ge(out_added, e * B + n + 1)
                        for j in range(TPB):
                            last = pe.matmul(k.bank[6 + n % 2][:, j * D:(j + 1) * D], place[:, n, j * P:(j + 1) * P], y[:, n, :],
                                             start=True, stop=True)
                        last.then_inc(out_ready, 1)



def layer_linear_attention(k, tag, Wq, Wk, Wv, Wo, bo, gamma, beta):
    nc = k.nc
    with ExitStack() as ctx:
        def sb(name, shape, dt=F32):
            return k.sb(f"{tag}_{name}", shape, dt, ctx)

        def sem(name):
            return k.sem(f"{tag}_{name}")

        norm = Norm(k, tag, ctx)
        norm2 = Norm(k, f"{tag}2", ctx)
        wqv = sb("wqv", [D, 2 * D])
        wk = sb("wk", [D, D])
        wo = sb("wo", [D, D])
        bov = sb("bov", [P, D])
        gam = sb("gam", [P, D])
        bet = sb("bet", [P, D])
        nqmax = sb("nqmax", [P, NT])
        qsum = sb("qsum", [P, NT])
        rq = sb("rq", [P, NT])
        qe = sb("qe", [P, NT, D])
        v = sb("v", [P, NT, D])
        nkmax = sb("nkmax", [D, B])
        ksum = sb("ksum", [D, B])
        rk = sb("rk", [D, B])
        keT = sb("keT", [D, B, T])
        ke = sb("ke", [P, NT, D])
        qeT = sb("qeT", [D, B, T])
        ctxT = sb("ctxT", [D, B, D])
        cw = sb("cw", [D, B, D])
        xb = sb("xb", [P, NT, D])
        r = sb("r", [P, NT, D])

        loaded_w = sem("loaded_w")
        order, pool_order = sem("order"), sem("pool_order")
        qv_done, qmax_ready, v_ready, qe_ready = sem("qv_done"), sem("qmax_ready"), sem("v_ready"), sem("qe_ready")
        k_done, kmax_ready, ke_ready, ke_turned, ke_copied = sem("k_done"), sem("kmax_ready"), sem("ke_ready"), sem("ke_turned"), sem("ke_copied")
        q_turned, qT_copied = sem("q_turned"), sem("qT_copied")
        ctx_done, ctx_copied, cw_done, cw_ready, out_done, out_added = (
            sem("ctx_done"), sem("ctx_copied"), sem("cw_done"), sem("cw_ready"), sem("out_done"), sem("out_added"))

        block = ctx.enter_context(nc.Block())

        @block.sync
        def _(sp):
            for dst, src in ((wqv[:, 0:D], Wq), (wqv[:, D:2 * D], Wv), (wk[:], Wk), (wo[:], Wo)):
                sp.dma_start(dst, src).then_inc(loaded_w, 16)
            for dst, src in ((bov, bo), (gam, gamma), (bet, beta)):
                sp.dma_start(dst[:], src.partition_broadcast(P)).then_inc(loaded_w, 16)

        @block.gpsimd
        def _(pool):
            k.clear_past()
            pool.wait_ge(loaded_w, 112)
            pool.wait_ge(norm.xn_ready, NT)
            pool.tensor_tensor(xb[:], k.xn[:], bcast(bov[:, 0:1], (0, NT), (1, D)), ALU.add).then_inc(pool_order, 1)
            pool.tensor_tensor(k.x[:], k.x[:], bcast(bet[:, 0:1], (0, NT), (1, D)), ALU.add).then_inc(pool_order, 1)

        @block.scalar
        def _(act):
            norm.scalar_sqrt(act)
            norm.scalar_copy(act)
            for t in range(NT):
                act.wait_ge(qmax_ready, t + 1)
                act.wait_ge(v_ready, t + 1)
                act.activation(qe[:, t, :], k.bank[4 + t % 2][:, 0:D], ACT.Exp, bias=nqmax[:, t:t + 1], accum_out=qsum[:, t:t + 1]).then_inc(qe_ready, 1)
            for b in range(B):
                act.wait_ge(kmax_ready, b + 1)
                act.activation(keT[:, b, :], k.bank[6 + b % 2][:], ACT.Exp, bias=nkmax[:, b:b + 1], accum_out=ksum[:, b:b + 1]).then_inc(ke_ready, 1)
            for b in range(B):
                act.wait_ge(q_turned, b + 1)
                act.activation(qeT[:, b, :], k.bank[2 + b % 2][:], ACT.Copy).then_inc(qT_copied, 1)
            norm2.scalar_sqrt(act)

        @block.vector
        def _(dve):
            link = Link(dve, order)
            norm.vector(dve, link)
            for t in range(NT):
                bank = k.bank[4 + t % 2]
                dve.wait_ge(qv_done, t + 1)
                dve.tensor_reduce(nqmax[:, t:t + 1], bank[:, 0:D], AX_X, ALU.max, negate=True).then_inc(qmax_ready, 1)
                dve.tensor_copy(v[:, t, :], bank[:, D:2 * D]).then_inc(v_ready, 1)
            for b in range(B):
                dve.wait_ge(k_done, b + 1)
                dve.tensor_reduce(nkmax[:, b:b + 1], k.bank[6 + b % 2][:], AX_X, ALU.max, negate=True).then_inc(kmax_ready, 1)
            for b in range(B):
                dve.wait_ge(ke_turned, b + 1)
                dve.tensor_copy(ke[:, b * TPB:(b + 1) * TPB, :].rearrange("p j d -> p (j d)"), k.bank[b % 2][:]).then_inc(ke_copied, 1)
            dve.wait_ge(qe_ready, NT)
            dve.reciprocal(rq[:], qsum[:])
            dve.wait_ge(ke_ready, B)
            link(dve.reciprocal(rk[:], ksum[:]))
            dve.wait_ge(ctx_done, 1)
            dve.tensor_copy(ctxT[:].rearrange("p b d -> p (b d)"), k.bank[4][:]).then_inc(ctx_copied, 1)
            dve.wait_ge(cw_done, 1)
            for b in range(B):
                dve.tensor_scalar(cw[:, b, :], k.bank[5][:, b * D:(b + 1) * D], rk[:, b:b + 1], float(D) ** -0.5, ALU.mult, ALU.mult)\
                    .then_inc(cw_ready, 1)
            dve.wait_ge(pool_order, 2)
            for t in range(NT):
                dve.wait_ge(out_done, t // TPB + 1)
                last = dve.scalar_tensor_tensor(r[:, t, :], k.bank[6 + (t // TPB) % 2][:, (t % TPB) * D:(t % TPB + 1) * D], rq[:, t:t + 1], xb[:, t, :],
                                                ALU.mult, ALU.add)
                if t % TPB == TPB - 1:
                    last.then_inc(out_added, 1)
            dve.wait_ge(out_added, B)
            norm2.statistics(dve, link, r)
            dve.wait_ge(norm2.std_ready, 1)
            link(dve.reciprocal(norm2.rstd[:], norm2.std[:]))
            for t in range(NT):
                last = dve.tensor_scalar(r[:, t, :], r[:, t, :], norm2.mv[:, t, 0:1], norm2.rstd[:, t:t + 1], ALU.subtract, ALU.mult)
            link(last)
            link(dve.tensor_tensor(r[:], r[:], bcast(gam[:, 0:1], (0, NT), (1, D)), ALU.mult))
            dve.tensor_tensor(k.x[:], k.x[:], r[:], ALU.add)

        @block.tensor
        def _(pe):
            norm.tensor(pe)
            pe.wait_ge(loaded_w, 112)
            for t in range(NT):
                pe.wait_ge(norm.xnT_ready, t // TPB + 1)
                if t >= 2:
                    pe.wait_ge(qe_ready, t - 1)
                    pe.wait_ge(v_ready, t - 1)
                pe.matmul(k.bank[4 + t % 2][:, 0:2 * D], k.xnT[:, t * P:(t + 1) * P], wqv[:], start=True, stop=True).then_inc(qv_done, 1)
            for b in range(B):
                if b >= 2:
                    pe.wait_ge(ke_ready, b - 1)
                pe.matmul(k.bank[6 + b % 2][:], wk[:], k.xnT[:, b * T:(b + 1) * T], start=True, stop=True).then_inc(k_done, 1)
            for b in range(B):
                pe.wait_ge(qe_ready, (b + 1) * TPB)
                if b >= 2:
                    pe.wait_ge(qT_copied, b - 1)
                for j in range(TPB):
                    last = pe.transpose(k.bank[2 + b % 2][:, j * P:(j + 1) * P], qe[:, b * TPB + j, :], k.ident[:])
                last.then_inc(q_turned, 1)
            for b in range(B):
                pe.wait_ge(ke_ready, b + 1)
                if b >= 2:
                    pe.wait_ge(ke_copied, b - 1)
                for j in range(TPB):
                    last = pe.transpose(k.bank[b % 2][:, j * P:(j + 1) * P], keT[:, b, j * P:(j + 1) * P], k.ident[:])
                last.then_inc(ke_turned, 1)
            for b in range(B):
                pe.wait_ge(ke_copied, b + 1)
                pe.wait_ge(v_ready, NT)
                for j in range(TPB):
                    last = pe.matmul(k.bank[4][:, b * D:(b + 1) * D], v[:, b * TPB + j, :], ke[:, b * TPB + j, :], start=(j == 0), stop=(j == TPB - 1))
            last.then_inc(ctx_done, 1)
            pe.wait_ge(ctx_copied, 1)
            for b in range(B):
                last = pe.matmul(k.bank[5][:, b * D:(b + 1) * D], ctxT[:, b, :], wo[:], start=True, stop=True)
            last.then_inc(cw_done, 1)
            for b in range(B):
                pe.wait_ge(cw_ready, b + 1)
                pe.wait_ge(qT_copied, b + 1)
                if b >= 2:
                    pe.wait_ge(out_added, b - 1)
                for j in range(TPB):
                    last = pe.matmul(k.bank[6 + b % 2][:, j * D:(j + 1) * D], qeT[:, b, j * P:(j + 1) * P], cw[:, b, :], start=True, stop=True)
                last.then_inc(out_done, 1)



def layer_scan(k, tag, w_in, conv_w, conv_b, w_xproj, w_dt, b_dt, A_log, Dskip, w_out, ln_g, ln_b):
    nc = k.nc
    DI, N = A_log.shape
    TAPS = conv_w.shape[2]
    C = DI // P
    G2 = 4 // C
    UN = G2 * C
    Q, QB = N * UN, N * G2
    with ExitStack() as ctx:
        def sb(name, shape, dt=F32):
            return k.sb(f"{tag}_{name}", shape, dt, ctx)

        def sem(name):
            return k.sem(f"{tag}_{name}")

        norm = Norm(k, tag, ctx)
        norm2 = Norm(k, f"{tag}2", ctx)
        win = sb("win", [D, 2 * DI])
        cw = sb("cw", [P, C, TAPS])
        cols = sb("cols", [P, 3, C])
        lngb = sb("lngb", [D, 2])
        wx3 = sb("wx3", [P, C, 3, 2 * N])
        wdt = sb("wdt", [P, C, DI])
        wout = sb("wout", [P, C, D])
        A = sb("A", [P, C, N])
        z2 = sb("z2", [P, NT, D])
        xp = sb("xp", [P, C, B, TAPS - 1 + T])
        xc = sb("xc", [P, C, B, T])
        zs = sb("zs", [P, C, B, T])
        dt_ = sb("dt", [P, C, B, T])
        dtx = sb("dtx", [P, C, B, T])
        t1 = sb("t1", [3 * 2 * N, T], BF16)
        t2 = sb("t2", [3 * 2 * N, T], BF16)
        r1 = sb("r1", [3 * 2 * N, T])
        r2 = sb("r2", [3 * 2 * N, T])
        bc = sb("bc", [3 * 2 * N, B, T], BF16)
        spread = sb("spread", [3 * 2 * N, 2 * N, P], BF16)
        keep = sb("keep", [P, B, T])
        bsb = sb("bsb", [P, B, T])
        push = sb("push", [P, B, T])
        h = sb("h", [P, B, T])
        hc = sb("hc", [P, B, T])

        loaded_w = sem("loaded_w")
        order, pool_order, act_order, waited = sem("order"), sem("pool_order"), sem("act_order"), sem("waited")
        z2_ready, xz_done, xz_copied, conv_ready, xc_ready = sem("z2_ready"), sem("xz_done"), sem("xz_copied"), sem("conv_ready"), sem("xc_ready")
        bc_done, bc_ready, dt_done, dt_ready, soft_ready = sem("bc_done"), sem("bc_ready"), sem("dt_done"), sem("dt_ready"), sem("soft_ready")
        dtx_ready, skip_ready = sem("dtx_ready"), sem("skip_ready")
        b_done, b_copied, c_done, push_ready, keep_ready = sem("b_done"), sem("b_copied"), sem("c_done"), sem("push_ready"), sem("keep_ready")
        scanned, hc_ready, summed, gated = sem("scanned"), sem("hc_ready"), sem("summed"), sem("gated")
        out_done, added, x_ready = sem("out_done"), sem("added"), sem("x_ready")
        NW = 12

        block = ctx.enter_context(nc.Block())

        @block.sync
        def _(sp):
            sp.dma_start(win[:], w_in).then_inc(loaded_w, 16)
            sp.dma_start(cw[:], conv_w.rearrange("(c p) a k -> p c (a k)", p=P)).then_inc(loaded_w, 16)
            for i, v in enumerate((conv_b, b_dt, Dskip)):
                sp.dma_start(cols[:, i, :], v.rearrange("(c p) -> p c", p=P), allow_slow_non_contiguous=True).then_inc(loaded_w, 16)
            sp.dma_start(A[:], A_log.rearrange("(c p) n -> p c n", p=P)).then_inc(loaded_w, 16)
            for r in range(3):
                sp.dma_start(wx3[:, :, r, :], w_xproj.rearrange("(c p) n -> p c n", p=P)).then_inc(loaded_w, 16)
            sp.dma_start(wdt[:], w_dt.rearrange("(c p) n -> p c n", p=P)).then_inc(loaded_w, 16)
            sp.dma_start(wout[:], w_out.rearrange("(c p) n -> p c n", p=P)).then_inc(loaded_w, 16)
            sp.dma_start(lngb[:, 0:1], ln_g.rearrange("(d a) -> d a", a=1)).then_inc(loaded_w, 16)
            sp.dma_start(lngb[:, 1:2], ln_b.rearrange("(d a) -> d a", a=1)).then_inc(loaded_w, 16)

        @block.gpsimd
        def _(pool):
            k.clear_past()
            link = Link(pool, pool_order)
            link(pool.memset(xp[:, :, :, 0:TAPS - 1], 0.0))
            link(pool.memset(spread[:], 0.0))
            for part in range(3):
                link(pool.affine_select(out=spread[:], in_=spread[:], compare_op=ALU.not_equal, fill=1.0, base=-2 * N * part,
                                        pattern=[[-1, 2 * N], [0, P]], channel_multiplier=1))
            pool.wait_ge(norm.xn_ready, NT)
            pool.tensor_tensor(k.x[:], k.x[:], k.xn[:], ALU.add).then_inc(x_ready, 1)
            pool.wait_ge(dtx_ready, C)
            for g in range(B // G2):
                with pool.Fori(0, N) as n:
                    for i in range(UN):
                        q = g * Q + n * UN + i
                        pool.wait_ge(b_copied, g * QB + n * G2 + i // C + 1 + G2)
                        pool.wait_ge(scanned, q + 1)
                        pool.tensor_tensor(push[:, i, :], dtx[:, i % C, g * G2 + i // C, :], bsb[:, i // C, :], ALU.mult).then_inc(push_ready, 1)

        @block.scalar
        def _(act):
            link = Link(act, act_order)
            norm.scalar_sqrt(act)
            norm2.scalar_sqrt(act)
            act.wait_ge(loaded_w, 16 * (NW + 1))
            for g in range(B):
                act.wait_ge(norm2.turned, g + 1)
                act.activation(k.xnT[:, g * T:(g + 1) * T], k.bank[g][:], ACT.Identity, bias=lngb[:, 1:2], scale=lngb[:, 0:1])\
                   .then_inc(norm2.xnT_ready, 1)
            act.wait_ge(pool_order, 1)
            for b in range(B):
                for m in range(2 * C):
                    i = b * 2 * C + m
                    act.wait_ge(xz_done, i + 1)
                    bank = k.bank[4 + i % 4]
                    if m < C:
                        act.activation(xp[:, m, b, TAPS - 1:], bank[:], ACT.Copy).then_inc(xz_copied, 1)
                    else:
                        act.activation(zs[:, m - C, b, :], bank[:], ACT.Silu).then_inc(xz_copied, 1)
            for c in range(C):
                act.wait_ge(conv_ready, c + 1)
                act.activation(xc[:, c, :, :], xc[:, c, :, :], ACT.Silu).then_inc(xc_ready, 1)
            for c in range(C):
                for b in range(B):
                    i = c * B + b
                    act.wait_ge(dt_done, i + 1)
                    link(act.activation(dtx[:, c, b, :], k.bank[i % 4][:], ACT.Abs, bias=cols[:, 1, c:c + 1]))
                    act.activation(dtx[:, c, b, :], dtx[:, c, b, :], ACT.Exp, scale=-1.0).then_inc(dt_ready, 1)
            act.wait_ge(dt_ready, C * B)
            link(act.activation(A[:].rearrange("p c n -> p (c n)"), A[:].rearrange("p c n -> p (c n)"), ACT.Exp))
            link(act.activation(A[:].rearrange("p c n -> p (c n)"), A[:].rearrange("p c n -> p (c n)"), ACT.Copy, scale=-1.0))
            for c in range(C):
                act.activation(dtx[:, c, :, :], dtx[:, c, :, :], ACT.Ln, bias=1.0).then_inc(soft_ready, 1)
            act.wait_ge(dtx_ready, C)
            for g in range(B // G2):
                with act.Fori(0, N) as n:
                    for i in range(UN):
                        q = g * Q + n * UN + i
                        bb, c = i // C, i % C
                        if c == 0:
                            act.wait_ge(b_done, g * QB + n * G2 + bb + 1)
                            act.wait_ge(push_ready, q + C)
                            act.activation(bsb[:, bb, :], k.bank[4 + bb][:], ACT.Copy).then_inc(b_copied, 1)
                        act.wait_ge(scanned, q + 1)
                        act.sem_inc(waited, 1)
                        act.activation(keep[:, i, :], dt_[:, c, g * G2 + bb, :], ACT.Exp, scale=A[:, c, bass.ds(n, 1)]).then_inc(keep_ready, 1)

        @block.vector
        def _(dve):
            link = Link(dve, order)
            for s, m in ((scanned, UN), (summed, UN), (b_copied, G2), (hc_ready, UN), (push_ready, UN)):
                dve.sem_inc(s, m)
            norm.vector(dve, link)
            dve.wait_ge(norm.xn_ready, NT)
            norm2.statistics(dve, link, k.xn)
            dve.wait_ge(norm2.std_ready, 1)
            link(dve.reciprocal(norm2.rstd[:], norm2.std[:]))
            for t in range(NT):
                dve.tensor_scalar(z2[:, t, :], k.xn[:, t, :], norm2.mv[:, t, 0:1], norm2.rstd[:, t:t + 1],
                                  ALU.subtract, ALU.mult).then_inc(z2_ready, 1)
            dve.wait_ge(loaded_w, 16 * (NW + 1))
            dve.wait_ge(pool_order, 1)
            dve.wait_ge(xz_copied, 2 * C * B)
            for c in range(C):
                link(dve.tensor_scalar(xc[:, c, :, :], xp[:, c, :, 0:T], cw[:, c, 0:1], cols[:, 0, c:c + 1], ALU.mult, ALU.add))
                for j in range(1, TAPS):
                    last = dve.scalar_tensor_tensor(xc[:, c, :, :], xp[:, c, :, j:j + T], cw[:, c, j:j + 1], xc[:, c, :, :], ALU.mult, ALU.add)
                    if j < TAPS - 1:
                        link(last)
                last.then_inc(conv_ready, 1)
            for b in range(B):
                dve.wait_ge(bc_done, b + 1)
                if b:
                    dve.wait_ge(bc_ready, b)
                ps = k.bank[4 + b][0:3 * 2 * N, :]
                G = 2 * N
                link(dve.tensor_copy(t1[:], ps))
                link(dve.tensor_tensor(r1[:], ps, t1[:], ALU.subtract))
                link(dve.tensor_copy(t2[:], r1[:]))
                link(dve.tensor_tensor(r2[:], r1[:], t2[:], ALU.subtract))
                dve.tensor_copy(bc[0:G, b, :], t1[0:G, :])
                dve.tensor_copy(bc[G:2 * G, b, :], t2[G:2 * G, :])
                dve.tensor_copy(bc[2 * G:3 * G, b, :], r2[2 * G:3 * G, :]).then_inc(bc_ready, 1)
            for c in range(C):
                for b in range(B):
                    i = c * B + b
                    dve.wait_ge(dt_done, i + 1)
                    dve.wait_ge(dt_ready, i + 1)
                    dve.tensor_scalar(dt_[:, c, b, :], k.bank[i % 4][:], cols[:, 1, c:c + 1], 0.0, ALU.add, ALU.max).then_inc(gated, 1)
            dve.wait_ge(gated, C * B)
            for c in range(C):
                dve.wait_ge(soft_ready, c + 1)
                link(dve.tensor_tensor(dt_[:, c, :, :], dt_[:, c, :, :], dtx[:, c, :, :], ALU.add))
                dve.tensor_tensor(dtx[:, c, :, :], dt_[:, c, :, :], xc[:, c, :, :], ALU.mult).then_inc(dtx_ready, 1)
            dve.wait_ge(dtx_ready, C)
            for c in range(C):
                dve.tensor_scalar(xc[:, c, :, :], xc[:, c, :, :], cols[:, 2, c:c + 1], None, ALU.mult).then_inc(skip_ready, 1)
            for g in range(B // G2):
                with dve.Fori(0, N) as n:
                    def scan(i):
                        q = g * Q + n * UN + i
                        dve.wait_ge(keep_ready, q + 1)
                        dve.wait_ge(push_ready, q + 1 + UN)
                        dve.wait_ge(hc_ready, q + 1)
                        dve.tensor_tensor_scan(h[:, i, :], keep[:, i, :], push[:, i, :], 0.0, ALU.mult, ALU.add).then_inc(scanned, 1)

                    def weigh(i):
                        q = g * Q + n * UN + i
                        dve.wait_ge(scanned, q + 1 + UN)
                        dve.wait_ge(c_done, g * QB + n * G2 + i // C + 1)
                        dve.wait_ge(summed, q + 1)
                        dve.tensor_tensor(hc[:, i, :], h[:, i, :], k.bank[6 + i // C][:], ALU.mult).then_inc(hc_ready, 1)

                    scan(0)
                    for i in range(1, UN):
                        scan(i)
                        weigh(i - 1)
                    weigh(UN - 1)
                dve.wait_ge(summed, (g + 1) * Q + UN)
                for i in range(UN):
                    c, b = i % C, g * G2 + i // C
                    dve.tensor_tensor(zs[:, c, b, :], zs[:, c, b, :], k.bank[i][:], ALU.mult).then_inc(gated, 1)
            dve.wait_ge(x_ready, 1)
            for g in range(B):
                dve.wait_ge(out_done, g + 1)
                xv = k.x[:, g * TPB:(g + 1) * TPB, :].rearrange("p j d -> p (j d)")
                dve.tensor_tensor(xv, xv, k.bank[4 + g % 4][:], ALU.add).then_inc(added, 1)

        @block.tensor
        def _(pe):
            norm2.tensor(pe, z2, z2_ready)
            pe.wait_ge(loaded_w, 16 * (NW + 1))
            for b in range(B):
                pe.wait_ge(norm2.xnT_ready, b + 1)
                for m in range(2 * C):
                    i = b * 2 * C + m
                    if i >= 4:
                        pe.wait_ge(xz_copied, i - 3)
                    pe.matmul(k.bank[4 + i % 4][:], win[:, m * P:(m + 1) * P], k.xnT[:, b * T:(b + 1) * T], start=True, stop=True).then_inc(xz_done, 1)
            pe.wait_ge(xc_ready, C)
            pe.wait_ge(xz_copied, 2 * C * B)
            for b in range(B):
                for c in range(C):
                    last = pe.matmul(k.bank[4 + b][0:3 * 2 * N, :], wx3[:, c, :, :].rearrange("p r n -> p (r n)"), xc[:, c, b, :], start=(c == 0), stop=(c == C - 1))
                last.then_inc(bc_done, 1)
            for m in range(C):
                for b in range(B):
                    i = m * B + b
                    if i >= 4:
                        pe.wait_ge(gated, i - 3)
                    for c in range(C):
                        last = pe.matmul(k.bank[i % 4][:], wdt[:, c, m * P:(m + 1) * P], xc[:, c, b, :], start=(c == 0), stop=(c == C - 1))
                    last.then_inc(dt_done, 1)
            pe.wait_ge(pool_order, 5)
            pe.wait_ge(bc_ready, B)
            pe.wait_ge(skip_ready, C)
            for g in range(B // G2):
                pe.wait_ge(gated, C * B + g * UN)

                def spread_b(n, bb):
                    pe.wait_ge(b_copied, g * QB + n * G2 + bb + 1)
                    sel = spread[:, bass.ds(n, 1), :].rearrange("r n p -> r (n p)")
                    pe.matmul(k.bank[4 + bb][:], sel, bc[:, g * G2 + bb, :], start=True, stop=True).then_inc(b_done, 1)

                def spread_c(n, bb):
                    pe.wait_ge(hc_ready, g * Q + n * UN + (bb + 1) * C)
                    sel = spread[:, bass.ds(n + N, 1), :].rearrange("r n p -> r (n p)")
                    pe.matmul(k.bank[6 + bb][:], sel, bc[:, g * G2 + bb, :], start=True, stop=True).then_inc(c_done, 1)

                def accumulate(n, i):
                    pe.wait_ge(hc_ready, g * Q + n * UN + i + 1 + UN)
                    pe.matmul(k.bank[i][:], k.ident[:], hc[:, i, :], start=False, stop=False, skip_group_check=True).then_inc(summed, 1)

                for bb in range(G2):
                    spread_b(0, bb)
                for bb in range(G2):
                    spread_c(0, bb)
                for i in range(UN):
                    pe.matmul(k.bank[i][:], k.ident[:], xc[:, i % C, g * G2 + i // C, :], start=True, stop=False, skip_group_check=True)
                with pe.Fori(0, N - 1) as n:
                    for i in range(UN):
                        if i % C == 0:
                            spread_b(n + 1, i // C)
                        if i % C == C - 1:
                            spread_c(n + 1, i // C)
                        accumulate(n, i)
                for i in range(UN):
                    accumulate(N - 1, i)
            pe.wait_ge(gated, C * B + C * B)
            for g in range(B):
                for j in range(TPB):
                    t = g * TPB + j
                    for c in range(C):
                        last = pe.matmul(k.bank[4 + g % 4][:, j * D:(j + 1) * D], zs[:, c, g, j * P:(j + 1) * P], wout[:, c, :], start=(c == 0), stop=(c == C - 1))
                last.then_inc(out_done, 1)



def layer_moe_tokens(k, tag, gate_weight, gate_bias, w_gate, w_up, w_down, s_gate, s_up, s_down, a_gate, a_up, a_down):
    nc = k.nc
    E, I = w_gate.shape[0], w_gate.shape[2]
    L, AI = a_gate.shape[0], a_gate.shape[2]
    SI = s_gate.shape[1]
    NG, TOPK, SCALE, ALPHA = 4, 6, 0.2, 0.1
    GE = E // NG
    ET, AT = E * I // P, L * AI // P
    TILES = ET + AT + 1
    LOW, HIT = -1e30, 3e38
    STK = 3 * E + L
    with ExitStack() as ctx:
        def sb(name, shape, dt=F32):
            return k.sb(f"{tag}_{name}", shape, dt, ctx)

        def sem(name):
            return k.sem(f"{tag}_{name}")

        norm = Norm(k, tag, ctx)
        gw = sb("gw", [E, D])
        gwT = sb("gwT", [D, E])
        gb = sb("gb", [P, E])
        wg = sb("wg", [D, TILES * P])
        wu = sb("wu", [D, TILES * P])
        wd = sb("wd", [P, TILES, D])
        score = sb("score", [P, NT, E])
        sc = sb("sc", [P, NT, E])
        hi = sb("hi", [P, NT * NG, GE // 2])
        lo = sb("lo", [P, NT * NG, GE // 2])
        hi2 = sb("hi2", [P, NT * NG, GE // 4])
        lo2 = sb("lo2", [P, NT * NG, GE // 4])
        t2 = sb("t2", [P, NT * NG, GE // 4])
        top1 = sb("top1", [P, NT * NG])
        top2 = sb("top2", [P, NT * NG])
        gs = sb("gs", [P, NT, NG])
        wins = sb("wins", [P, NT, NG])
        duel = sb("duel", [P, 6, NT])
        gmask = sb("gmask", [P, NT, NG])
        masked = sb("masked", [P, NT, E])
        low = sb("low", [P, NT, E])
        best = sb("best", [P, NT, 8])
        only1 = sb("only1", [P, NT, 8])
        work = sb("work", [P, NT, E])
        work1 = sb("work1", [P, NT, E])
        total = sb("total", [P, NT])
        rtotal = sb("rtotal", [P, NT])
        cw = sb("cw", [P, NT, E])
        rest = sb("rest", [P, NT, E])
        stack = sb("stack", [P, NT, STK], BF16)
        stackT = sb("stackT", [STK, B * T], BF16)
        spread = sb("spread", [P, (ET + AT) * P], BF16)
        silu = sb("silu", [P, 2, T])
        gated = sb("gated", [P, 2, T])
        hidden = sb("hidden", [P, 2, T])

        loaded_gw, loaded_w = sem("loaded_gw"), sem("loaded_w")
        order, spread_made = sem("order"), sem("spread_made")
        gwT_turned, gwT_ready = sem("gwT_turned"), sem("gwT_ready")
        logits_ready, score_ready = sem("logits_ready"), sem("score_ready")
        stack_ready, stack_turned, stackT_ready = sem("stack_ready"), sem("stack_turned"), sem("stackT_ready")
        in_ready, silu_ready, hidden_ready = sem("in_ready"), sem("silu_ready"), sem("hidden_ready")
        down_done, acc_used = sem("down_done"), sem("acc_used")

        block = ctx.enter_context(nc.Block())
        NW = 9

        @block.sync
        def _(sp):
            sp.dma_start(gw[:], gate_weight).then_inc(loaded_gw, 16)
            sp.dma_start(gb[:], gate_bias.partition_broadcast(P)).then_inc(loaded_gw, 16)
            for dst, e, l, s in ((wg, w_gate, a_gate, s_gate), (wu, w_up, a_up, s_up)):
                sp.dma_start(dst[:, 0:E * I].rearrange("h (e i) -> h e i", i=I), e.rearrange("e h i -> h e i")).then_inc(loaded_w, 16)
                sp.dma_start(dst[:, E * I:E * I + L * AI].rearrange("h (e i) -> h e i", i=AI),
                             l.rearrange("e h i -> h e i")).then_inc(loaded_w, 16)
                sp.dma_start(dst[:, E * I + L * AI:E * I + L * AI + SI], s).then_inc(loaded_w, 16)
            sp.dma_start(wd[:, 0:ET, :], w_down.rearrange("(t e) i d -> (e i) t d", e=P // I)).then_inc(loaded_w, 16)
            sp.dma_start(wd[:, ET:ET + AT, :], a_down.rearrange("(t e) i d -> (e i) t d", e=P // AI)).then_inc(loaded_w, 16)
            sp.dma_start(wd[0:SI, ET + AT, :], s_down).then_inc(loaded_w, 16)

        @block.gpsimd
        def _(pool):
            k.clear_past()
            link = Link(pool, spread_made)
            link(pool.memset(wg[:, TILES * P - (P - SI):], 0.0))
            link(pool.memset(wu[:, TILES * P - (P - SI):], 0.0))
            link(pool.memset(wd[SI:P, TILES - 1, :], 0.0))
            link(pool.memset(spread[:], 0.0))
            for part in range(3):
                v = spread[:, 0:ET * P].rearrange("r (e i) -> r e i", i=I)
                link(pool.affine_select(out=v, in_=v, compare_op=ALU.not_equal, fill=1.0, base=-E * part,
                                        pattern=[[-1, E], [0, I]], channel_multiplier=1))
            v = spread[:, ET * P:].rearrange("r (e i) -> r e i", i=AI)
            link(pool.affine_select(out=v, in_=v, compare_op=ALU.not_equal, fill=1.0, base=-3 * E,
                                    pattern=[[-1, L], [0, AI]], channel_multiplier=1))

        @block.scalar
        def _(act):
            norm.scalar_sqrt(act)
            norm.scalar_copy(act)
            act.wait_ge(logits_ready, 1)
            act.activation(score[:].rearrange("p j e -> p (j e)"), k.bank[5][:], ACT.Sigmoid).then_inc(score_ready, 1)
            for g in range(2):
                act.wait_ge(stack_turned, g + 1)
                act.activation(stackT[:, g * 1024:(g + 1) * 1024], k.bank[6 + g][0:STK, :].bitcast(BF16), ACT.Copy)\
                   .then_inc(stackT_ready, 1)
            with act.Fori(0, B) as c:
                for t in range(TILES):
                    act.wait_ge(in_ready, c * TILES + t + 1)
                    act.wait_ge(hidden_ready, c * TILES + t + (1 if t else 2))
                    act.activation(silu[:, t % 2, :], k.bank[t % 2][:, :], ACT.Silu).then_inc(silu_ready, 1)

        @block.vector
        def _(dve):
            link = Link(dve, order)
            dve.sem_inc(hidden_ready, 2)
            dve.sem_inc(down_done, 2)
            dve.sem_inc(acc_used, 1)
            norm.vector(dve, link)
            dve.wait_ge(gwT_turned, 1)
            dve.tensor_copy(gwT[:], k.bank[4][:, 0:E]).then_inc(gwT_ready, 1)
            dve.wait_ge(loaded_gw, 32)
            dve.wait_ge(score_ready, 1)
            link(dve.tensor_tensor(sc[:], score[:], bcast(gb[:, 0:1], (0, NT), (1, E)), ALU.add))
            g8 = sc[:].rearrange("p j (g e) -> p (j g) e", e=GE)
            h = GE // 2
            dve.tensor_tensor(hi[:], g8[:, :, 0:h], g8[:, :, h:GE], ALU.max)
            link(dve.tensor_tensor(lo[:], g8[:, :, 0:h], g8[:, :, h:GE], ALU.min))
            q = h // 2
            dve.tensor_tensor(t2[:], hi[:, :, 0:q], hi[:, :, q:h], ALU.min)
            dve.tensor_tensor(lo2[:], lo[:, :, 0:q], lo[:, :, q:h], ALU.max)
            link(dve.tensor_tensor(hi2[:], hi[:, :, 0:q], hi[:, :, q:h], ALU.max))
            link(dve.tensor_tensor(lo2[:], lo2[:], t2[:], ALU.max))
            dve.tensor_tensor(top1[:], hi2[:, :, 0], hi2[:, :, 1], ALU.max)
            dve.tensor_tensor(t2[:, :, 0], hi2[:, :, 0], hi2[:, :, 1], ALU.min)
            link(dve.tensor_tensor(top2[:], lo2[:, :, 0], lo2[:, :, 1], ALU.max))
            link(dve.tensor_tensor(top2[:], top2[:], t2[:, :, 0], ALU.max))
            link(dve.tensor_tensor(gs[:].rearrange("p j g -> p (j g)"), top1[:], top2[:], ALU.add))
            pairs = [(a, b) for a in range(NG) for b in range(a + 1, NG)]
            dve.memset(wins[:], 0.0)
            for n, (a, b) in enumerate(pairs):
                last = dve.tensor_tensor(duel[:, n, :], gs[:, :, a], gs[:, :, b], ALU.is_ge)
            link(last)
            for n, (a, b) in enumerate(pairs):
                link(dve.tensor_tensor(wins[:, :, a], wins[:, :, a], duel[:, n, :], ALU.add))
                link(dve.scalar_tensor_tensor(wins[:, :, b], duel[:, n, :], -1.0, wins[:, :, b], ALU.mult, ALU.add))
            for g in range(NG):
                last = dve.tensor_scalar(gmask[:, :, g], wins[:, :, g], float(g), 2.0, ALU.add, ALU.is_ge)
            link(last)
            emask = bcast(gmask[:, 0, 0:1], (1, NT * NG), (0, GE))
            link(dve.tensor_scalar(low[:].rearrange("p j (g e) -> p (j g) e", e=GE), emask, -LOW, LOW, ALU.mult, ALU.add))
            link(dve.tensor_tensor(masked[:].rearrange("p j (g e) -> p (j g) e", e=GE), g8, emask, ALU.mult))
            link(dve.tensor_tensor(masked[:], masked[:], low[:], ALU.add))
            for j in range(NT):
                last = dve.max(best[:, j, :], masked[:, j, :])
            link(last)
            dve.memset(only1[:, :, 1:8], LOW)
            dve.tensor_copy(only1[:, :, 0], best[:, :, 0])
            link(dve.memset(best[:, :, TOPK:8], LOW))
            for j in range(NT):
                dve.match_replace(work[:, j, :], best[:, j, :], masked[:, j, :], HIT)
                last = dve.match_replace(work1[:, j, :], only1[:, j, :], masked[:, j, :], HIT)
            link(last)
            w8 = work[:].rearrange("p j (g e) -> p (j g) e", e=GE)
            w18 = work1[:].rearrange("p j (g e) -> p (j g) e", e=GE)
            dve.scalar_tensor_tensor(w8, w8, HIT, emask, ALU.is_equal, ALU.mult)
            link(dve.scalar_tensor_tensor(w18, w18, HIT, emask, ALU.is_equal, ALU.mult))
            dve.tensor_tensor(stack[:, :, 3 * E:], work1[:, :, 0::2], work1[:, :, 1::2], ALU.add)
            link(dve.tensor_tensor(cw[:], work[:], score[:], ALU.mult))
            link(dve.tensor_reduce(total[:], cw[:], AX_X, ALU.add))
            link(dve.tensor_scalar(total[:], total[:], 1e-20, None, ALU.add))
            link(dve.reciprocal(rtotal[:], total[:]))
            link(dve.scalar_tensor_tensor(cw[:], cw[:], SCALE, bcast(rtotal[:, 0:1], (1, NT), (0, E)), ALU.mult, ALU.mult))
            link(dve.tensor_copy(stack[:, :, 0:E], cw[:]))
            link(dve.tensor_tensor(rest[:], cw[:], stack[:, :, 0:E], ALU.subtract))
            link(dve.tensor_copy(stack[:, :, E:2 * E], rest[:]))
            link(dve.tensor_tensor(rest[:], rest[:], stack[:, :, E:2 * E], ALU.subtract))
            dve.tensor_copy(stack[:, :, 2 * E:3 * E], rest[:]).then_inc(stack_ready, 1)
            with dve.Fori(0, B) as c:
                link.start(c, TILES - 1)
                for t in range(TILES):
                    sl, up, wt = silu[:, t % 2, :], k.bank[2 + t % 2][:, :], k.bank[4 + t % 2][:, :]
                    dve.wait_ge(silu_ready, c * TILES + t + 1)
                    dve.wait_ge(down_done, c * TILES + t + (1 if t else 2))
                    if t == TILES - 1:
                        dve.tensor_tensor(hidden[:, t % 2, :], sl, up, ALU.mult).then_inc(hidden_ready, 1)
                        continue
                    link(dve.scalar_tensor_tensor(gated[:, t % 2, :], sl, 1.0 if t < ET else ALPHA, up, ALU.mult, ALU.mult))
                    dve.tensor_tensor(hidden[:, t % 2, :], gated[:, t % 2, :], wt, ALU.mult).then_inc(hidden_ready, 1)
                dve.wait_ge(down_done, (c + 1) * TILES + 2)
                xc = k.x[:].rearrange("p j d -> p (j d)")[:, bass.ds(c * T, T)]
                dve.tensor_tensor(xc, xc, k.bank[6][:], ALU.add).then_inc(acc_used, 1)
                link.end(TILES - 1, B)

        @block.tensor
        def _(pe):
            norm.tensor(pe)
            pe.wait_ge(loaded_gw, 32)
            pe.transpose(k.bank[4][:, 0:E], gw[:], k.ident[0:E, 0:E]).then_inc(gwT_turned, 1)
            pe.wait_ge(gwT_ready, 1)
            pe.wait_ge(norm.xnT_ready, B)
            for j in range(NT):
                last = pe.matmul(k.bank[5][:, j * E:(j + 1) * E], k.xnT[:, j * P:(j + 1) * P], gwT[:], start=True, stop=True)
            last.then_inc(logits_ready, 1)
            pe.wait_ge(stack_ready, 1)
            for j in range(NT):
                g, o = 6 + j // 8, j % 8
                last = pe.transpose(k.bank[g][0:STK, :].bitcast(BF16)[:, o * P:(o + 1) * P], stack[:, j, :], k.ident16[:])
                if o == 7:
                    last.then_inc(stack_turned, 1)
            pe.wait_ge(stackT_ready, 2)
            pe.wait_ge(loaded_w, 16 * NW)
            pe.wait_ge(spread_made, 8)
            with pe.Fori(0, B) as c:
                xc = k.xnT[:, bass.ds(c * T, T)]
                wc = stackT[:, bass.ds(c * T, T)]

                def products(t):
                    pe.wait_ge(hidden_ready, c * TILES + t + (1 if t else 2))
                    pe.matmul(k.bank[2 + t % 2][:, :], wu[:, t * P:(t + 1) * P], xc, start=True, stop=True)
                    if t < TILES - 1:
                        pe.matmul(k.bank[4 + t % 2][:], spread[0:STK, t * P:(t + 1) * P], wc, start=True, stop=True)
                    pe.matmul(k.bank[t % 2][:, :], wg[:, t * P:(t + 1) * P], xc, start=True, stop=True).then_inc(in_ready, 1)

                def down(t):
                    pe.wait_ge(hidden_ready, c * TILES + t + 3)
                    if t == 0:
                        pe.wait_ge(acc_used, c + 1)
                    for j in range(TPB):
                        last = pe.matmul(k.bank[6][:, j * D:(j + 1) * D], hidden[:, t % 2, j * P:(j + 1) * P],
                                         wd[:, t, :], start=(t == 0 and j == 0), stop=(t == TILES - 1), skip_group_check=True)
                    last.then_inc(down_done, 1)

                products(0)
                for t in range(TILES):
                    if t + 1 < TILES:
                        products(t + 1)
                    down(t)



def layer_delta(k, tag, Wq, Wk, Wv, Wb, conv_q, conv_k, conv_v, g, Wo):
    nc = k.nc
    H = Wb.shape[1]
    HD = D // H
    TAPS = conv_q.shape[2]
    CH = 64
    NCH = T // CH
    LEVELS = CH.bit_length() - 1
    with ExitStack() as ctx:
        def sb(name, shape, dt=F32):
            return k.sb(f"{tag}_{name}", shape, dt, ctx)

        def sem(name):
            return k.sem(f"{tag}_{name}")

        norm = Norm(k, tag, ctx)
        w3 = sb("w3", [D, 3, D])
        wb = sb("wb", [D, H])
        wbr = sb("wbr", [D, H, HD])
        wo = sb("wo", [D, D])
        cw = sb("cw", [P, 3, TAPS])
        gc = sb("gc", [P, 1])
        xp = sb("xp", [P, 3, B, TAPS - 1 + T])
        s3 = sb("s3", [P, 3, B, T])
        beta = sb("beta", [P, B, T])
        kb = sb("kb", [P, B, T])
        heads = sb("heads", [P, P])
        ones = sb("ones", [P, P])
        ident2 = sb("ident2", [P, P])
        masks = sb("masks", [P, LEVELS, P])
        kbn = sb("kbn", [P, NT, D])
        vbn = sb("vbn", [P, NT, D])
        aT = sb("aT", [P, B, T])
        cT = sb("cT", [P, B, T])
        m = sb("m", [P, B, T])
        mT = sb("mT", [P, B, T])
        xx = sb("xx", [P, B, T])
        wT = sb("wT", [P, B, T])
        prod = sb("prod", [P, T])
        ka = sb("ka", [P, B, NCH])
        kbv = sb("kbv", [P, B, NCH])
        sd = sb("sd", [P, B, NCH + 1])
        early = sb("early", [P, B, NCH, B])
        qk = sb("qk", [P, B, NCH, B])
        u0 = sb("u0", [P, B, NCH, B])
        sq = xx
        uT = beta
        o = cT

        loaded_w = sem("loaded_w")
        order, pool_order = sem("order"), sem("pool_order")
        in_done, in_copied, conv_ready, act_ready = sem("in_done"), sem("in_copied"), sem("conv_ready"), sem("act_ready")
        wbr_ready, beta_done, beta_ready = sem("wbr_ready"), sem("beta_done"), sem("beta_ready")
        sq_ready, norm_done, root_ready, unit_ready = sem("sq_ready"), sem("norm_done"), sem("root_ready"), sem("unit_ready")
        kb_ready, vb_ready, a_done, aT_ready = sem("kb_ready"), sem("vb_ready"), sem("a_done"), sem("aT_ready")
        n_turned, n_ready = sem("n_turned"), sem("n_ready")
        cT_ready, x_done, x_ready, y_done, yT_done, m_ready, mT_ready = (sem("cT_ready"), sem("x_done"), sem("x_ready"), sem("y_done"),
                                                                          sem("yT_done"), sem("m_ready"), sem("mT_ready"))
        t_ready, wu_done, w_copied, u_copied = sem("t_ready"), sem("wu_done"), sem("w_copied"), sem("u_copied")
        qk_ready, qk_done, o_ready, osq_ready, on_done, oroot_ready, on_ready, out_done = (
            sem("qk_ready"), sem("qk_done"), sem("o_ready"), sem("osq_ready"), sem("on_done"), sem("oroot_ready"), sem("on_ready"), sem("out_done"))
        NW = 5 + 3 + H

        block = ctx.enter_context(nc.Block())

        def flat(ap):
            return ap.rearrange("p b t -> p (b t)")

        @block.sync
        def _(sp):
            for i, w in enumerate((Wq, Wk, Wv)):
                sp.dma_start(w3[:, i, :], w).then_inc(loaded_w, 16)
            sp.dma_start(wb[:], Wb).then_inc(loaded_w, 16)
            sp.dma_start(wo[:], Wo).then_inc(loaded_w, 16)
            for i, w in enumerate((conv_q, conv_k, conv_v)):
                sp.dma_start(cw[:, i, :], w.rearrange("d a k -> d (a k)")).then_inc(loaded_w, 16)
            for h in range(H):
                sp.dma_start(gc[h * HD:(h + 1) * HD, :], g.rearrange("(d a) -> d a", a=1)).then_inc(loaded_w, 16)

        @block.gpsimd
        def _(pool):
            k.clear_past()
            link = Link(pool, pool_order)
            link(pool.memset(xp[:, :, :, 0:TAPS - 1], 0.0))
            link(pool.memset(ones[:], 1.0))
            hv = heads[:].rearrange("p (h d) -> p h d", d=HD)
            link(pool.memset(heads[:], 1.0))
            link(pool.affine_select(out=hv, in_=hv, compare_op=ALU.is_ge, fill=0.0, base=0, pattern=[[-HD, H], [0, HD]], channel_multiplier=1))
            link(pool.affine_select(out=hv, in_=hv, compare_op=ALU.is_ge, fill=0.0, base=HD - 1, pattern=[[HD, H], [0, HD]], channel_multiplier=-1))
            link(pool.memset(masks[:], 0.0))
            for l in range(LEVELS):
                s = 1 << l
                v = masks[:, l, :].rearrange("p (n a s) -> p n a s", a=2, s=s)[:, :, 1, :]
                link(pool.memset(v, 1.0))
                link(pool.affine_select(out=v, in_=v, compare_op=ALU.is_ge, fill=0.0, base=0, pattern=[[-2 * s, P // (2 * s)], [0, s]], channel_multiplier=1))
                link(pool.affine_select(out=v, in_=v, compare_op=ALU.is_ge, fill=0.0, base=s - 1, pattern=[[2 * s, P // (2 * s)], [0, s]], channel_multiplier=-1))
            link(pool.memset(sd[:, :, 0:1], 0.0))
            link(pool.memset(early[:], 1.0))
            link(pool.affine_select(out=early[:], in_=early[:], compare_op=ALU.is_ge, fill=0.0, base=0,
                                    pattern=[[1, B], [0, NCH], [-1, B]], channel_multiplier=0))
            link(pool.tensor_scalar(ident2[:], k.ident[:], 2.0, None, ALU.mult))
            for l in range(LEVELS):
                for b in range(B):
                    pool.wait_ge(aT_ready, b + 1)
                    if l:
                        pool.wait_ge(x_done, (l - 1) * B + b + 1)
                        if l == 1:
                            pool.wait_ge(mT_ready, b + 1)
                    pool.tensor_tensor(cT[:, b, :].rearrange("p (j i) -> p j i", i=P), aT[:, b, :].rearrange("p (j i) -> p j i", i=P),
                                       bcast(masks[:, l, 0:1], (0, TPB), (1, P)), ALU.mult).then_inc(cT_ready, 1)

        @block.scalar
        def _(act):
            norm.scalar_sqrt(act)
            norm.scalar_copy(act)
            act.wait_ge(pool_order, 1)
            for b in range(B):
                for i in range(3):
                    n = b * 3 + i
                    act.wait_ge(in_done, n + 1)
                    act.activation(xp[:, i, b, TAPS - 1:], k.bank[4 + n % 4][:], ACT.Copy).then_inc(in_copied, 1)
            for i in range(3):
                act.wait_ge(conv_ready, i + 1)
                act.activation(s3[:, i, :, :], s3[:, i, :, :], ACT.Silu).then_inc(act_ready, 1)
            for b in range(B):
                act.wait_ge(beta_done, b + 1)
                act.activation(beta[:, b, :], k.bank[b][:], ACT.Sigmoid).then_inc(beta_ready, 1)
            for n in range(2 * B):
                act.wait_ge(norm_done, n + 1)
                act.activation(xp[:, n // B, n % B, 0:T], k.bank[4 + n % 4][:], ACT.Sqrt).then_inc(root_ready, 1)
            for n in range(2 * B):
                act.wait_ge(n_turned, n + 1)
                dst = (kbn, vbn)[n // B]
                act.activation(dst[:, (n % B) * TPB:(n % B + 1) * TPB, :].rearrange("p j d -> p (j d)"), k.bank[n % 2][:], ACT.Copy).then_inc(n_ready, 1)
            for l in range(1, LEVELS):
                for b in range(B):
                    act.wait_ge(x_done, l * B + b + 1)
                    if l > 1:
                        act.wait_ge(yT_done, (l - 2) * B + b + 1)
                    act.activation(xx[:, b, :], k.bank[b % 2][:], ACT.Copy).then_inc(x_ready, 1)
            for b in range(B):
                act.wait_ge(wu_done, b + 1)
                act.activation(wT[:, b, :], k.bank[b % 2][:], ACT.Copy).then_inc(w_copied, 1)
            for b in range(B):
                act.wait_ge(o_ready, b + 1)
                act.activation(sq[:, b, :], o[:, b, :], ACT.Square).then_inc(osq_ready, 1)
            for b in range(B):
                act.wait_ge(on_done, b + 1)
                act.activation(wT[:, b, :], k.bank[4 + b][:], ACT.Sqrt, scale=1.0 / HD, bias=k.eps[:, 0:1]).then_inc(oroot_ready, 1)

        @block.vector
        def _(dve):
            link = Link(dve, order)
            norm.vector(dve, link)
            dve.wait_ge(loaded_w, 16 * NW)
            dve.tensor_copy(wbr[:], bcast(wb[:, 0:1], (1, H), (0, HD))).then_inc(wbr_ready, 1)
            dve.wait_ge(in_copied, 3 * B)
            for i in range(3):
                link(dve.tensor_scalar(s3[:, i, :, :], xp[:, i, :, 0:T], cw[:, i, 0:1], None, ALU.mult))
                for j in range(1, TAPS):
                    last = dve.scalar_tensor_tensor(s3[:, i, :, :], xp[:, i, :, j:j + T], cw[:, i, j:j + 1], s3[:, i, :, :], ALU.mult, ALU.add)
                    if j < TAPS - 1:
                        link(last)
                last.then_inc(conv_ready, 1)
            for i in range(2):
                dve.wait_ge(act_ready, i + 1)
                for b in range(B):
                    n = i * B + b
                    if i:
                        dve.wait_ge(norm_done, b + 1)
                    dve.tensor_tensor(sq[:, b, :], s3[:, i, b, :], s3[:, i, b, :], ALU.mult).then_inc(sq_ready, 1)
            for n in range(2 * B):
                i, b = n // B, n % B
                dve.wait_ge(root_ready, n + 1)
                link(dve.reciprocal(xp[:, i, b, 0:T], xp[:, i, b, 0:T]))
                last = dve.tensor_tensor(s3[:, i, b, :], s3[:, i, b, :], xp[:, i, b, 0:T], ALU.mult)
                last.then_inc(unit_ready, 1)
            dve.wait_ge(unit_ready, 2 * B)
            dve.wait_ge(act_ready, 3)
            for b in range(B):
                dve.wait_ge(beta_ready, b + 1)
                dve.tensor_tensor(kb[:, b, :], s3[:, 1, b, :], beta[:, b, :], ALU.mult).then_inc(kb_ready, 1)
            for b in range(B):
                dve.tensor_tensor(s3[:, 2, b, :], s3[:, 2, b, :], beta[:, b, :], ALU.mult).then_inc(vb_ready, 1)
            for b in range(B):
                dve.wait_ge(a_done, b + 1)
                dve.tensor_copy(aT[:, b, :], k.bank[4 + b % 2][:]).then_inc(aT_ready, 1)
            idb = bcast(k.ident[:, 0:1], (0, TPB), (1, P))
            for b in range(B):
                dve.wait_ge(x_done, b + 1)
                dve.wait_ge(cT_ready, b + 1)
                dve.tensor_tensor(m[:, b, :].rearrange("p (j i) -> p j i", i=P), idb, k.bank[b % 2][:].rearrange("p (j i) -> p j i", i=P), ALU.subtract)\
                    .then_inc(m_ready, 1)
                dve.tensor_tensor(mT[:, b, :].rearrange("p (j i) -> p j i", i=P), idb, cT[:, b, :].rearrange("p (j i) -> p j i", i=P), ALU.subtract)\
                    .then_inc(mT_ready, 1)
            for l in range(1, LEVELS):
                for b in range(B):
                    n = (l - 1) * B + b
                    dve.wait_ge(yT_done, n + 1)
                    dve.wait_ge(m_ready, l * B)
                    dve.wait_ge(mT_ready, l * B)
                    dve.tensor_tensor(m[:, b, :], m[:, b, :], k.bank[4 + b % 2][:], ALU.subtract).then_inc(m_ready, 1)
                    dve.tensor_tensor(mT[:, b, :], mT[:, b, :], k.bank[6 + b % 2][:], ALU.subtract).then_inc(mT_ready, 1)
            dve.wait_ge(mT_ready, LEVELS * B)
            id2 = bcast(ident2[:, 0:1], (0, TPB), (1, P))
            for b in range(B):
                mv = mT[:, b, :].rearrange("p (j i) -> p j i", i=P)
                dve.scalar_tensor_tensor(mv, mv, 3.0, id2, ALU.mult, ALU.subtract).then_inc(t_ready, 1)
            for b in range(B):
                dve.wait_ge(wu_done, b + 1)
                dve.tensor_copy(uT[:, b, :], k.bank[2 + b % 2][:]).then_inc(u_copied, 1)
            dve.wait_ge(u_copied, B)
            dve.wait_ge(w_copied, B)
            for src, dst in ((wT, ka), (uT, kbv)):
                for b in range(B):
                    link(dve.tensor_tensor(prod[:], s3[:, 1, b, :], src[:, b, :], ALU.mult))
                    link(dve.tensor_reduce(dst[:, b, :], prod[:].rearrange("p (n c) -> p n c", c=CH), AX_X, ALU.add))
            link(dve.tensor_scalar(ka[:], ka[:], -1.0, 1.0, ALU.mult, ALU.add))
            for b in range(B):
                last = dve.tensor_tensor_scan(sd[:, b, 1:NCH + 1], ka[:, b, :], kbv[:, b, :], 0.0, ALU.mult, ALU.add)
            link(last)
            def first(ap):
                return ap.rearrange("p b (n c) -> p b n c", c=CH)[:, :, :, 0:B]

            dve.tensor_tensor(qk[:], first(s3[:, 0, :, :]), first(s3[:, 1, :, :]), ALU.mult).then_inc(qk_ready, 1)
            for b in range(B):
                sdb = bcast(sd[:, b, 0:1], (1, NCH), (0, B))
                last = dve.tensor_tensor(u0[:, b, :, :], first(wT[:])[:, b], sdb, ALU.mult)
            link(last)
            link(dve.tensor_tensor(u0[:], first(uT[:]), u0[:], ALU.subtract))
            link(dve.tensor_tensor(u0[:], u0[:], early[:], ALU.mult))
            dve.wait_ge(qk_done, 1)
            link(dve.tensor_tensor(u0[:], u0[:], k.bank[4][:, 0:B * NCH * B].rearrange("p (b n c) -> p b n c", b=B, n=NCH), ALU.mult))
            for b in range(B):
                ov = o[:, b, :].rearrange("p (n c) -> p n c", c=CH)
                link(dve.tensor_tensor(ov, s3[:, 0, b, :].rearrange("p (n c) -> p n c", c=CH), bcast(sd[:, b, 0:1], (1, NCH), (0, CH)), ALU.mult))
                dve.tensor_tensor(ov[:, :, 0:B], ov[:, :, 0:B], u0[:, b, :, :], ALU.add).then_inc(o_ready, 1)
            dve.wait_ge(o_ready, B)
            for b in range(B):
                dve.wait_ge(oroot_ready, b + 1)
                link(dve.reciprocal(wT[:, b, :], wT[:, b, :]))
                dve.scalar_tensor_tensor(o[:, b, :], o[:, b, :], gc[:, 0:1], wT[:, b, :], ALU.mult, ALU.mult).then_inc(on_ready, 1)
            for b in range(B):
                dve.wait_ge(out_done, b + 1)
                xv = k.x[:, b * TPB:(b + 1) * TPB, :].rearrange("p j d -> p (j d)")
                dve.tensor_tensor(xv, xv, k.bank[b][:], ALU.add)

        @block.tensor
        def _(pe):
            norm.tensor(pe)
            pe.wait_ge(loaded_w, 16 * NW)
            for b in range(B):
                pe.wait_ge(norm.xnT_ready, b + 1)
                for i in range(3):
                    n = b * 3 + i
                    if n >= 4:
                        pe.wait_ge(in_copied, n - 3)
                    pe.matmul(k.bank[4 + n % 4][:], w3[:, i, :], k.xnT[:, b * T:(b + 1) * T], start=True, stop=True).then_inc(in_done, 1)
            pe.wait_ge(wbr_ready, 1)
            for b in range(B):
                pe.matmul(k.bank[b][:], wbr[:].rearrange("p h d -> p (h d)"), k.xnT[:, b * T:(b + 1) * T], start=True, stop=True).then_inc(beta_done, 1)
            pe.wait_ge(pool_order, 5)
            pe.wait_ge(in_copied, 3 * B)
            for n in range(2 * B):
                pe.wait_ge(sq_ready, n + 1)
                if n >= 4:
                    pe.wait_ge(root_ready, n - 3)
                pe.matmul(k.bank[4 + n % 4][:], heads[:], sq[:, n % B, :], start=True, stop=True).then_inc(norm_done, 1)
            pe.wait_ge(beta_ready, B)
            for n in range(2 * B):
                i, b = n // B, n % B
                pe.wait_ge((kb_ready, vb_ready)[i], b + 1)
                if n >= 2:
                    pe.wait_ge(n_ready, n - 1)
                for j in range(TPB):
                    src = (kb[:, b, j * P:(j + 1) * P], s3[:, 2, b, j * P:(j + 1) * P])[i]
                    last = pe.transpose(k.bank[n % 2][:, j * P:(j + 1) * P], src, k.ident[:])
                last.then_inc(n_turned, 1)
            pe.wait_ge(root_ready, 2 * B)
            for b in range(B):
                if b >= 2:
                    pe.wait_ge(aT_ready, b - 1)
                for j in range(TPB):
                    c = slice(j * P, (j + 1) * P)
                    last = pe.matmul(k.bank[4 + b % 2][:, c], s3[:, 1, b, c], kb[:, b, c], start=True, stop=True)
                last.then_inc(a_done, 1)
            pe.wait_ge(n_ready, 2 * B)
            pe.wait_ge(aT_ready, B)
            for b in range(B):
                pe.wait_ge(cT_ready, b + 1)
                if b >= 2:
                    pe.wait_ge(m_ready, b - 1)
                for j in range(TPB):
                    c = slice(j * P, (j + 1) * P)
                    last = pe.transpose(k.bank[b % 2][:, c], cT[:, b, c], k.ident[:])
                last.then_inc(x_done, 1)
            for l in range(1, LEVELS):
                def cross(b):
                    pe.wait_ge(cT_ready, l * B + b + 1)
                    pe.wait_ge(m_ready, l * B if l == 1 else (l - 1) * B + b + 1)
                    if (l - 1) * B + b >= 2:
                        pe.wait_ge(x_ready, (l - 1) * B + b - 1)
                    for j in range(TPB):
                        c = slice(j * P, (j + 1) * P)
                        last = pe.matmul(k.bank[b % 2][:, c], cT[:, b, c], m[:, b, c], start=True, stop=True)
                    last.then_inc(x_done, 1)

                def close(b):
                    n = (l - 1) * B + b
                    pe.wait_ge(x_ready, n + 1)
                    pe.wait_ge(mT_ready, B + n if n >= B else B)
                    if n >= 2:
                        pe.wait_ge(mT_ready, B + n - 1)
                    for j in range(TPB):
                        c = slice(j * P, (j + 1) * P)
                        pe.matmul(k.bank[4 + b % 2][:, c], mT[:, b, c], xx[:, b, c], start=True, stop=True)
                    for j in range(TPB):
                        c = slice(j * P, (j + 1) * P)
                        last = pe.matmul(k.bank[6 + b % 2][:, c], xx[:, b, c], mT[:, b, c], start=True, stop=True)
                    last.then_inc(yT_done, 1)

                cross(0)
                for b in range(B):
                    if b + 1 < B:
                        cross(b + 1)
                    close(b)
            pe.wait_ge(x_ready, (LEVELS - 1) * B)
            for b in range(B):
                pe.wait_ge(t_ready, b + 1)
                if b >= 2:
                    pe.wait_ge(w_copied, b - 1)
                    pe.wait_ge(u_copied, b - 1)
                for src, bank in ((kbn, k.bank[b % 2]), (vbn, k.bank[2 + b % 2])):
                    for j in range(TPB):
                        c = slice(j * P, (j + 1) * P)
                        last = pe.matmul(bank[:, c], src[:, b * TPB + j, :], mT[:, b, c], start=True, stop=True)
                last.then_inc(wu_done, 1)
            pe.wait_ge(qk_ready, 1)
            pe.matmul(k.bank[4][:, 0:B * NCH * B], ones[:], qk[:].rearrange("p b n c -> p (b n c)"), start=True, stop=True).then_inc(qk_done, 1)
            pe.wait_ge(o_ready, B)
            for b in range(B):
                pe.wait_ge(osq_ready, b + 1)
                pe.matmul(k.bank[4 + b][:], heads[:], sq[:, b, :], start=True, stop=True).then_inc(on_done, 1)
            for b in range(B):
                pe.wait_ge(on_ready, b + 1)
                for j in range(TPB):
                    c = slice(j * P, (j + 1) * P)
                    last = pe.matmul(k.bank[b][:, c], o[:, b, c], wo[:], start=True, stop=True)
                last.then_inc(out_done, 1)


def build(nc, a, out):
    with ExitStack() as ctx:
        k = Core(nc, ctx)
        x_loaded, made = k.sem("x_loaded"), k.sem("made")
        with nc.Block() as block:
            @block.sync
            def _(sp):
                sp.dma_start(k.x[:], a["L0_attn_a_x"].rearrange("b (j p) d -> p (b j) d", p=P)).then_inc(x_loaded, 16)
                sp.wait_ge(x_loaded, 16)

            @block.gpsimd
            def _(pool):
                link = Link(pool, made)
                link(pool.memset(k.eps[:], LN_EPS))
                pool.memset(k.ident16[:], 0.0)
                link(pool.memset(k.ident[:], 0.0))
                for m in (k.ident, k.ident16):
                    pool.affine_select(out=m[:], in_=m[:], compare_op=ALU.not_equal, fill=1.0,
                                       base=0, pattern=[[-1, P]], channel_multiplier=1)
        l0a = [a[f"L0_attn_a_{n}"] for n in ("w_qkv", "b_qkv", "w_out", "b_out", "w1_rpe", "b1_rpe", "w2_rpe", "b2_rpe")]
        l0f = [a[f"L0_ffn_{n}"] for n in ("gate_w", "w1", "w2")]
        l0b = [a[f"L0_attn_b_{n}"] for n in ("Wq", "Wk", "Wv", "Wo", "bo", "gamma", "beta")]
        l1a = [a[f"L1_attn_a_{n}"] for n in ("w_in", "conv_w", "conv_b", "w_xproj", "w_dt", "b_dt", "A_log", "D", "w_out",
                                             "ln_g", "ln_b")]
        l1b = [a[f"L1_attn_b_{n}"] for n in ("Wq", "Wk", "Wv", "Wb", "conv_q", "conv_k", "conv_v", "g", "Wo")]
        l1f = [a[f"L1_ffn_{n}"] for n in ("gate_weight", "gate_bias", "w_gate", "w_up", "w_down", "shared_w_gate", "shared_w_up",
                                          "shared_w_down", "anchor_w_gate", "anchor_w_up", "anchor_w_down")]
        layers = [("la", layer_attention, l0a), ("lb", layer_moe_experts, l0f), ("lc", layer_linear_attention, l0b),
                  ("ld", layer_moe_experts, l0f), ("le", layer_scan, l1a), ("lf", layer_moe_tokens, l1f),
                  ("lg", layer_delta, l1b), ("lh", layer_moe_tokens, l1f)]
        for n in PHASES:
            tag, layer, args = layers[n]
            k.next_layer()
            layer(k, tag, *args)
        k.next_layer()
        stored = k.sem("stored")
        with nc.Block() as block:
            @block.sync
            def _(sp):
                sp.dma_start(out.rearrange("b (j p) d -> p (b j) d", p=P), k.x[:]).then_inc(stored, 16)
                sp.wait_ge(stored, 16)


_INS = ['L0_attn_a_x', 'L0_attn_a_w_qkv', 'L0_attn_a_b_qkv', 'L0_attn_a_w_out', 'L0_attn_a_b_out', 'L0_attn_a_w1_rpe',
        'L0_attn_a_b1_rpe', 'L0_attn_a_w2_rpe', 'L0_attn_a_b2_rpe', 'L0_attn_b_Wq', 'L0_attn_b_Wk', 'L0_attn_b_Wv',
        'L0_attn_b_Wo', 'L0_attn_b_bo', 'L0_attn_b_gamma', 'L0_attn_b_beta', 'L0_ffn_gate_w', 'L0_ffn_w1', 'L0_ffn_w2',
        'L1_attn_a_w_in', 'L1_attn_a_conv_w', 'L1_attn_a_conv_b', 'L1_attn_a_w_xproj', 'L1_attn_a_w_dt', 'L1_attn_a_b_dt',
        'L1_attn_a_A_log', 'L1_attn_a_D', 'L1_attn_a_w_out', 'L1_attn_a_ln_g', 'L1_attn_a_ln_b', 'L1_attn_b_Wq',
        'L1_attn_b_Wk', 'L1_attn_b_Wv', 'L1_attn_b_Wb', 'L1_attn_b_conv_q', 'L1_attn_b_conv_k', 'L1_attn_b_conv_v',
        'L1_attn_b_g', 'L1_attn_b_Wo', 'L1_ffn_gate_weight', 'L1_ffn_gate_bias', 'L1_ffn_w_gate', 'L1_ffn_w_up',
        'L1_ffn_w_down', 'L1_ffn_shared_w_gate', 'L1_ffn_shared_w_up', 'L1_ffn_shared_w_down', 'L1_ffn_anchor_w_gate',
        'L1_ffn_anchor_w_up', 'L1_ffn_anchor_w_down']


def kernel(**inputs):
    import numpy as _np
    import concourse.bacc as _bacc
    from concourse import mybir as _mybir
    from concourse.bass_utils import run_bass_kernel_spmd as _run

    nc = _bacc.Bacc("TRN2", target_bir_lowering=False, num_devices=1)
    arrays, args = {}, {}
    for name in _INS:
        arr = _np.ascontiguousarray(inputs[name])
        arrays[f"in_{name}_dram"] = arr
        args[name] = nc.dram_tensor(f"in_{name}_dram", arr.shape, _mybir.dt.from_np(arr.dtype), kind="ExternalInput").ap()
    out = nc.dram_tensor("out_0_dram", (4, 512, 128), _mybir.dt.float32, kind="ExternalOutput").ap()
    build(nc, args, out)
    r = _run(nc, [arrays], core_ids=[0])
    return r.results[0]["out_0_dram"]
```

```python
from contextlib import ExitStack

import concourse.bass as bass
from concourse import mybir

F32 = mybir.dt.float32
F32R = mybir.dt.float32r
BF16 = mybir.dt.bfloat16
I32 = mybir.dt.int32
ALU = mybir.AluOpType
ACT = mybir.ActivationFunctionType
AX_X = mybir.AxisListType.X

P = 128
B, T, D = 4, 512, 128
NT = B * T // P
TPB = T // P
LN_EPS = 1e-5
PHASES = [0, 1, 2, 3, 4, 5, 6, 7]


class Core:

    def __init__(self, nc, ctx):
        self.nc, self.ctx = nc, ctx
        self.past, self.own = [], []
        self.x = self.sb("x", [P, NT, D])
        self.xn = self.sb("xn", [P, NT, D])
        self.xnT = self.sb("xnT", [D, B * T])
        self.ident = self.sb("ident", [P, P])
        self.ident16 = self.sb("ident16", [P, P], BF16)
        self.eps = self.sb("eps", [P, 1])
        self.bank = [ctx.enter_context(nc.psum_tensor(f"bank{i}", [P, 512], F32)) for i in range(8)]

    def sb(self, name, shape, dt=F32, ctx=None):
        return (ctx or self.ctx).enter_context(self.nc.sbuf_tensor(name, shape, dt))

    def sem(self, name):
        s = self.nc.alloc_semaphore(name=name)
        self.own.append(s)
        return s

    def next_layer(self):
        self.past, self.own = self.own, []

    def clear_past(self):
        self.nc.clear_and_free_semaphores(self.past)


class Link:

    def __init__(self, eng, sem, waited=None):
        self.eng, self.sem, self.n, self.base, self.waited = eng, sem, 0, 0, waited

    def __call__(self, ins):
        ins.then_inc(self.sem, 1)
        self.n += 1
        self.eng.wait_ge(self.sem, self.base + self.n)
        if self.waited is not None:
            self.eng.sem_inc(self.waited, 1)

    def start(self, i, per):
        self.first, self.n, self.base = self.n, 0, self.n + i * per

    def end(self, per, passes):
        assert self.n == per, (self.n, per)
        self.n, self.base = self.first + per * passes, 0


def bcast(ap, *dims):
    return bass.AP(ap.tensor, ap.offset, [ap.ap[0], *dims])



class Norm:
    def __init__(self, k, tag, ctx):
        self.k = k
        self.stats = k.sb(f"{tag}_stats", [P, NT, 6], ctx=ctx)
        self.mv = k.sb(f"{tag}_mv", [P, NT, 2], ctx=ctx)
        self.vare = k.sb(f"{tag}_vare", [P, NT], ctx=ctx)
        self.std = k.sb(f"{tag}_std", [P, NT], ctx=ctx)
        self.rstd = k.sb(f"{tag}_rstd", [P, NT], ctx=ctx)
        self.var_ready = k.sem(f"{tag}_var_ready")
        self.std_ready = k.sem(f"{tag}_std_ready")
        self.xn_ready = k.sem(f"{tag}_xn_ready")
        self.turned = k.sem(f"{tag}_turned")
        self.xnT_ready = k.sem(f"{tag}_xnT_ready")

    def statistics(self, dve, link, src):
        for j in range(NT):
            last = dve.bn_stats(self.stats[:, j, :], src[:, j, :])
        link(last)
        for j in range(NT):
            last = dve.bn_aggr(self.mv[:, j, :], self.stats[:, j, :])
        link(last)
        dve.tensor_scalar(self.vare[:], self.mv[:, :, 1], LN_EPS, None, ALU.add).then_inc(self.var_ready, 1)

    def scalar_sqrt(self, act, n=1):
        act.wait_ge(self.var_ready, n)
        act.activation(self.std[:], self.vare[:], ACT.Sqrt).then_inc(self.std_ready, 1)

    def vector(self, dve, link):
        k = self.k
        self.statistics(dve, link, k.x)
        self.normalise(dve, link)

    def normalise(self, dve, link):
        k = self.k
        dve.wait_ge(self.std_ready, 1)
        link(dve.reciprocal(self.rstd[:], self.std[:]))
        for j in range(NT):
            dve.tensor_scalar(k.xn[:, j, :], k.x[:, j, :], self.mv[:, j, 0:1], self.rstd[:, j:j + 1],
                              ALU.subtract, ALU.mult).then_inc(self.xn_ready, 1)

    def tensor(self, pe, src=None, ready=None):
        k = self.k
        src = k.xn if src is None else src
        ready = self.xn_ready if ready is None else ready
        for g in range(B):
            pe.wait_ge(ready, 4 * (g + 1))
            for j in range(4):
                last = pe.transpose(k.bank[g][:, j * P:(j + 1) * P], src[:, 4 * g + j, :], k.ident[:])
            last.then_inc(self.turned, 1)

    def scalar_copy(self, act):
        k = self.k
        for g in range(B):
            act.wait_ge(self.turned, g + 1)
            act.activation(k.xnT[:, g * T:(g + 1) * T], k.bank[g][:], ACT.Copy).then_inc(self.xnT_ready, 1)



def layer_attention(k, tag, w_qkv, b_qkv, w_out, b_out, w1_rpe, b1_rpe, w2_rpe, b2_rpe):
    nc = k.nc
    HID, H = w2_rpe.shape
    HD = D // H
    HP = H // 2
    PARTS = 8
    SCALE = float(HD) ** -0.5
    SPAN = 2 * T
    WIDE = 2 * T - P
    U = H * TPB
    GH = 4
    NG = H // GH
    VW = 32
    NN, NR, NV = 4, 4, 12
    TURN, COPY = 2, 3
    MIX = COPY + TPB
    GROUP = GH * TPB
    LEAVE, BACK, SCALE_O = MIX + GROUP, MIX + GROUP + 1, MIX + GROUP + 3
    PRODUCTS = [(0, 0), (0, 1), (1, 0), (1, 1), (0, 2), (2, 0)]
    with ExitStack() as ctx:
        def sb(name, shape, dt=F32):
            return k.sb(f"{tag}_{name}", shape, dt, ctx)

        def sem(name):
            return k.sem(f"{tag}_{name}")

        norm = Norm(k, tag, ctx)
        wqkv = sb("wqkv", [D, 3 * D])
        wout = sb("wout", [D, D])
        bqkv = sb("bqkv", [P, 3 * D])
        bout = sb("bout", [P, D])
        w1c = sb("w1c", [HID, 1])
        b1c = sb("b1c", [HID, 1])
        w2 = sb("w2", [HID, H])
        b2c = sb("b2c", [H, 1])
        rel = sb("rel", [HID, SPAN])
        mag = sb("mag", [HID, SPAN])
        curve = rel[0:H]
        bias = sb("bias", [P, H, WIDE])
        scratch = nc.dram_tensor(f"{tag}_scratch", [H, SPAN], F32)
        qk = sb("qk", [P, NT, 2, D])
        v = k.xn
        v1 = sb("v1", [P, TPB, H, VW])
        rest = sb("rest", [P, 2, TPB, D])
        part = sb("part", [P, 2, 3, TPB, D], BF16)
        stack = sb("stack", [P, 2, TPB, H, PARTS, HD], BF16)
        qkT = sb("qkT", [P, HP, 2, T], BF16)
        neg = sb("neg", [P, NN, T])
        nmax = sb("nmax", [P, NN, 1])
        prob = sb("prob", [P, NR, T])
        side = prob[0:HID, 0:2, :].rearrange("p a t -> p (a t)")
        probT = sb("probT", [P, NV, T])
        mixT = sb("mixT", [P, 2, GH, P])
        rsum = sb("rsum", [P, GH, TPB])
        o, oT = k.xn, k.xnT

        loaded_w, loaded_r, loaded_bias = sem("loaded_w"), sem("loaded_r"), sem("loaded_bias")
        waited, order, pool_order, act_order = sem("waited"), sem("order"), sem("pool_order"), sem("act_order")
        rel_ready, curve_turned, curve_ready, curve_stored = sem("rel_ready"), sem("curve_turned"), sem("curve_ready"), sem("curve_stored")
        side_ready, logd = sem("side_ready"), sem("logd")
        qkv_done, qkv_ready = sem("qkv_done"), sem("qkv_ready")
        parts_made = sem("parts_made")
        stacked, parts_turned, parts_ready = sem("stacked"), sem("parts_turned"), sem("parts_ready")
        scored, biased, exped, prob_turned = sem("scored"), sem("biased"), sem("exped"), sem("prob_turned")
        probT_ready = [sem("probT_by_act"), sem("probT_by_dve")]
        mixed, mixT_ready, mix_back, o_ready, v1_ready = sem("mixed"), sem("mixT_ready"), sem("mix_back"), sem("o_ready"), sem("v1_ready")
        o_turned, oT_ready, projected, added, x_ready = sem("o_turned"), sem("oT_ready"), sem("projected"), sem("added"), sem("x_ready")

        block = ctx.enter_context(nc.Block())

        @block.sync
        def _(sp):
            sp.dma_start(w1c[:], w1_rpe.rearrange("a h -> h a"), allow_slow_non_contiguous=True).then_inc(loaded_r, 16)
            sp.dma_start(b1c[:], b1_rpe.rearrange("(h a) -> h a", a=1)).then_inc(loaded_r, 16)
            sp.dma_start(w2[:], w2_rpe).then_inc(loaded_r, 16)
            sp.dma_start(b2c[:], b2_rpe.rearrange("(h a) -> h a", a=1)).then_inc(loaded_r, 16)
            sp.dma_start(wqkv[:], w_qkv).then_inc(loaded_w, 16)
            sp.dma_start(bqkv[:], b_qkv.partition_broadcast(P)).then_inc(loaded_w, 16)
            sp.dma_start(wout[:], w_out).then_inc(loaded_w, 16)
            sp.dma_start(bout[:], b_out.partition_broadcast(P)).then_inc(loaded_w, 16)
            sp.wait_ge(curve_ready, 2)
            sp.dma_start(scratch[:, :], curve).then_inc(curve_stored, 16)
            sp.wait_ge(curve_stored, 16)
            for h in range(0, H, 4):
                src = bass.AP(scratch, h * SPAN, [[1, P], [SPAN, 4], [1, WIDE]])
                sp.dma_start(bias[:, h:h + 4, :], src).then_inc(loaded_bias, 16)
                sp.wait_ge(loaded_bias, 4 * h + 16)

        @block.gpsimd
        def _(pool):
            k.clear_past()
            link = Link(pool, pool_order, waited)
            pool.iota(rel[:], [[1, SPAN]], base=1 - T, channel_multiplier=0, allow_small_or_imprecise_dtypes=True).then_inc(rel_ready, 1)
            link(pool.memset(stack[:], 0.0))
            link(pool.memset(v1[:], 0.0))
            link(pool.memset(v1[:, :, :, HD:HD + 1], 1.0))
            pool.wait_ge(loaded_w, 64)
            pool.wait_ge(norm.xn_ready, NT)
            pool.tensor_tensor(k.x[:], k.x[:], bcast(bout[:, 0:1], (0, NT), (1, D)), ALU.add).then_inc(x_ready, 1)
            pool.wait_ge(qkv_ready, NT)
            pool.tensor_copy(v1[:, :, :, 0:HD], v[:, 0:TPB, :].rearrange("p j (h d) -> p j h d", d=HD)).then_inc(v1_ready, 1)
            pool.wait_ge(stacked, 2)
            with pool.Fori(0, B - 1) as b:
                link.start(b, 2 * (2 * 3) + 1)
                for s in range(2):
                    whole, left = rest[:, 0, :, :], rest[:, 1, :, :]
                    link(pool.tensor_copy(whole, qk[:, bass.ds(b * TPB + TPB, TPB), s, :]))
                    for i in range(3):
                        link(pool.tensor_copy(part[:, s, i, :, :], whole if i == 0 else left))
                        if i < 2:
                            link(pool.tensor_tensor(left, whole if i == 0 else left, part[:, s, i, :, :], ALU.subtract))
                pool.wait_ge(parts_turned, b * HP + HP)
                pool.sem_inc(waited, 1)
                for s in range(2):
                    for r, pair in enumerate(PRODUCTS):
                        last = pool.tensor_copy(stack[:, s, :, :, r, :], part[:, s, pair[s], :, :].rearrange("p j (h d) -> p j h d", d=HD))
                    last.then_inc(stacked, 1)
                pool.wait_ge(mixed, b * H + H + NV // TPB)
                pool.sem_inc(waited, 1)
                link(pool.tensor_copy(v1[:, :, :, 0:HD], v[:, bass.ds(b * TPB + TPB, TPB), :].rearrange("p j (h d) -> p j h d", d=HD)))
                pool.sem_inc(v1_ready, 1)
                link.end(2 * (2 * 3) + 1, B - 1)

        @block.scalar
        def _(act):
            link = Link(act, act_order)
            norm.scalar_sqrt(act)
            act.wait_ge(side_ready, 1)
            act.activation(mag[:], mag[:], ACT.Ln, bias=1.0).then_inc(logd, 1)
            act.wait_ge(side_ready, 2)
            act.wait_ge(loaded_r, 64)
            link(act.activation(mag[:], mag[:], ACT.Relu, bias=b1c[:, 0:1], scale=w1c[:, 0:1]))
            norm.scalar_copy(act)
            for i in range(2):
                act.wait_ge(curve_turned, i + 1)
                act.activation(curve[:, i * T:(i + 1) * T], k.bank[4 + i][0:H, :], ACT.Identity, bias=b2c[:, 0:1]).then_inc(curve_ready, 1)
            act.wait_ge(pool_order, 1)
            for s in range(2):
                act.wait_ge(parts_made, s + 1)
                for r, pair in enumerate(PRODUCTS):
                    last = act.activation(stack[:, s, :, :, r, :], part[:, s, pair[s], :, :].rearrange("p j (h d) -> p j h d", d=HD), ACT.Copy)
                last.then_inc(stacked, 1)
            with act.Fori(0, B) as b:
                def copy_parts(hp):
                    act.wait_ge(parts_turned, b * HP + hp + 1)
                    if hp == 0:
                        act.wait_ge(scored, b * U + 1)
                    act.activation(qkT[:, hp, :, :].rearrange("p s t -> p (s t)"), k.bank[6][:].bitcast(BF16), ACT.Copy).then_inc(parts_ready, 1)

                copy_parts(0)
                for step in range(U - GROUP + LEAVE + 1):
                    if step % TPB == 2 and step // TPB + 1 < HP:
                        copy_parts(step // TPB + 1)
                    u = step - COPY
                    if 0 <= u < U and u % 2 == 0:
                        act.wait_ge(prob_turned, b * U + u + 1 + NR)
                        act.wait_ge(mixed, b * H + u // TPB + 1)
                        act.activation(probT[:, u % NV, :], k.bank[2 + u % 2][:], ACT.Copy).then_inc(probT_ready[0], 1)
                    if step < U:
                        u = step
                        act.wait_ge(biased, b * U + u + 3)
                        act.wait_ge(prob_turned, b * U + u + 1)
                        act.activation(prob[:, u % NR, :], neg[:, u % NN, :], ACT.Exp, bias=nmax[:, u % NN, :], scale=-1.0).then_inc(exped, 1)
                    g = (step - LEAVE) // GROUP
                    if step >= LEAVE and (step - LEAVE) % GROUP == 0:
                        act.wait_ge(mixed, b * H + (g + 1) * GH + NV // TPB)
                        act.wait_ge(mix_back, b * NG + g + 1)
                        act.activation(mixT[:, g % 2, :, :].rearrange("p h t -> p (h t)"), k.bank[4 + g % 2][:], ACT.Copy).then_inc(mixT_ready, 1)
            for g in range(B):
                act.wait_ge(o_turned, g + 1)
                act.activation(oT[:, g * T:(g + 1) * T], k.bank[g][:], ACT.Copy).then_inc(oT_ready, 1)

        @block.vector
        def _(dve):
            link = Link(dve, order)
            for s, n in ((biased, 2), (exped, NN), (prob_turned, NR), (mixed, NV // TPB), (probT_ready[0], 1), (probT_ready[1], 1),
                         (mixT_ready, 2), (mix_back, 2), (o_ready, 1), (parts_ready, 1), (scored, 1)):
                dve.sem_inc(s, n)
            norm.statistics(dve, link, k.x)
            dve.wait_ge(rel_ready, 1)
            dve.scalar_tensor_tensor(mag[:], rel[:], -1.0, rel[:], ALU.mult, ALU.max).then_inc(side_ready, 1)
            link(dve.tensor_scalar(side, rel[:], 0.0, 2.0, ALU.is_ge, ALU.mult))
            link(dve.tensor_scalar(side, side, -1.0, None, ALU.add))
            dve.wait_ge(logd, 1)
            dve.tensor_tensor(mag[:], mag[:], side, ALU.mult).then_inc(side_ready, 1)
            norm.normalise(dve, link)

            def split_first_batch():
                dve.wait_ge(qkv_ready, TPB)
                for s in range(2):
                    left = rest[:, s, :, :]
                    for i in range(3):
                        src = qk[:, 0:TPB, s, :] if i == 0 else left
                        last = dve.tensor_copy(part[:, s, i, :, :], src)
                        if i < 2:
                            link(last)
                            link(dve.tensor_tensor(left, src, part[:, s, i, :, :], ALU.subtract))
                    last.then_inc(parts_made, 1)

            dve.wait_ge(loaded_w, 64)
            dve.wait_ge(norm.turned, B)
            for t in range(NT):
                dve.wait_ge(qkv_done, t + 1)
                ps = k.bank[4 + t % 4]
                dve.tensor_tensor(v[:, t, :], ps[:, 2 * D:3 * D], bqkv[:, 2 * D:3 * D], ALU.add)
                if t == 0:
                    link(dve.tensor_scalar(bqkv[:, 0:D], bqkv[:, 0:D], SCALE, None, ALU.mult))
                dve.scalar_tensor_tensor(qk[:, t, 0, :], ps[:, 0:D], SCALE, bqkv[:, 0:D], ALU.mult, ALU.add)
                dve.tensor_tensor(qk[:, t, 1, :], ps[:, D:2 * D], bqkv[:, D:2 * D], ALU.add).then_inc(qkv_ready, 1)
                if t == TPB - 1:
                    split_first_batch()
            with dve.Fori(0, B) as b:
                link.start(b, NG)
                for step in range(U - GROUP + SCALE_O + 1):
                    u = step - COPY
                    if 0 <= u < U and u % 2 == 1:
                        dve.wait_ge(prob_turned, b * U + u + 1 + NR)
                        dve.wait_ge(mixed, b * H + u // TPB + 1)
                        dve.tensor_copy(probT[:, u % NV, :], k.bank[2 + u % 2][:]).then_inc(probT_ready[1], 1)
                    if step < U:
                        u = step
                        h, j = u // TPB, u % TPB
                        if j == 0 and h % 4 == 0:
                            dve.wait_ge(loaded_bias, 4 * h + 16)
                        dve.wait_ge(scored, b * U + u + 2)
                        dve.wait_ge(exped, b * U + u + 1)
                        dve.sem_inc(waited, 1)
                        key0 = bias[:, h, T - 1 + j * P:T + j * P]
                        keys_back = bcast(key0, (-1, T))
                        dve.tensor_tensor_reduce(out=neg[:, u % NN, :], in0=k.bank[u % 2][:], in1=keys_back,
                                                 scale=-1.0, scalar=3e38, op0=ALU.add, op1=ALU.min, accum_out=nmax[:, u % NN, :]).then_inc(biased, 1)
                    if step >= SCALE_O and (step - SCALE_O) % GROUP == 0:
                        g = (step - SCALE_O) // GROUP
                        dve.wait_ge(mix_back, b * NG + g + 3)
                        dve.sem_inc(waited, 1)
                        ov = k.bank[7][:].rearrange("p (h j d) -> p h j d", j=TPB, d=VW)
                        link(dve.reciprocal(rsum[:], ov[:, :, :, HD]))
                        dst = o[:, bass.ds(b * TPB, TPB), g * GH * HD:(g + 1) * GH * HD].rearrange("p j (h d) -> p h j d", d=HD)
                        dve.tensor_tensor(dst, ov[:, :, :, 0:HD], rsum[:].unsqueeze(3).to_broadcast([P, GH, TPB, HD]), ALU.mult).then_inc(o_ready, 1)
                link.end(NG, B)
            dve.wait_ge(x_ready, 1)
            for g in range(B):
                dve.wait_ge(projected, g + 1)
                xb = k.x[:, g * TPB:(g + 1) * TPB, :].rearrange("p j d -> p (j d)")
                dve.tensor_tensor(xb, xb, k.bank[4 + g][:], ALU.add).then_inc(added, 1)

        @block.tensor
        def _(pe):
            pe.wait_ge(act_order, 1)
            for i in range(2):
                pe.matmul(k.bank[4 + i][0:H, :], w2[:], mag[:, i * T:(i + 1) * T], start=True, stop=True).then_inc(curve_turned, 1)
            norm.tensor(pe)
            pe.wait_ge(loaded_w, 64)
            pe.wait_ge(curve_ready, 2)
            for t in range(NT):
                pe.wait_ge(norm.xnT_ready, t // TPB + 1)
                if t >= 4:
                    pe.wait_ge(qkv_ready, t - 3)
                pe.matmul(k.bank[4 + t % 4][:, 0:3 * D], k.xnT[:, t * P:(t + 1) * P], wqkv[:], start=True, stop=True).then_inc(qkv_done, 1)
            pe.wait_ge(qkv_ready, NT)
            with pe.Fori(0, B) as b:
                def turn_parts(hp):
                    pe.wait_ge(parts_ready, b * HP + hp + 1)
                    bank = k.bank[6][:].bitcast(BF16)
                    for s in range(2):
                        for j in range(TPB):
                            last = pe.transpose(bank[:, s * T + j * P:s * T + (j + 1) * P],
                                                stack[:, s, j, 2 * hp:2 * hp + 2, :, :].rearrange("p h r d -> p (h r d)"), k.ident16[:])
                    last.then_inc(parts_turned, 1)

                pe.wait_ge(stacked, b * 2 + 2)
                turn_parts(0)
                for step in range(U - GROUP + BACK + 1):
                    if step % TPB == 1 and step // TPB + 1 < HP:
                        turn_parts(step // TPB + 1)
                    if step < U:
                        u = step
                        h, j = u // TPB, u % TPB
                        if j == 0:
                            pe.wait_ge(parts_ready, b * HP + h // 2 + 2)
                        pe.wait_ge(biased, b * U + u + 1)
                        r = slice(64 * (h % 2), 64 * (h % 2) + 64)
                        pe.matmul(k.bank[u % 2][:], qkT[r, h // 2, 0, j * P:(j + 1) * P], qkT[r, h // 2, 1, :], start=True, stop=True).then_inc(scored, 1)
                    u = step - MIX
                    if 0 <= u < U:
                        h, c = u // TPB, u % TPB
                        g = h // GH
                        if c == 0:
                            if h == 0:
                                pe.wait_ge(v1_ready, b + 1)
                            if h % GH == 0:
                                pe.wait_ge(mixT_ready, b * NG + g + 1)
                            for ready in probT_ready:
                                pe.wait_ge(ready, b * (U // 2) + 2 * h + 3)
                        for j in range(TPB):
                            last = pe.matmul(k.bank[4 + g % 2][VW * j:VW * (j + 1), (h % GH) * P:(h % GH + 1) * P], v1[:, c, h, :],
                                             probT[:, (h * TPB + j) % NV, c * P:(c + 1) * P], start=(c == 0), stop=(c == TPB - 1),
                                             tile_position=(0, VW * j))
                        if c == TPB - 1:
                            last.then_inc(mixed, 1)
                    u = step - TURN
                    if 0 <= u < U:
                        pe.wait_ge(exped, b * U + u + 1 + NN)
                        pe.wait_ge(probT_ready[u % 2], b * (U // 2) + u // 2 + 1)
                        for c in range(TPB):
                            last = pe.transpose(k.bank[2 + u % 2][:, c * P:(c + 1) * P], prob[:, u % NR, c * P:(c + 1) * P], k.ident[:])
                        last.then_inc(prob_turned, 1)
                    if step >= BACK and (step - BACK) % GROUP == 0:
                        g = (step - BACK) // GROUP
                        pe.wait_ge(mixT_ready, b * NG + g + 3)
                        pe.wait_ge(o_ready, b * NG + g + 1)
                        for i in range(GH):
                            last = pe.transpose(k.bank[7][:, i * P:(i + 1) * P], mixT[:, g % 2, i, :], k.ident[:])
                        last.then_inc(mix_back, 1)
            pe.wait_ge(o_ready, NG * B + 1)
            for g in range(B):
                for j in range(TPB):
                    last = pe.transpose(k.bank[g][:, j * P:(j + 1) * P], o[:, g * TPB + j, :], k.ident[:])
                last.then_inc(o_turned, 1)
            for g in range(B):
                pe.wait_ge(oT_ready, g + 1)
                for j in range(TPB):
                    last = pe.matmul(k.bank[4 + g][:, j * D:(j + 1) * D], oT[:, (g * TPB + j) * P:(g * TPB + j + 1) * P], wout[:], start=True, stop=True)
                last.then_inc(projected, 1)



def layer_moe_experts(k, tag, gate_w, w1, w2):
    nc = k.nc
    E, F = w1.shape[0], w1.shape[2]
    CAP = int(2.0 * T / E)
    FT = F // P
    OUT_BANKS = (6, 7, 3, 4)
    R = B * E
    assert CAP == P and CAP % 8 == 0 and E % 2 == 0 and FT == B
    with ExitStack() as ctx:
        def sb(name, shape, dt=F32):
            return k.sb(f"{tag}_{name}", shape, dt, ctx)

        def sem(name):
            return k.sem(f"{tag}_{name}")

        norm = Norm(k, tag, ctx)
        gw = sb("gw", [E, D])
        gwT = sb("gwT", [D, E])
        w1s = sb("w1s", [D, 2, F])
        w2s = sb("w2s", [P, 2, FT, D])
        lmax = sb("lmax", [P, NT])
        table = sb("table", [P, 1])
        probs = sb("probs", [P, NT, E])
        psum_e = sb("psum_e", [P, NT])
        prec = sb("prec", [P, NT])
        rows = sb("rows", [R, 2, T])
        best = sb("best", [R, 8])
        ones = sb("ones", [R, T])
        chosen = sb("chosen", [R, T])
        count = sb("count", [R, T])
        slot = sb("slot", [R, T])
        slots = sb("slots", [P, E, NT])
        gates = sb("gates", [P, E, NT])
        number = sb("number", [P, P])
        xpart = sb("xpart", [P, 3, NT, D], BF16)
        left = sb("left", [P, NT, D])
        pick = sb("pick", [P, 2, NT, P], BF16)
        own = sb("own", [P, 2, NT])
        place = sb("place", [P, B, T])
        xin = sb("xin", [D, T])
        hid = sb("hid", [P, FT, T])
        gate = sb("gate", [P, NT])
        y = sb("y", [P, B, D])

        loaded_gw = sem("loaded_gw")
        loaded_w = [sem("loaded_w0"), sem("loaded_w1")]
        order, pool_order, number_made = sem("order"), sem("pool_order"), sem("number_made")
        gwT_turned, gwT_ready, logits_ready = sem("gwT_turned"), sem("gwT_ready"), sem("logits_ready")
        shifted, exped, probs_ready = sem("shifted"), sem("exped"), sem("probs_ready")
        rows_turned, slot_ready, slot_turned, slots_ready = sem("rows_turned"), sem("slot_ready"), sem("slot_turned"), sem("slots_ready")
        part_made, part_taken = sem("part_made"), sem("part_taken")
        own_ready, own_seen, pick_ready, pick_used = sem("own_ready"), sem("own_seen"), sem("pick_ready"), sem("pick_used")
        xin_ready, xin_copied, h_ready, gelu_done = sem("xin_ready"), sem("xin_copied"), sem("h_ready"), sem("gelu_done")
        turned, place_ready, gate_ready = sem("pturned"), sem("place_ready"), sem("gate_ready")
        y_done, y_ready, out_ready, out_added, w_used = sem("y_done"), sem("y_ready"), sem("out_ready"), sem("out_added"), sem("w_used")

        block = ctx.enter_context(nc.Block())

        @block.sync
        def _(sp):
            sp.dma_start(gw[:], gate_w).then_inc(loaded_gw, 16)
            sp.sem_inc(w_used, 2)
            with sp.Fori(0, E // 2) as i:
                for s in range(2):
                    sp.wait_ge(w_used, i * 2 + s + 1)
                    sp.dma_start(w1s[:, s, :], w1[bass.ds(i * 2 + s, 1), :, :].rearrange("e d f -> d (e f)")).then_inc(loaded_w[s], 16)
                    sp.dma_start(w2s[:, s, :, :], w2[bass.ds(i * 2 + s, 1), :, :].rearrange("e (t p) d -> p (e t) d", p=P))\
                        .then_inc(loaded_w[s], 16)

        @block.gpsimd
        def _(pool):
            k.clear_past()
            pool.iota(number[:], [[1, P]], base=0, channel_multiplier=0, allow_small_or_imprecise_dtypes=True).then_inc(number_made, 1)
            pool.memset(ones[:], 1.0).then_inc(number_made, 1)
            pool.wait_ge(number_made, 2)
            pool.sem_inc(pick_used, 2)
            for i in range(2):
                pool.wait_ge(part_made, i + 1)
                pool.tensor_tensor(left[:], k.xn[:] if i == 0 else left[:], xpart[:, i, :, :], ALU.subtract).then_inc(part_taken, 1)
            pool.wait_ge(slots_ready, 1)
            with pool.Fori(0, E // 2) as i:
                for s in range(2):
                    pool.wait_ge(pick_used, i * 2 + s + 1)
                    pool.tensor_copy(own[:, s, :], slots[:, bass.ds(i * 2 + s, 1), :].rearrange("p e j -> p (e j)")).then_inc(own_ready, 1)
                    pool.wait_ge(own_ready, i * 2 + s + 1)
                    pool.sem_inc(own_seen, 1)
                    for n in range(B):
                        for j in range(n * TPB, (n + 1) * TPB):
                            last = pool.tensor_scalar(pick[:, s, j, :], number[:], own[:, s, j:j + 1], None, ALU.is_equal)
                        last.then_inc(pick_ready, 1)

        @block.scalar
        def _(act):
            norm.scalar_sqrt(act)
            norm.scalar_copy(act)
            act.wait_ge(norm.xn_ready, NT)
            act.activation(xpart[:, 0, :, :], k.xn[:], ACT.Copy).then_inc(part_made, 1)
            act.wait_ge(shifted, 1)
            act.activation(probs[:], probs[:], ACT.Exp).then_inc(exped, 1)
            for i in range(2):
                act.wait_ge(part_taken, i + 1)
                act.activation(xpart[:, i + 1, :, :], left[:], ACT.Copy).then_inc(part_made, 1)
            act.activation(table[:], k.eps[:], ACT.Gelu)
            with act.Fori(0, E // 2) as i:
                for s in range(2):
                    e = i * 2 + s
                    act.wait_ge(xin_ready, e + 1)
                    act.wait_ge(h_ready, e * FT + 1)
                    act.activation(xin[:], k.bank[0][:], ACT.Copy).then_inc(xin_copied, 1)
                    for f in range(FT):
                        act.wait_ge(h_ready, e * FT + f + 2)
                        if f == 0:
                            act.wait_ge(y_done, e + 1)
                        act.activation(hid[:, f, :], k.bank[1 + f % 2][:], ACT.Gelu).then_inc(gelu_done, 1)

        @block.vector
        def _(dve):
            link = Link(dve, order)
            dve.sem_inc(gelu_done, 2)
            dve.sem_inc(out_added, B)
            dve.sem_inc(h_ready, 1)
            dve.sem_inc(y_done, 1)
            dve.sem_inc(y_ready, 1)
            dve.sem_inc(place_ready, 2)
            norm.vector(dve, link)
            dve.wait_ge(gwT_turned, 1)
            dve.tensor_copy(gwT[:], k.bank[4][:, 0:E]).then_inc(gwT_ready, 1)
            dve.wait_ge(logits_ready, 1)
            logits = k.bank[5][:, 0:NT * E].rearrange("p (j e) -> p j e", e=E)
            link(dve.tensor_reduce(lmax[:], logits, AX_X, ALU.max))
            dve.tensor_tensor(probs[:], logits, bcast(lmax[:, 0:1], (1, NT), (0, E)), ALU.subtract).then_inc(shifted, 1)
            dve.wait_ge(exped, 1)
            link(dve.tensor_reduce(psum_e[:], probs[:], AX_X, ALU.add))
            link(dve.reciprocal(prec[:], psum_e[:]))
            link(dve.tensor_tensor(probs[:], probs[:], bcast(prec[:, 0:1], (1, NT), (0, E)), ALU.mult))
            dve.tensor_copy(gates[:].rearrange("p e (n j) -> p j n e", j=TPB), probs[:].rearrange("p (j n) e -> p j n e", j=TPB))\
                .then_inc(probs_ready, 1)
            dve.wait_ge(rows_turned, 1)
            link(dve.tensor_copy(rows[:, 0, :], k.bank[6][0:R, :]))
            for r in range(CAP // 8):
                link(dve.max(best[:], rows[:, r % 2, :]))
                link(dve.match_replace(rows[:, 1 - r % 2, :], best[:], rows[:, r % 2, :], -1.0))
            link(dve.tensor_scalar(chosen[:], rows[:, (CAP // 8) % 2, :], 0.0, None, ALU.is_lt))
            dve.wait_ge(number_made, 2)
            link(dve.tensor_tensor_scan(count[:], ones[:], chosen[:], 0.0, ALU.mult, ALU.add))
            link(dve.tensor_tensor(slot[:], count[:], chosen[:], ALU.mult))
            dve.tensor_scalar(slot[:], slot[:], -1.0, None, ALU.add).then_inc(slot_ready, 1)
            dve.wait_ge(slot_turned, 1)
            dve.tensor_copy(slots[:].rearrange("p e (n j) -> p j n e", j=TPB),
                            k.bank[7][:, 0:TPB * R].rearrange("p (j n e) -> p j n e", j=TPB, n=B)).then_inc(slots_ready, 1)
            with dve.Fori(0, E // 2) as i:
                for s in range(2):
                    e = i * 2 + s
                    dve.tensor_copy(gate[:], gates[:, bass.ds(e, 1), :].rearrange("p e j -> p (e j)")).then_inc(gate_ready, 1)
                    for n in range(B):
                        dve.wait_ge(turned, e * B + n + 1)
                        dve.tensor_copy(place[:, n, :], k.bank[3 + n % 2][:].bitcast(BF16)[:, 0:T]).then_inc(place_ready, 1)
                    dve.wait_ge(y_done, e + 2)
                    dve.tensor_copy(y[:], k.bank[5][:].rearrange("p (n d) -> p n d", d=D)).then_inc(y_ready, 1)
                    dve.wait_ge(gate_ready, e + 1)
                    for n in range(B):
                        dve.wait_ge(out_ready, e * B + n + 1)
                        for j in range(TPB):
                            t = n * TPB + j
                            last = dve.scalar_tensor_tensor(k.x[:, t, :], k.bank[OUT_BANKS[n]][:, j * D:(j + 1) * D], gate[:, t:t + 1],
                                                            k.x[:, t, :], ALU.mult, ALU.add)
                        last.then_inc(out_added, 1)
                    dve.wait_ge(out_added, e * B + B + B)

        @block.tensor
        def _(pe):
            norm.tensor(pe)
            pe.wait_ge(loaded_gw, 16)
            pe.transpose(k.bank[4][:, 0:E], gw[:], k.ident[0:E, 0:E]).then_inc(gwT_turned, 1)
            pe.wait_ge(gwT_ready, 1)
            pe.wait_ge(norm.xnT_ready, B)
            for j in range(TPB):
                for n in range(B):
                    o = (j * B + n) * E
                    t = n * TPB + j
                    last = pe.matmul(k.bank[5][:, o:o + E], k.xnT[:, t * P:(t + 1) * P], gwT[:], start=True, stop=True)
            last.then_inc(logits_ready, 1)
            pe.wait_ge(probs_ready, 1)
            for j in range(TPB):
                last = pe.transpose(k.bank[6][0:R, j * P:(j + 1) * P], probs[:, j * B:(j + 1) * B, :].rearrange("p n e -> p (n e)"), k.ident[:])
            last.then_inc(rows_turned, 1)
            pe.wait_ge(slot_ready, 1)
            for j in range(TPB):
                last = pe.transpose(k.bank[7][:, j * R:(j + 1) * R], slot[:, j * P:(j + 1) * P], k.ident[0:R, 0:R])
            last.then_inc(slot_turned, 1)
            pe.wait_ge(slots_ready, 1)

            def gather(e, s, n):
                pe.wait_ge(pick_ready, e * B + n + 1)
                for j in range(TPB):
                    t = n * TPB + j
                    for i in range(3):
                        last = pe.matmul(k.bank[0][:, n * CAP:(n + 1) * CAP], xpart[:, i, t, :], pick[:, s, t, :],
                                         start=(j == 0 and i == 0), stop=(j == TPB - 1 and i == 2))
                if n == B - 1:
                    last.then_inc(xin_ready, 1)

            def turn(e, s, n):
                pe.wait_ge(place_ready, e * B + n + 1)
                if n < 2:
                    pe.wait_ge(out_added, e * B + n + 3)
                for j in range(TPB):
                    last = pe.transpose(k.bank[3 + n % 2][:].bitcast(BF16)[:, j * P:(j + 1) * P], pick[:, s, n * TPB + j, :], k.ident16[:])
                last.then_inc(turned, 1)

            def expert(i, s, more):
                e = i * 2 + s
                pe.wait_ge(xin_copied, e + 1)
                pe.wait_ge(loaded_w[s], i * 32 + 32)
                for f in range(FT):
                    pe.wait_ge(gelu_done, e * FT + f + 1)
                    pe.matmul(k.bank[1 + f % 2][:], w1s[:, s, f * P:(f + 1) * P], xin[:], start=True, stop=True).then_inc(h_ready, 1)
                    turn(e, s, f)
                if more:
                    gather(e + 1, 1 - s, 0)
                    gather(e + 1, 1 - s, 1)
                pe.wait_ge(turned, e * B + B)
                pe.sem_inc(pick_used, 1)
                pe.wait_ge(gelu_done, e * FT + FT + 2)
                pe.wait_ge(y_ready, e + 1)
                for n in range(B):
                    for f in range(FT):
                        last = pe.matmul(k.bank[5][:, n * D:(n + 1) * D], hid[:, f, n * CAP:(n + 1) * CAP], w2s[:, s, f, :],
                                         start=(f == 0), stop=(f == FT - 1))
                last.then_inc(y_done, 1)
                if more:
                    gather(e + 1, 1 - s, 2)
                    gather(e + 1, 1 - s, 3)
                pe.wait_ge(y_done, e + 2)
                pe.sem_inc(w_used, 1)
                pe.wait_ge(y_ready, e + 2)
                pe.wait_ge(place_ready, e * B + B + 2)
                for n in range(B):
                    if n < 2:
                        pe.wait_ge(out_added, e * B + n + 1)
                    for j in range(TPB):
                        last = pe.matmul(k.bank[OUT_BANKS[n]][:, j * D:(j + 1) * D], place[:, n, j * P:(j + 1) * P], y[:, n, :],
                                         start=True, stop=True)
                    last.then_inc(out_ready, 1)

            pe.wait_ge(part_made, 3)
            for n in range(B):
                gather(0, 0, n)
            with pe.Fori(0, E // 2 - 1) as i:
                expert(i, 0, True)
                expert(i, 1, True)
            expert(E // 2 - 1, 0, True)
            expert(E // 2 - 1, 1, False)



def layer_linear_attention(k, tag, Wq, Wk, Wv, Wo, bo, gamma, beta):
    nc = k.nc
    with ExitStack() as ctx:
        def sb(name, shape, dt=F32):
            return k.sb(f"{tag}_{name}", shape, dt, ctx)

        def sem(name):
            return k.sem(f"{tag}_{name}")

        norm = Norm(k, tag, ctx)
        norm2 = Norm(k, f"{tag}2", ctx)
        wqv = sb("wqv", [D, 2 * D])
        wk = sb("wk", [D, D])
        wo = sb("wo", [D, D])
        bov = sb("bov", [P, D])
        gam = sb("gam", [P, D])
        bet = sb("bet", [P, D])
        nqmax = sb("nqmax", [P, NT])
        qsum = sb("qsum", [P, NT])
        rq = sb("rq", [P, NT])
        qe = sb("qe", [P, NT, D])
        v = sb("v", [P, NT, D])
        nkmax = sb("nkmax", [D, B])
        ksum = sb("ksum", [D, B])
        rk = sb("rk", [D, B])
        keT = sb("keT", [D, B, T])
        ke = sb("ke", [P, NT, D])
        qeT = sb("qeT", [D, B, T])
        ctxT = sb("ctxT", [D, B, D])
        cw = sb("cw", [D, B, D])
        xb = sb("xb", [P, NT, D])
        r = sb("r", [P, NT, D])

        loaded_w = sem("loaded_w")
        order, pool_order = sem("order"), sem("pool_order")
        qv_done, qmax_ready, v_ready, qe_ready = sem("qv_done"), sem("qmax_ready"), sem("v_ready"), sem("qe_ready")
        k_done, kmax_ready, ke_ready, ke_turned, ke_copied = sem("k_done"), sem("kmax_ready"), sem("ke_ready"), sem("ke_turned"), sem("ke_copied")
        q_turned, qT_copied = sem("q_turned"), sem("qT_copied")
        ctx_done, ctx_copied, cw_done, cw_ready, out_done, out_added = (
            sem("ctx_done"), sem("ctx_copied"), sem("cw_done"), sem("cw_ready"), sem("out_done"), sem("out_added"))

        block = ctx.enter_context(nc.Block())

        @block.sync
        def _(sp):
            for dst, src in ((wqv[:, 0:D], Wq), (wqv[:, D:2 * D], Wv), (wk[:], Wk), (wo[:], Wo)):
                sp.dma_start(dst, src).then_inc(loaded_w, 16)
            for dst, src in ((bov, bo), (gam, gamma), (bet, beta)):
                sp.dma_start(dst[:], src.partition_broadcast(P)).then_inc(loaded_w, 16)

        @block.gpsimd
        def _(pool):
            k.clear_past()
            pool.wait_ge(loaded_w, 112)
            pool.wait_ge(norm.xn_ready, NT)
            pool.tensor_tensor(xb[:], k.xn[:], bcast(bov[:, 0:1], (0, NT), (1, D)), ALU.add).then_inc(pool_order, 1)
            pool.tensor_tensor(k.x[:], k.x[:], bcast(bet[:, 0:1], (0, NT), (1, D)), ALU.add).then_inc(pool_order, 1)

        @block.scalar
        def _(act):
            norm.scalar_sqrt(act)
            norm.scalar_copy(act)
            for t in range(NT):
                act.wait_ge(qmax_ready, t + 1)
                act.wait_ge(v_ready, t + 1)
                act.activation(qe[:, t, :], k.bank[4 + t % 2][:, 0:D], ACT.Exp, bias=nqmax[:, t:t + 1], accum_out=qsum[:, t:t + 1]).then_inc(qe_ready, 1)
            for b in range(B):
                act.wait_ge(kmax_ready, b + 1)
                act.activation(keT[:, b, :], k.bank[6 + b % 2][:], ACT.Exp, bias=nkmax[:, b:b + 1], accum_out=ksum[:, b:b + 1]).then_inc(ke_ready, 1)
            for b in range(B):
                act.wait_ge(q_turned, b + 1)
                act.activation(qeT[:, b, :], k.bank[2 + b % 2][:], ACT.Copy).then_inc(qT_copied, 1)
            norm2.scalar_sqrt(act)

        @block.vector
        def _(dve):
            link = Link(dve, order)
            norm.vector(dve, link)
            for t in range(NT):
                bank = k.bank[4 + t % 2]
                dve.wait_ge(qv_done, t + 1)
                dve.tensor_reduce(nqmax[:, t:t + 1], bank[:, 0:D], AX_X, ALU.max, negate=True).then_inc(qmax_ready, 1)
                dve.tensor_copy(v[:, t, :], bank[:, D:2 * D]).then_inc(v_ready, 1)
            for b in range(B):
                dve.wait_ge(k_done, b + 1)
                dve.tensor_reduce(nkmax[:, b:b + 1], k.bank[6 + b % 2][:], AX_X, ALU.max, negate=True).then_inc(kmax_ready, 1)
            for b in range(B):
                dve.wait_ge(ke_turned, b + 1)
                dve.tensor_copy(ke[:, b * TPB:(b + 1) * TPB, :].rearrange("p j d -> p (j d)"), k.bank[b % 2][:]).then_inc(ke_copied, 1)
            dve.wait_ge(qe_ready, NT)
            dve.reciprocal(rq[:], qsum[:])
            dve.wait_ge(ke_ready, B)
            link(dve.reciprocal(rk[:], ksum[:]))
            dve.wait_ge(ctx_done, 1)
            dve.tensor_copy(ctxT[:].rearrange("p b d -> p (b d)"), k.bank[4][:]).then_inc(ctx_copied, 1)
            dve.wait_ge(cw_done, 1)
            for b in range(B):
                dve.tensor_scalar(cw[:, b, :], k.bank[5][:, b * D:(b + 1) * D], rk[:, b:b + 1], float(D) ** -0.5, ALU.mult, ALU.mult)\
                    .then_inc(cw_ready, 1)
            dve.wait_ge(pool_order, 2)
            for t in range(NT):
                dve.wait_ge(out_done, t // TPB + 1)
                last = dve.scalar_tensor_tensor(r[:, t, :], k.bank[6 + (t // TPB) % 2][:, (t % TPB) * D:(t % TPB + 1) * D], rq[:, t:t + 1], xb[:, t, :],
                                                ALU.mult, ALU.add)
                if t % TPB == TPB - 1:
                    last.then_inc(out_added, 1)
            dve.wait_ge(out_added, B)
            norm2.statistics(dve, link, r)
            dve.wait_ge(norm2.std_ready, 1)
            link(dve.reciprocal(norm2.rstd[:], norm2.std[:]))
            for t in range(NT):
                last = dve.tensor_scalar(r[:, t, :], r[:, t, :], norm2.mv[:, t, 0:1], norm2.rstd[:, t:t + 1], ALU.subtract, ALU.mult)
            link(last)
            link(dve.tensor_tensor(r[:], r[:], bcast(gam[:, 0:1], (0, NT), (1, D)), ALU.mult))
            dve.tensor_tensor(k.x[:], k.x[:], r[:], ALU.add)

        @block.tensor
        def _(pe):
            norm.tensor(pe)
            pe.wait_ge(loaded_w, 112)
            for t in range(NT):
                pe.wait_ge(norm.xnT_ready, t // TPB + 1)
                if t >= 2:
                    pe.wait_ge(qe_ready, t - 1)
                    pe.wait_ge(v_ready, t - 1)
                pe.matmul(k.bank[4 + t % 2][:, 0:2 * D], k.xnT[:, t * P:(t + 1) * P], wqv[:], start=True, stop=True).then_inc(qv_done, 1)
            for b in range(B):
                if b >= 2:
                    pe.wait_ge(ke_ready, b - 1)
                pe.matmul(k.bank[6 + b % 2][:], wk[:], k.xnT[:, b * T:(b + 1) * T], start=True, stop=True).then_inc(k_done, 1)
            for b in range(B):
                pe.wait_ge(qe_ready, (b + 1) * TPB)
                if b >= 2:
                    pe.wait_ge(qT_copied, b - 1)
                for j in range(TPB):
                    last = pe.transpose(k.bank[2 + b % 2][:, j * P:(j + 1) * P], qe[:, b * TPB + j, :], k.ident[:])
                last.then_inc(q_turned, 1)
            for b in range(B):
                pe.wait_ge(ke_ready, b + 1)
                if b >= 2:
                    pe.wait_ge(ke_copied, b - 1)
                for j in range(TPB):
                    last = pe.transpose(k.bank[b % 2][:, j * P:(j + 1) * P], keT[:, b, j * P:(j + 1) * P], k.ident[:])
                last.then_inc(ke_turned, 1)
            for b in range(B):
                pe.wait_ge(ke_copied, b + 1)
                pe.wait_ge(v_ready, NT)
                for j in range(TPB):
                    last = pe.matmul(k.bank[4][:, b * D:(b + 1) * D], v[:, b * TPB + j, :], ke[:, b * TPB + j, :], start=(j == 0), stop=(j == TPB - 1))
            last.then_inc(ctx_done, 1)
            pe.wait_ge(ctx_copied, 1)
            for b in range(B):
                last = pe.matmul(k.bank[5][:, b * D:(b + 1) * D], ctxT[:, b, :], wo[:], start=True, stop=True)
            last.then_inc(cw_done, 1)
            for b in range(B):
                pe.wait_ge(cw_ready, b + 1)
                pe.wait_ge(qT_copied, b + 1)
                if b >= 2:
                    pe.wait_ge(out_added, b - 1)
                for j in range(TPB):
                    last = pe.matmul(k.bank[6 + b % 2][:, j * D:(j + 1) * D], qeT[:, b, j * P:(j + 1) * P], cw[:, b, :], start=True, stop=True)
                last.then_inc(out_done, 1)



def layer_scan(k, tag, w_in, conv_w, conv_b, w_xproj, w_dt, b_dt, A_log, Dskip, w_out, ln_g, ln_b):
    nc = k.nc
    DI, N = A_log.shape
    TAPS = conv_w.shape[2]
    C = DI // P
    G2 = 4 // C
    UN = G2 * C
    Q, QB = N * UN, N * G2
    with ExitStack() as ctx:
        def sb(name, shape, dt=F32):
            return k.sb(f"{tag}_{name}", shape, dt, ctx)

        def sem(name):
            return k.sem(f"{tag}_{name}")

        norm = Norm(k, tag, ctx)
        norm2 = Norm(k, f"{tag}2", ctx)
        win = sb("win", [D, 2 * DI])
        cw = sb("cw", [P, C, TAPS])
        cols = sb("cols", [P, 3, C])
        lngb = sb("lngb", [D, 2])
        wx3 = sb("wx3", [P, C, 3, 2 * N])
        wdt = sb("wdt", [P, C, DI])
        wout = sb("wout", [P, C, D])
        A = sb("A", [P, C, N])
        z2 = sb("z2", [P, NT, D])
        xp = sb("xp", [P, C, B, TAPS - 1 + T])
        xc = sb("xc", [P, C, B, T])
        zs = sb("zs", [P, C, B, T])
        dt_ = sb("dt", [P, C, B, T])
        dtx = sb("dtx", [P, C, B, T])
        t1 = sb("t1", [3 * 2 * N, T], BF16)
        t2 = sb("t2", [3 * 2 * N, T], BF16)
        r1 = sb("r1", [3 * 2 * N, T])
        r2 = sb("r2", [3 * 2 * N, T])
        bc = sb("bc", [3 * 2 * N, B, T], BF16)
        spread = sb("spread", [3 * 2 * N, 2 * N, P], BF16)
        keep = sb("keep", [P, B, T])
        bsb = sb("bsb", [P, B, T])
        push = sb("push", [P, B, T])
        h = sb("h", [P, B, T])
        hc = sb("hc", [P, B, T])

        loaded_w = sem("loaded_w")
        order, pool_order, act_order, waited = sem("order"), sem("pool_order"), sem("act_order"), sem("waited")
        z2_ready, xz_done, xz_copied, conv_ready, xc_ready = sem("z2_ready"), sem("xz_done"), sem("xz_copied"), sem("conv_ready"), sem("xc_ready")
        bc_done, bc_ready, dt_done, dt_ready, soft_ready = sem("bc_done"), sem("bc_ready"), sem("dt_done"), sem("dt_ready"), sem("soft_ready")
        dtx_ready, skip_ready = sem("dtx_ready"), sem("skip_ready")
        b_done, b_copied, c_done, push_ready, keep_ready = sem("b_done"), sem("b_copied"), sem("c_done"), sem("push_ready"), sem("keep_ready")
        scanned, hc_ready, summed, gated = sem("scanned"), sem("hc_ready"), sem("summed"), sem("gated")
        out_done, added, x_ready = sem("out_done"), sem("added"), sem("x_ready")
        NW = 12

        block = ctx.enter_context(nc.Block())

        @block.sync
        def _(sp):
            sp.dma_start(win[:], w_in).then_inc(loaded_w, 16)
            sp.dma_start(cw[:], conv_w.rearrange("(c p) a k -> p c (a k)", p=P)).then_inc(loaded_w, 16)
            for i, v in enumerate((conv_b, b_dt, Dskip)):
                sp.dma_start(cols[:, i, :], v.rearrange("(c p) -> p c", p=P), allow_slow_non_contiguous=True).then_inc(loaded_w, 16)
            sp.dma_start(A[:], A_log.rearrange("(c p) n -> p c n", p=P)).then_inc(loaded_w, 16)
            for r in range(3):
                sp.dma_start(wx3[:, :, r, :], w_xproj.rearrange("(c p) n -> p c n", p=P)).then_inc(loaded_w, 16)
            sp.dma_start(wdt[:], w_dt.rearrange("(c p) n -> p c n", p=P)).then_inc(loaded_w, 16)
            sp.dma_start(wout[:], w_out.rearrange("(c p) n -> p c n", p=P)).then_inc(loaded_w, 16)
            sp.dma_start(lngb[:, 0:1], ln_g.rearrange("(d a) -> d a", a=1)).then_inc(loaded_w, 16)
            sp.dma_start(lngb[:, 1:2], ln_b.rearrange("(d a) -> d a", a=1)).then_inc(loaded_w, 16)

        @block.gpsimd
        def _(pool):
            k.clear_past()
            link = Link(pool, pool_order)
            link(pool.memset(xp[:, :, :, 0:TAPS - 1], 0.0))
            link(pool.memset(spread[:], 0.0))
            for part in range(3):
                link(pool.affine_select(out=spread[:], in_=spread[:], compare_op=ALU.not_equal, fill=1.0, base=-2 * N * part,
                                        pattern=[[-1, 2 * N], [0, P]], channel_multiplier=1))
            pool.wait_ge(norm.xn_ready, NT)
            pool.tensor_tensor(k.x[:], k.x[:], k.xn[:], ALU.add).then_inc(x_ready, 1)
            pool.wait_ge(dtx_ready, C)
            for g in range(B // G2):
                with pool.Fori(0, N) as n:
                    for i in range(UN):
                        q = g * Q + n * UN + i
                        pool.wait_ge(b_copied, g * QB + n * G2 + i // C + 1 + G2)
                        pool.wait_ge(scanned, q + 1)
                        pool.tensor_tensor(push[:, i, :], dtx[:, i % C, g * G2 + i // C, :], bsb[:, i // C, :], ALU.mult).then_inc(push_ready, 1)

        @block.scalar
        def _(act):
            link = Link(act, act_order)
            norm.scalar_sqrt(act)
            norm2.scalar_sqrt(act)
            act.wait_ge(loaded_w, 16 * (NW + 1))
            for g in range(B):
                act.wait_ge(norm2.turned, g + 1)
                act.activation(k.xnT[:, g * T:(g + 1) * T], k.bank[g][:], ACT.Identity, bias=lngb[:, 1:2], scale=lngb[:, 0:1])\
                   .then_inc(norm2.xnT_ready, 1)

            def silu(b):
                for c in range(C):
                    act.wait_ge(conv_ready, b * C + c + 1)
                    act.activation(xc[:, c, b, :], xc[:, c, b, :], ACT.Silu).then_inc(xc_ready, 1)

            act.wait_ge(pool_order, 1)
            for b in range(B):
                for m in range(2 * C):
                    i = b * 2 * C + m
                    act.wait_ge(xz_done, i + 1)
                    bank = k.bank[4 + i % 4]
                    if m < C:
                        act.activation(xp[:, m, b, TAPS - 1:], bank[:], ACT.Copy).then_inc(xz_copied, 1)
                    else:
                        act.activation(zs[:, m - C, b, :], bank[:], ACT.Silu).then_inc(xz_copied, 1)
                if b:
                    silu(b - 1)
            silu(B - 1)
            for b in range(B):
                for c in range(C):
                    i = b * C + c
                    act.wait_ge(dt_done, i + 1)
                    link(act.activation(dtx[:, c, b, :], k.bank[i % 4][:], ACT.Abs, bias=cols[:, 1, c:c + 1]))
                    act.activation(dtx[:, c, b, :], dtx[:, c, b, :], ACT.Exp, scale=-1.0).then_inc(dt_ready, 1)
            act.wait_ge(dt_ready, C * B)
            for c in range(C):
                act.activation(dtx[:, c, :, :], dtx[:, c, :, :], ACT.Ln, bias=1.0).then_inc(soft_ready, 1)
            link(act.activation(A[:].rearrange("p c n -> p (c n)"), A[:].rearrange("p c n -> p (c n)"), ACT.Exp))
            link(act.activation(A[:].rearrange("p c n -> p (c n)"), A[:].rearrange("p c n -> p (c n)"), ACT.Copy, scale=-1.0))
            act.wait_ge(dtx_ready, C)
            for g in range(B // G2):
                with act.Fori(0, N) as n:
                    for i in range(UN):
                        q = g * Q + n * UN + i
                        bb, c = i // C, i % C
                        if c == 0:
                            act.wait_ge(b_done, g * QB + n * G2 + bb + 1)
                            act.wait_ge(push_ready, q + C)
                            act.activation(bsb[:, bb, :], k.bank[4 + bb][:], ACT.Copy).then_inc(b_copied, 1)
                        act.wait_ge(scanned, q + 1)
                        act.sem_inc(waited, 1)
                        act.activation(keep[:, i, :], dt_[:, c, g * G2 + bb, :], ACT.Exp, scale=A[:, c, bass.ds(n, 1)]).then_inc(keep_ready, 1)

        @block.vector
        def _(dve):
            link = Link(dve, order)
            for s, m in ((scanned, UN), (summed, UN), (b_copied, G2), (hc_ready, UN), (push_ready, UN)):
                dve.sem_inc(s, m)
            norm.vector(dve, link)
            dve.wait_ge(norm.xn_ready, NT)
            norm2.statistics(dve, link, k.xn)
            dve.wait_ge(norm2.std_ready, 1)
            link(dve.reciprocal(norm2.rstd[:], norm2.std[:]))
            for t in range(NT):
                dve.tensor_scalar(z2[:, t, :], k.xn[:, t, :], norm2.mv[:, t, 0:1], norm2.rstd[:, t:t + 1],
                                  ALU.subtract, ALU.mult).then_inc(z2_ready, 1)
            dve.wait_ge(loaded_w, 16 * (NW + 1))
            dve.wait_ge(pool_order, 1)
            for b in range(B):
                for c in range(C):
                    dve.wait_ge(xz_copied, b * 2 * C + c + 1)
                    link(dve.tensor_scalar(xc[:, c, b, :], xp[:, c, b, 0:T], cw[:, c, 0:1], cols[:, 0, c:c + 1], ALU.mult, ALU.add))
                    for j in range(1, TAPS):
                        last = dve.scalar_tensor_tensor(xc[:, c, b, :], xp[:, c, b, j:j + T], cw[:, c, j:j + 1], xc[:, c, b, :], ALU.mult, ALU.add)
                        if j < TAPS - 1:
                            link(last)
                    last.then_inc(conv_ready, 1)
            for b in range(B):
                dve.wait_ge(bc_done, b + 1)
                if b:
                    dve.wait_ge(bc_ready, b)
                ps = k.bank[4 + b][0:3 * 2 * N, :]
                G = 2 * N
                link(dve.tensor_copy(t1[:], ps))
                link(dve.tensor_tensor(r1[:], ps, t1[:], ALU.subtract))
                link(dve.tensor_copy(t2[:], r1[:]))
                link(dve.tensor_tensor(r2[:], r1[:], t2[:], ALU.subtract))
                dve.tensor_copy(bc[0:G, b, :], t1[0:G, :])
                dve.tensor_copy(bc[G:2 * G, b, :], t2[G:2 * G, :])
                dve.tensor_copy(bc[2 * G:3 * G, b, :], r2[2 * G:3 * G, :]).then_inc(bc_ready, 1)
                for c in range(C):
                    i = b * C + c
                    dve.wait_ge(dt_done, i + 1)
                    dve.wait_ge(dt_ready, i + 1)
                    dve.tensor_scalar(dt_[:, c, b, :], k.bank[i % 4][:], cols[:, 1, c:c + 1], 0.0, ALU.add, ALU.max).then_inc(gated, 1)
            dve.wait_ge(gated, C * B)
            for c in range(C):
                dve.wait_ge(soft_ready, c + 1)
                link(dve.tensor_tensor(dt_[:, c, :, :], dt_[:, c, :, :], dtx[:, c, :, :], ALU.add))
                dve.tensor_tensor(dtx[:, c, :, :], dt_[:, c, :, :], xc[:, c, :, :], ALU.mult).then_inc(dtx_ready, 1)
            dve.wait_ge(dtx_ready, C)
            for c in range(C):
                dve.tensor_scalar(xc[:, c, :, :], xc[:, c, :, :], cols[:, 2, c:c + 1], None, ALU.mult).then_inc(skip_ready, 1)
            for g in range(B // G2):
                with dve.Fori(0, N) as n:
                    def scan(i):
                        q = g * Q + n * UN + i
                        dve.wait_ge(keep_ready, q + 1)
                        dve.wait_ge(push_ready, q + 1 + UN)
                        dve.wait_ge(hc_ready, q + 1)
                        dve.tensor_tensor_scan(h[:, i, :], keep[:, i, :], push[:, i, :], 0.0, ALU.mult, ALU.add).then_inc(scanned, 1)

                    def weigh(i):
                        q = g * Q + n * UN + i
                        dve.wait_ge(scanned, q + 1 + UN)
                        dve.wait_ge(c_done, g * QB + n * G2 + i // C + 1)
                        dve.wait_ge(summed, q + 1)
                        dve.tensor_tensor(hc[:, i, :], h[:, i, :], k.bank[6 + i // C][:], ALU.mult).then_inc(hc_ready, 1)

                    scan(0)
                    for i in range(1, UN):
                        scan(i)
                        weigh(i - 1)
                    weigh(UN - 1)
                dve.wait_ge(summed, (g + 1) * Q + UN)
                for i in range(UN):
                    c, b = i % C, g * G2 + i // C
                    dve.tensor_tensor(zs[:, c, b, :], zs[:, c, b, :], k.bank[i][:], ALU.mult).then_inc(gated, 1)
            dve.wait_ge(x_ready, 1)
            for g in range(B):
                dve.wait_ge(out_done, g + 1)
                xv = k.x[:, g * TPB:(g + 1) * TPB, :].rearrange("p j d -> p (j d)")
                dve.tensor_tensor(xv, xv, k.bank[4 + g % 4][:], ALU.add).then_inc(added, 1)

        @block.tensor
        def _(pe):
            norm2.tensor(pe, z2, z2_ready)
            pe.wait_ge(loaded_w, 16 * (NW + 1))
            for b in range(B):
                pe.wait_ge(norm2.xnT_ready, b + 1)
                for m in range(2 * C):
                    i = b * 2 * C + m
                    if i >= 4:
                        pe.wait_ge(xz_copied, i - 3)
                    pe.matmul(k.bank[4 + i % 4][:], win[:, m * P:(m + 1) * P], k.xnT[:, b * T:(b + 1) * T], start=True, stop=True).then_inc(xz_done, 1)
            pe.wait_ge(xz_copied, 2 * C * B)
            for b in range(B):
                pe.wait_ge(xc_ready, (b + 1) * C)
                for c in range(C):
                    last = pe.matmul(k.bank[4 + b][0:3 * 2 * N, :], wx3[:, c, :, :].rearrange("p r n -> p (r n)"), xc[:, c, b, :], start=(c == 0), stop=(c == C - 1))
                last.then_inc(bc_done, 1)
                for m in range(C):
                    i = b * C + m
                    if i >= 4:
                        pe.wait_ge(gated, i - 3)
                    for c in range(C):
                        last = pe.matmul(k.bank[i % 4][:], wdt[:, c, m * P:(m + 1) * P], xc[:, c, b, :], start=(c == 0), stop=(c == C - 1))
                    last.then_inc(dt_done, 1)
            pe.wait_ge(pool_order, 5)
            pe.wait_ge(bc_ready, B)
            pe.wait_ge(skip_ready, C)
            for g in range(B // G2):
                pe.wait_ge(gated, C * B + g * UN)

                def spread_b(n, bb):
                    pe.wait_ge(b_copied, g * QB + n * G2 + bb + 1)
                    sel = spread[:, bass.ds(n, 1), :].rearrange("r n p -> r (n p)")
                    pe.matmul(k.bank[4 + bb][:], sel, bc[:, g * G2 + bb, :], start=True, stop=True).then_inc(b_done, 1)

                def spread_c(n, bb):
                    pe.wait_ge(hc_ready, g * Q + n * UN + (bb + 1) * C)
                    sel = spread[:, bass.ds(n + N, 1), :].rearrange("r n p -> r (n p)")
                    pe.matmul(k.bank[6 + bb][:], sel, bc[:, g * G2 + bb, :], start=True, stop=True).then_inc(c_done, 1)

                def accumulate(n, i):
                    pe.wait_ge(hc_ready, g * Q + n * UN + i + 1 + UN)
                    pe.matmul(k.bank[i][:], k.ident[:], hc[:, i, :], start=False, stop=False, skip_group_check=True).then_inc(summed, 1)

                for bb in range(G2):
                    spread_b(0, bb)
                for bb in range(G2):
                    spread_c(0, bb)
                for i in range(UN):
                    pe.matmul(k.bank[i][:], k.ident[:], xc[:, i % C, g * G2 + i // C, :], start=True, stop=False, skip_group_check=True)
                with pe.Fori(0, N - 1) as n:
                    for i in range(UN):
                        if i % C == 0:
                            spread_b(n + 1, i // C)
                        if i % C == C - 1:
                            spread_c(n + 1, i // C)
                        accumulate(n, i)
                for i in range(UN):
                    accumulate(N - 1, i)
            pe.wait_ge(gated, C * B + C * B)
            for g in range(B):
                for j in range(TPB):
                    t = g * TPB + j
                    for c in range(C):
                        last = pe.matmul(k.bank[4 + g % 4][:, j * D:(j + 1) * D], zs[:, c, g, j * P:(j + 1) * P], wout[:, c, :], start=(c == 0), stop=(c == C - 1))
                last.then_inc(out_done, 1)



def layer_moe_tokens(k, tag, gate_weight, gate_bias, w_gate, w_up, w_down, s_gate, s_up, s_down, a_gate, a_up, a_down):
    nc = k.nc
    E, I = w_gate.shape[0], w_gate.shape[2]
    L, AI = a_gate.shape[0], a_gate.shape[2]
    SI = s_gate.shape[1]
    NG, TOPK, SCALE, ALPHA = 4, 6, 0.2, 0.1
    GE = E // NG
    ET, AT = E * I // P, L * AI // P
    TILES = ET + AT + 1
    EARLY = 3
    LATE = TILES - EARLY
    assert EARLY <= AT + 1 and LATE * P - E * I <= AT * P
    LOW, HIT = -1e30, 3e38
    STK = 3 * E + L
    with ExitStack() as ctx:
        def sb(name, shape, dt=F32):
            return k.sb(f"{tag}_{name}", shape, dt, ctx)

        def sem(name):
            return k.sem(f"{tag}_{name}")

        norm = Norm(k, tag, ctx)
        gw = sb("gw", [E, D])
        gwT = sb("gwT", [D, E])
        gb = sb("gb", [P, E])
        wg = sb("wg", [D, TILES * P])
        wu = sb("wu", [D, TILES * P])
        wd = sb("wd", [P, TILES, D])
        wg_high = sb("wg_high", [D, TILES * P], F32R)
        wu_high = sb("wu_high", [D, TILES * P], F32R)
        wg_low = sb("wg_low", [D, TILES * P], F32R)
        wu_low = sb("wu_low", [D, TILES * P], F32R)
        x_high = sb("x_high", [D, B * T], F32R)
        x_low = sb("x_low", [D, B * T], F32R)
        score = sb("score", [P, NT, E])
        sc = sb("sc", [P, NT, E])
        hi = sb("hi", [P, NT * NG, GE // 2])
        lo = sb("lo", [P, NT * NG, GE // 2])
        hi2 = sb("hi2", [P, NT * NG, GE // 4])
        lo2 = sb("lo2", [P, NT * NG, GE // 4])
        t2 = sb("t2", [P, NT * NG, GE // 4])
        top1 = sb("top1", [P, NT * NG])
        top2 = sb("top2", [P, NT * NG])
        gs = sb("gs", [P, NT, NG])
        wins = sb("wins", [P, NT, NG])
        duel = sb("duel", [P, 6, NT])
        gmask = sb("gmask", [P, NT, NG])
        masked = sb("masked", [P, NT, E])
        low = sb("low", [P, NT, E])
        best = sb("best", [P, NT, 8])
        only1 = sb("only1", [P, NT, 8])
        work = sb("work", [P, NT, E])
        work1 = sb("work1", [P, NT, E])
        total = sb("total", [P, NT])
        rtotal = sb("rtotal", [P, NT])
        cw = sb("cw", [P, NT, E])
        rest = sb("rest", [P, NT, E])
        stack = sb("stack", [P, NT, STK], BF16)
        stackT = sb("stackT", [STK, B * T], BF16)
        spread = sb("spread", [P, (ET + AT) * P], BF16)
        silu = k.xn[:, 0:2 * TPB, :].rearrange("p (s j) d -> p s (j d)", s=2)
        silu_e = sb("silu_e", [P, EARLY, B * T])
        up_e = sb("up_e", [P, EARLY, B * T])
        gated = k.xn[:, 2 * TPB:4 * TPB, :].rearrange("p (s j) d -> p s (j d)", s=2)
        hidden = sb("hidden", [P, 2, T])

        loaded_gw, loaded_early, loaded_in, loaded_w = sem("loaded_gw"), sem("loaded_early"), sem("loaded_in"), sem("loaded_w")
        x_high_ready, x_low_ready, high_ready, low_ready = sem("x_high_ready"), sem("x_low_ready"), sem("high_ready"), sem("low_ready")
        early_done, early_kept, early_spread = sem("early_done"), sem("early_kept"), sem("early_spread")
        order, spread_made = sem("order"), sem("spread_made")
        gwT_turned, gwT_ready = sem("gwT_turned"), sem("gwT_ready")
        logits_ready, score_ready = sem("logits_ready"), sem("score_ready")
        stack_ready, stack_turned, stackT_ready = sem("stack_ready"), sem("stack_turned"), sem("stackT_ready")
        in_ready, silu_ready, hidden_ready = sem("in_ready"), sem("silu_ready"), sem("hidden_ready")
        down_done, acc_used = sem("down_done"), sem("acc_used")

        block = ctx.enter_context(nc.Block())
        NE, NI, NW = 4, 2, 3

        @block.sync
        def _(sp):
            sp.dma_start(gw[:], gate_weight).then_inc(loaded_gw, 16)
            sp.dma_start(gb[:], gate_bias.partition_broadcast(P)).then_inc(loaded_gw, 16)
            for dst, l, s in ((wg, a_gate, s_gate), (wu, a_up, s_up)):
                sp.dma_start(dst[:, E * I:E * I + L * AI].rearrange("h (e i) -> h e i", i=AI),
                             l.rearrange("e h i -> h e i")).then_inc(loaded_early, 16)
                sp.dma_start(dst[:, E * I + L * AI:E * I + L * AI + SI], s).then_inc(loaded_early, 16)
            for dst, e in ((wg, w_gate), (wu, w_up)):
                sp.dma_start(dst[:, 0:E * I].rearrange("h (e i) -> h e i", i=I), e.rearrange("e h i -> h e i")).then_inc(loaded_in, 16)
            sp.dma_start(wd[:, 0:ET, :], w_down.rearrange("(t e) i d -> (e i) t d", e=P // I)).then_inc(loaded_w, 16)
            sp.dma_start(wd[:, ET:ET + AT, :], a_down.rearrange("(t e) i d -> (e i) t d", e=P // AI)).then_inc(loaded_w, 16)
            sp.dma_start(wd[0:SI, ET + AT, :], s_down).then_inc(loaded_w, 16)

        @block.gpsimd
        def _(pool):
            k.clear_past()
            link = Link(pool, spread_made)
            link(pool.memset(wg[:, TILES * P - (P - SI):], 0.0))
            link(pool.memset(wu[:, TILES * P - (P - SI):], 0.0))
            link(pool.memset(wd[SI:P, TILES - 1, :], 0.0))
            link(pool.memset(spread[:], 0.0))
            for part in range(3):
                v = spread[:, 0:ET * P].rearrange("r (e i) -> r e i", i=I)
                link(pool.affine_select(out=v, in_=v, compare_op=ALU.not_equal, fill=1.0, base=-E * part,
                                        pattern=[[-1, E], [0, I]], channel_multiplier=1))
            v = spread[:, ET * P:].rearrange("r (e i) -> r e i", i=AI)
            link(pool.affine_select(out=v, in_=v, compare_op=ALU.not_equal, fill=1.0, base=-3 * E,
                                    pattern=[[-1, L], [0, AI]], channel_multiplier=1))

            pool.wait_ge(loaded_early, 16 * NE)
            pool.wait_ge(spread_made, 8)
            for n, (t0, t1) in enumerate(((LATE, TILES), (0, LATE // 2), (LATE // 2, LATE))):
                piece = slice(t0 * P, t1 * P)
                if n == 1:
                    pool.wait_ge(loaded_in, 16 * NI)
                for raw, high in ((wu, wu_high), (wg, wg_high)):
                    last = pool.tensor_copy(high[:, piece], raw[:, piece])
                last.then_inc(high_ready, 1)
                pool.wait_ge(high_ready, n + 1)
                for raw, high, low in ((wu, wu_high, wu_low), (wg, wg_high, wg_low)):
                    last = pool.tensor_tensor(low[:, piece], raw[:, piece], high[:, piece].bitcast(F32), ALU.subtract)
                last.then_inc(low_ready, 1)

        @block.scalar
        def _(act):
            norm.scalar_sqrt(act)
            for g in range(B):
                act.wait_ge(norm.turned, g + 1)
                act.activation(k.xnT[:, g * T:(g + 1) * T], k.bank[g][:], ACT.Copy).then_inc(norm.xnT_ready, 1)
                act.activation(x_high[:, g * T:(g + 1) * T], k.bank[g][:], ACT.Copy).then_inc(x_high_ready, 1)
            act.wait_ge(logits_ready, 1)
            act.activation(score[:].rearrange("p j e -> p (j e)"), k.bank[5][:], ACT.Sigmoid).then_inc(score_ready, 1)
            for n in range(EARLY * B):
                i, c = n // B, n % B
                act.wait_ge(early_done, n + 1)
                act.activation(silu_e[:, i, c * T:(c + 1) * T], k.bank[n % 2][:], ACT.Silu)
                act.activation(up_e[:, i, c * T:(c + 1) * T], k.bank[2 + n % 2][:], ACT.Copy).then_inc(early_kept, 1)
            for g in range(2):
                act.wait_ge(stack_turned, g + 1)
                act.activation(stackT[:, g * 1024:(g + 1) * 1024], k.bank[6 + g][0:STK, :].bitcast(BF16), ACT.Copy)\
                   .then_inc(stackT_ready, 1)
            with act.Fori(0, B) as c:
                for t in range(LATE):
                    act.wait_ge(in_ready, c * LATE + t + 1)
                    act.wait_ge(hidden_ready, c * TILES + t + (1 if t else 2))
                    act.activation(silu[:, t % 2, :], k.bank[t % 2][:, :], ACT.Silu).then_inc(silu_ready, 1)

        @block.vector
        def _(dve):
            link = Link(dve, order)
            dve.sem_inc(hidden_ready, 2)
            dve.sem_inc(down_done, 2)
            dve.sem_inc(acc_used, 1)
            norm.vector(dve, link)
            dve.wait_ge(gwT_turned, 1)
            dve.tensor_copy(gwT[:], k.bank[4][:, 0:E]).then_inc(gwT_ready, 1)
            for g in range(B):
                dve.wait_ge(x_high_ready, g + 1)
                xg = slice(g * T, (g + 1) * T)
                dve.tensor_tensor(x_low[:, xg], k.xnT[:, xg], x_high[:, xg].bitcast(F32), ALU.subtract).then_inc(x_low_ready, 1)
            dve.wait_ge(loaded_gw, 32)
            dve.wait_ge(score_ready, 1)
            link(dve.tensor_tensor(sc[:], score[:], bcast(gb[:, 0:1], (0, NT), (1, E)), ALU.add))
            g8 = sc[:].rearrange("p j (g e) -> p (j g) e", e=GE)
            h = GE // 2
            dve.tensor_tensor(hi[:], g8[:, :, 0:h], g8[:, :, h:GE], ALU.max)
            link(dve.tensor_tensor(lo[:], g8[:, :, 0:h], g8[:, :, h:GE], ALU.min))
            q = h // 2
            dve.tensor_tensor(t2[:], hi[:, :, 0:q], hi[:, :, q:h], ALU.min)
            dve.tensor_tensor(lo2[:], lo[:, :, 0:q], lo[:, :, q:h], ALU.max)
            link(dve.tensor_tensor(hi2[:], hi[:, :, 0:q], hi[:, :, q:h], ALU.max))
            link(dve.tensor_tensor(lo2[:], lo2[:], t2[:], ALU.max))
            dve.tensor_tensor(top1[:], hi2[:, :, 0], hi2[:, :, 1], ALU.max)
            dve.tensor_tensor(t2[:, :, 0], hi2[:, :, 0], hi2[:, :, 1], ALU.min)
            link(dve.tensor_tensor(top2[:], lo2[:, :, 0], lo2[:, :, 1], ALU.max))
            link(dve.tensor_tensor(top2[:], top2[:], t2[:, :, 0], ALU.max))
            link(dve.tensor_tensor(gs[:].rearrange("p j g -> p (j g)"), top1[:], top2[:], ALU.add))
            pairs = [(a, b) for a in range(NG) for b in range(a + 1, NG)]
            dve.memset(wins[:], 0.0)
            for n, (a, b) in enumerate(pairs):
                last = dve.tensor_tensor(duel[:, n, :], gs[:, :, a], gs[:, :, b], ALU.is_ge)
            link(last)
            for n, (a, b) in enumerate(pairs):
                link(dve.tensor_tensor(wins[:, :, a], wins[:, :, a], duel[:, n, :], ALU.add))
                link(dve.scalar_tensor_tensor(wins[:, :, b], duel[:, n, :], -1.0, wins[:, :, b], ALU.mult, ALU.add))
            for g in range(NG):
                last = dve.tensor_scalar(gmask[:, :, g], wins[:, :, g], float(g), 2.0, ALU.add, ALU.is_ge)
            link(last)
            emask = bcast(gmask[:, 0, 0:1], (1, NT * NG), (0, GE))
            link(dve.tensor_scalar(low[:].rearrange("p j (g e) -> p (j g) e", e=GE), emask, -LOW, LOW, ALU.mult, ALU.add))
            link(dve.tensor_tensor(masked[:].rearrange("p j (g e) -> p (j g) e", e=GE), g8, emask, ALU.mult))
            link(dve.tensor_tensor(masked[:], masked[:], low[:], ALU.add))
            for j in range(NT):
                last = dve.max(best[:, j, :], masked[:, j, :])
            link(last)
            dve.memset(only1[:, :, 1:8], LOW)
            dve.tensor_copy(only1[:, :, 0], best[:, :, 0])
            link(dve.memset(best[:, :, TOPK:8], LOW))
            for j in range(NT):
                dve.match_replace(work[:, j, :], best[:, j, :], masked[:, j, :], HIT)
                last = dve.match_replace(work1[:, j, :], only1[:, j, :], masked[:, j, :], HIT)
            link(last)
            w8 = work[:].rearrange("p j (g e) -> p (j g) e", e=GE)
            w18 = work1[:].rearrange("p j (g e) -> p (j g) e", e=GE)
            dve.scalar_tensor_tensor(w8, w8, HIT, emask, ALU.is_equal, ALU.mult)
            link(dve.scalar_tensor_tensor(w18, w18, HIT, emask, ALU.is_equal, ALU.mult))
            dve.tensor_tensor(stack[:, :, 3 * E:], work1[:, :, 0::2], work1[:, :, 1::2], ALU.add)
            link(dve.tensor_tensor(cw[:], work[:], score[:], ALU.mult))
            link(dve.tensor_reduce(total[:], cw[:], AX_X, ALU.add))
            link(dve.tensor_scalar(total[:], total[:], 1e-20, None, ALU.add))
            link(dve.reciprocal(rtotal[:], total[:]))
            link(dve.scalar_tensor_tensor(cw[:], cw[:], SCALE, bcast(rtotal[:, 0:1], (1, NT), (0, E)), ALU.mult, ALU.mult))
            link(dve.tensor_copy(stack[:, :, 0:E], cw[:]))
            link(dve.tensor_tensor(rest[:], cw[:], stack[:, :, 0:E], ALU.subtract))
            link(dve.tensor_copy(stack[:, :, E:2 * E], rest[:]))
            link(dve.tensor_tensor(rest[:], rest[:], stack[:, :, E:2 * E], ALU.subtract))
            dve.tensor_copy(stack[:, :, 2 * E:3 * E], rest[:]).then_inc(stack_ready, 1)
            dve.wait_ge(early_kept, EARLY * B)
            with dve.Fori(0, B) as c:
                link.start(c, TILES - 1)
                for t in range(TILES):
                    wt = k.bank[4 + t % 2][:, :]
                    if t < LATE:
                        sl, up = silu[:, t % 2, :], k.bank[2 + t % 2][:, :]
                        dve.wait_ge(silu_ready, c * LATE + t + 1)
                    else:
                        sl, up = silu_e[:, t - LATE, bass.ds(c * T, T)], up_e[:, t - LATE, bass.ds(c * T, T)]
                        if t < TILES - 1:
                            dve.wait_ge(early_spread, c * (EARLY - 1) + t - LATE + 1)
                    dve.wait_ge(down_done, c * TILES + t + (1 if t else 2))
                    if t == TILES - 1:
                        dve.tensor_tensor(hidden[:, t % 2, :], sl, up, ALU.mult).then_inc(hidden_ready, 1)
                        continue
                    link(dve.scalar_tensor_tensor(gated[:, t % 2, :], sl, 1.0 if t < ET else ALPHA, up, ALU.mult, ALU.mult))
                    dve.tensor_tensor(hidden[:, t % 2, :], gated[:, t % 2, :], wt, ALU.mult).then_inc(hidden_ready, 1)
                dve.wait_ge(down_done, (c + 1) * TILES + 2)
                xc = k.x[:].rearrange("p j d -> p (j d)")[:, bass.ds(c * T, T)]
                dve.tensor_tensor(xc, xc, k.bank[6][:], ALU.add).then_inc(acc_used, 1)
                link.end(TILES - 1, B)

        @block.tensor
        def _(pe):
            def gate_up(bank, high, low, t, c):
                w, x = slice(t * P, (t + 1) * P), bass.ds(c * T, T)
                pe.matmul(bank[:], high[:, w], x_high[:, x], start=True, stop=False)
                pe.matmul(bank[:], high[:, w], x_low[:, x], start=False, stop=False)
                return pe.matmul(bank[:], low[:, w], x_high[:, x], start=False, stop=True)

            norm.tensor(pe)
            pe.wait_ge(loaded_gw, 32)
            pe.transpose(k.bank[4][:, 0:E], gw[:], k.ident[0:E, 0:E]).then_inc(gwT_turned, 1)
            pe.wait_ge(gwT_ready, 1)
            pe.wait_ge(norm.xnT_ready, B)
            for j in range(NT):
                last = pe.matmul(k.bank[5][:, j * E:(j + 1) * E], k.xnT[:, j * P:(j + 1) * P], gwT[:], start=True, stop=True)
            last.then_inc(logits_ready, 1)
            pe.wait_ge(x_low_ready, B)
            pe.wait_ge(low_ready, 1)
            for n in range(EARLY * B):
                i, c = n // B, n % B
                if n >= 2:
                    pe.wait_ge(early_kept, n - 1)
                gate_up(k.bank[2 + n % 2], wu_high, wu_low, LATE + i, c)
                gate_up(k.bank[n % 2], wg_high, wg_low, LATE + i, c).then_inc(early_done, 1)
            pe.wait_ge(stack_ready, 1)
            for j in range(NT):
                g, o = 6 + j // 8, j % 8
                last = pe.transpose(k.bank[g][0:STK, :].bitcast(BF16)[:, o * P:(o + 1) * P], stack[:, j, :], k.ident16[:])
                if o == 7:
                    last.then_inc(stack_turned, 1)
            pe.wait_ge(stackT_ready, 2)
            pe.wait_ge(loaded_w, 16 * NW)
            pe.wait_ge(early_kept, EARLY * B)
            pe.wait_ge(spread_made, 8)
            with pe.Fori(0, B) as c:
                wc = stackT[:, bass.ds(c * T, T)]

                def products(t):
                    if t == TILES - 1:
                        return
                    pe.wait_ge(hidden_ready, c * TILES + t + (1 if t else 2))
                    if t in (0, LATE // 2):
                        pe.wait_ge(low_ready, 3 if t else 2)
                    if t < LATE:
                        gate_up(k.bank[2 + t % 2], wu_high, wu_low, t, c)
                    spread_t = pe.matmul(k.bank[4 + t % 2][:], spread[0:STK, t * P:(t + 1) * P], wc, start=True, stop=True)
                    if t < LATE:
                        gate_up(k.bank[t % 2], wg_high, wg_low, t, c).then_inc(in_ready, 1)
                    else:
                        spread_t.then_inc(early_spread, 1)

                def down(t):
                    pe.wait_ge(hidden_ready, c * TILES + t + 3)
                    if t == 0:
                        pe.wait_ge(acc_used, c + 1)
                    for j in range(TPB):
                        last = pe.matmul(k.bank[6][:, j * D:(j + 1) * D], hidden[:, t % 2, j * P:(j + 1) * P],
                                         wd[:, t, :], start=(t == 0 and j == 0), stop=(t == TILES - 1), skip_group_check=True)
                    last.then_inc(down_done, 1)

                products(0)
                for t in range(TILES):
                    if t + 1 < TILES:
                        products(t + 1)
                    down(t)



def layer_delta(k, tag, Wq, Wk, Wv, Wb, conv_q, conv_k, conv_v, g, Wo):
    nc = k.nc
    H = Wb.shape[1]
    HD = D // H
    TAPS = conv_q.shape[2]
    CH = 64
    NCH = T // CH
    LEVELS = CH.bit_length() - 1
    with ExitStack() as ctx:
        def sb(name, shape, dt=F32):
            return k.sb(f"{tag}_{name}", shape, dt, ctx)

        def sem(name):
            return k.sem(f"{tag}_{name}")

        norm = Norm(k, tag, ctx)
        w3 = sb("w3", [D, 3, D])
        wb = sb("wb", [D, H])
        wbr = sb("wbr", [D, H, HD])
        wo = sb("wo", [D, D])
        cw = sb("cw", [P, 3, TAPS])
        gc = sb("gc", [P, 1])
        xp = sb("xp", [P, 3, B, TAPS - 1 + T])
        s3 = sb("s3", [P, 3, B, T])
        beta = sb("beta", [P, B, T])
        kb = sb("kb", [P, B, T])
        of_head = sb("of_head", [P, HD])
        to_head = sb("to_head", [P, P])
        root = sb("root", [P, 2, T])
        ones = sb("ones", [P, P])
        ident2 = sb("ident2", [P, P])
        masks = sb("masks", [P, LEVELS, P])
        kbn = sb("kbn", [P, NT, D])
        vbn = sb("vbn", [P, NT, D])
        aT = sb("aT", [P, B, T])
        cT = sb("cT", [P, B, T])
        m = sb("m", [P, B, T])
        mT = sb("mT", [P, B, T])
        xx = sb("xx", [P, B, T])
        wT = sb("wT", [P, B, T])
        prod = sb("prod", [P, T])
        ka = sb("ka", [P, B, NCH])
        kbv = sb("kbv", [P, B, NCH])
        sd = sb("sd", [P, B, NCH + 1])
        early = sb("early", [P, B, NCH, B])
        qk = sb("qk", [P, B, NCH, B])
        u0 = sb("u0", [P, B, NCH, B])
        sq = xx
        sq_k = wT
        uT = beta
        o = cT

        loaded_w = sem("loaded_w")
        order, pool_order = sem("order"), sem("pool_order")
        in_done, in_copied, conv_ready, act_ready = sem("in_done"), sem("in_copied"), sem("conv_ready"), sem("act_ready")
        wbr_ready, beta_done, beta_ready = sem("wbr_ready"), sem("beta_done"), sem("beta_ready")
        inv_ready, inv_spread = sem("inv_ready"), sem("inv_spread")
        sq_ready, norm_done, root_ready, unit_ready = sem("sq_ready"), sem("norm_done"), sem("root_ready"), sem("unit_ready")
        kb_ready, vb_ready, a_done, aT_ready = sem("kb_ready"), sem("vb_ready"), sem("a_done"), sem("aT_ready")
        n_turned, n_ready = sem("n_turned"), sem("n_ready")
        cT_ready, x_done, x_ready, y_done, yT_done, m_ready, mT_ready = (sem("cT_ready"), sem("x_done"), sem("x_ready"), sem("y_done"),
                                                                          sem("yT_done"), sem("m_ready"), sem("mT_ready"))
        t_ready, wu_done, w_copied, u_copied = sem("t_ready"), sem("wu_done"), sem("w_copied"), sem("u_copied")
        qk_ready, qk_done, o_ready, osq_ready, on_done, oroot_ready, on_ready, out_done = (
            sem("qk_ready"), sem("qk_done"), sem("o_ready"), sem("osq_ready"), sem("on_done"), sem("oroot_ready"), sem("on_ready"), sem("out_done"))
        NW = 5 + 3 + H

        block = ctx.enter_context(nc.Block())

        def flat(ap):
            return ap.rearrange("p b t -> p (b t)")

        @block.sync
        def _(sp):
            for i, w in enumerate((Wq, Wk, Wv)):
                sp.dma_start(w3[:, i, :], w).then_inc(loaded_w, 16)
            sp.dma_start(wb[:], Wb).then_inc(loaded_w, 16)
            sp.dma_start(wo[:], Wo).then_inc(loaded_w, 16)
            for i, w in enumerate((conv_q, conv_k, conv_v)):
                sp.dma_start(cw[:, i, :], w.rearrange("d a k -> d (a k)")).then_inc(loaded_w, 16)
            for h in range(H):
                sp.dma_start(gc[h * HD:(h + 1) * HD, :], g.rearrange("(d a) -> d a", a=1)).then_inc(loaded_w, 16)

        @block.gpsimd
        def _(pool):
            k.clear_past()
            link = Link(pool, pool_order)
            link(pool.memset(xp[:, :, :, 0:TAPS - 1], 0.0))
            link(pool.memset(ones[:], 1.0))
            hcol = of_head[:].rearrange("p (a h) -> p a h", h=H)
            link(pool.memset(of_head[:], 1.0))
            link(pool.affine_select(out=hcol, in_=hcol, compare_op=ALU.is_ge, fill=0.0, base=0, pattern=[[0, HD // H], [-HD, H]], channel_multiplier=1))
            link(pool.affine_select(out=hcol, in_=hcol, compare_op=ALU.is_ge, fill=0.0, base=HD - 1, pattern=[[0, HD // H], [HD, H]], channel_multiplier=-1))
            link(pool.memset(to_head[:], 0.0))
            for b in range(B):
                tv = to_head[:].rearrange("p (h d) -> p h d", d=HD)
                link(pool.affine_select(out=tv, in_=tv, compare_op=ALU.not_equal, fill=1.0, base=-HD * b, pattern=[[-1, H], [0, HD]], channel_multiplier=1))
            link(pool.memset(masks[:], 0.0))
            for l in range(LEVELS):
                s = 1 << l
                v = masks[:, l, :].rearrange("p (n a s) -> p n a s", a=2, s=s)[:, :, 1, :]
                link(pool.memset(v, 1.0))
                link(pool.affine_select(out=v, in_=v, compare_op=ALU.is_ge, fill=0.0, base=0, pattern=[[-2 * s, P // (2 * s)], [0, s]], channel_multiplier=1))
                link(pool.affine_select(out=v, in_=v, compare_op=ALU.is_ge, fill=0.0, base=s - 1, pattern=[[2 * s, P // (2 * s)], [0, s]], channel_multiplier=-1))
            link(pool.memset(sd[:, :, 0:1], 0.0))
            link(pool.memset(early[:], 1.0))
            link(pool.affine_select(out=early[:], in_=early[:], compare_op=ALU.is_ge, fill=0.0, base=0,
                                    pattern=[[1, B], [0, NCH], [-1, B]], channel_multiplier=0))
            link(pool.tensor_scalar(ident2[:], k.ident[:], 2.0, None, ALU.mult))
            for l in range(LEVELS):
                for b in range(B):
                    pool.wait_ge(aT_ready, b + 1)
                    if l:
                        pool.wait_ge(x_done, (l - 1) * B + b + 1)
                        if l == 1:
                            pool.wait_ge(mT_ready, b + 1)
                    pool.tensor_tensor(cT[:, b, :].rearrange("p (j i) -> p j i", i=P), aT[:, b, :].rearrange("p (j i) -> p j i", i=P),
                                       bcast(masks[:, l, 0:1], (0, TPB), (1, P)), ALU.mult).then_inc(cT_ready, 1)

        @block.scalar
        def _(act):
            norm.scalar_sqrt(act)
            norm.scalar_copy(act)

            def silu_and_squares(b):
                for i in range(3):
                    act.wait_ge(conv_ready, b * 3 + i + 1)
                    act.activation(s3[:, i, b, :], s3[:, i, b, :], ACT.Silu).then_inc(act_ready, 1)
                for i, squares in enumerate((sq, sq_k)):
                    act.wait_ge(act_ready, b * 3 + i + 1)
                    act.activation(squares[:, b, :], s3[:, i, b, :], ACT.Square).then_inc(sq_ready, 1)

            act.wait_ge(pool_order, 1)
            for b in range(B):
                for i in range(3):
                    n = b * 3 + i
                    act.wait_ge(in_done, n + 1)
                    act.activation(xp[:, i, b, TAPS - 1:], k.bank[4 + n % 4][:], ACT.Copy).then_inc(in_copied, 1)
                if b:
                    silu_and_squares(b - 1)
            silu_and_squares(B - 1)
            for b in range(B):
                act.wait_ge(beta_done, b + 1)
                act.activation(beta[:, b, :], k.bank[b][:], ACT.Sigmoid).then_inc(beta_ready, 1)
            for i in range(2):
                act.wait_ge(norm_done, i + 1)
                act.activation(root[:, i, :], k.bank[i][:], ACT.Sqrt).then_inc(root_ready, 1)
            for n in range(2 * B):
                act.wait_ge(n_turned, n + 1)
                dst = (kbn, vbn)[n // B]
                act.activation(dst[:, (n % B) * TPB:(n % B + 1) * TPB, :].rearrange("p j d -> p (j d)"), k.bank[n % 2][:], ACT.Copy).then_inc(n_ready, 1)
            for l in range(1, LEVELS):
                for b in range(B):
                    act.wait_ge(x_done, l * B + b + 1)
                    if l > 1:
                        act.wait_ge(yT_done, (l - 2) * B + b + 1)
                    act.activation(xx[:, b, :], k.bank[b % 2][:], ACT.Copy).then_inc(x_ready, 1)
            for b in range(B):
                act.wait_ge(wu_done, b + 1)
                act.activation(wT[:, b, :], k.bank[b % 2][:], ACT.Copy).then_inc(w_copied, 1)
            for b in range(B):
                act.wait_ge(o_ready, b + 1)
                act.activation(sq[:, b, :], o[:, b, :], ACT.Square).then_inc(osq_ready, 1)
            act.wait_ge(on_done, 1)
            act.activation(root[:, 0, :], k.bank[0][:], ACT.Sqrt, scale=1.0 / HD, bias=k.eps[:, 0:1]).then_inc(oroot_ready, 1)

        @block.vector
        def _(dve):
            link = Link(dve, order)
            norm.vector(dve, link)
            dve.wait_ge(loaded_w, 16 * NW)
            dve.tensor_copy(wbr[:], bcast(wb[:, 0:1], (1, H), (0, HD))).then_inc(wbr_ready, 1)
            for b in range(B):
                for i in range(3):
                    dve.wait_ge(in_copied, b * 3 + i + 1)
                    link(dve.tensor_scalar(s3[:, i, b, :], xp[:, i, b, 0:T], cw[:, i, 0:1], None, ALU.mult))
                    for j in range(1, TAPS):
                        last = dve.scalar_tensor_tensor(s3[:, i, b, :], xp[:, i, b, j:j + T], cw[:, i, j:j + 1], s3[:, i, b, :], ALU.mult, ALU.add)
                        if j < TAPS - 1:
                            link(last)
                    last.then_inc(conv_ready, 1)
            dve.wait_ge(act_ready, 3 * B)
            for i in range(2):
                dve.wait_ge(root_ready, i + 1)
                dve.reciprocal(root[:, i, :], root[:, i, :]).then_inc(inv_ready, 1)
            for n in range(2 * B):
                i, b = n // B, n % B
                dve.wait_ge(inv_spread, n + 1)
                dve.tensor_tensor(s3[:, i, b, :], s3[:, i, b, :], k.bank[4 + n % 4][:], ALU.mult).then_inc(unit_ready, 1)
            dve.wait_ge(unit_ready, 2 * B)
            for b in range(B):
                dve.wait_ge(beta_ready, b + 1)
                dve.tensor_tensor(kb[:, b, :], s3[:, 1, b, :], beta[:, b, :], ALU.mult).then_inc(kb_ready, 1)
            for b in range(B):
                dve.tensor_tensor(s3[:, 2, b, :], s3[:, 2, b, :], beta[:, b, :], ALU.mult).then_inc(vb_ready, 1)
            for b in range(B):
                dve.wait_ge(a_done, b + 1)
                dve.tensor_copy(aT[:, b, :], k.bank[4 + b % 2][:]).then_inc(aT_ready, 1)
            idb = bcast(k.ident[:, 0:1], (0, TPB), (1, P))
            for b in range(B):
                dve.wait_ge(x_done, b + 1)
                dve.wait_ge(cT_ready, b + 1)
                dve.tensor_tensor(m[:, b, :].rearrange("p (j i) -> p j i", i=P), idb, k.bank[b % 2][:].rearrange("p (j i) -> p j i", i=P), ALU.subtract)\
                    .then_inc(m_ready, 1)
                dve.tensor_tensor(mT[:, b, :].rearrange("p (j i) -> p j i", i=P), idb, cT[:, b, :].rearrange("p (j i) -> p j i", i=P), ALU.subtract)\
                    .then_inc(mT_ready, 1)
            for l in range(1, LEVELS):
                for b in range(B):
                    n = (l - 1) * B + b
                    dve.wait_ge(yT_done, n + 1)
                    dve.wait_ge(m_ready, l * B)
                    dve.wait_ge(mT_ready, l * B)
                    dve.tensor_tensor(m[:, b, :], m[:, b, :], k.bank[4 + b % 2][:], ALU.subtract).then_inc(m_ready, 1)
                    dve.tensor_tensor(mT[:, b, :], mT[:, b, :], k.bank[6 + b % 2][:], ALU.subtract).then_inc(mT_ready, 1)
            dve.wait_ge(mT_ready, LEVELS * B)
            id2 = bcast(ident2[:, 0:1], (0, TPB), (1, P))
            for b in range(B):
                mv = mT[:, b, :].rearrange("p (j i) -> p j i", i=P)
                dve.scalar_tensor_tensor(mv, mv, 3.0, id2, ALU.mult, ALU.subtract).then_inc(t_ready, 1)
            for b in range(B):
                dve.wait_ge(wu_done, b + 1)
                dve.tensor_copy(uT[:, b, :], k.bank[2 + b % 2][:]).then_inc(u_copied, 1)
            dve.wait_ge(u_copied, B)
            dve.wait_ge(w_copied, B)
            for src, dst in ((wT, ka), (uT, kbv)):
                for b in range(B):
                    link(dve.tensor_tensor(prod[:], s3[:, 1, b, :], src[:, b, :], ALU.mult))
                    link(dve.tensor_reduce(dst[:, b, :], prod[:].rearrange("p (n c) -> p n c", c=CH), AX_X, ALU.add))
            link(dve.tensor_scalar(ka[:], ka[:], -1.0, 1.0, ALU.mult, ALU.add))
            for b in range(B):
                last = dve.tensor_tensor_scan(sd[:, b, 1:NCH + 1], ka[:, b, :], kbv[:, b, :], 0.0, ALU.mult, ALU.add)
            link(last)
            def first(ap):
                return ap.rearrange("p b (n c) -> p b n c", c=CH)[:, :, :, 0:B]

            dve.tensor_tensor(qk[:], first(s3[:, 0, :, :]), first(s3[:, 1, :, :]), ALU.mult).then_inc(qk_ready, 1)
            for b in range(B):
                sdb = bcast(sd[:, b, 0:1], (1, NCH), (0, B))
                last = dve.tensor_tensor(u0[:, b, :, :], first(wT[:])[:, b], sdb, ALU.mult)
            link(last)
            link(dve.tensor_tensor(u0[:], first(uT[:]), u0[:], ALU.subtract))
            link(dve.tensor_tensor(u0[:], u0[:], early[:], ALU.mult))
            dve.wait_ge(qk_done, 1)
            link(dve.tensor_tensor(u0[:], u0[:], k.bank[4][:, 0:B * NCH * B].rearrange("p (b n c) -> p b n c", b=B, n=NCH), ALU.mult))
            for b in range(B):
                ov = o[:, b, :].rearrange("p (n c) -> p n c", c=CH)
                link(dve.tensor_tensor(ov, s3[:, 0, b, :].rearrange("p (n c) -> p n c", c=CH), bcast(sd[:, b, 0:1], (1, NCH), (0, CH)), ALU.mult))
                dve.tensor_tensor(ov[:, :, 0:B], ov[:, :, 0:B], u0[:, b, :, :], ALU.add).then_inc(o_ready, 1)
            dve.wait_ge(o_ready, B)
            dve.wait_ge(oroot_ready, 1)
            dve.reciprocal(root[:, 0, :], root[:, 0, :]).then_inc(inv_ready, 1)
            for b in range(B):
                dve.wait_ge(inv_spread, 2 * B + b + 1)
                dve.scalar_tensor_tensor(o[:, b, :], o[:, b, :], gc[:, 0:1], k.bank[4 + b][:], ALU.mult, ALU.mult).then_inc(on_ready, 1)
            for b in range(B):
                dve.wait_ge(out_done, b + 1)
                xv = k.x[:, b * TPB:(b + 1) * TPB, :].rearrange("p j d -> p (j d)")
                dve.tensor_tensor(xv, xv, k.bank[b][:], ALU.add)

        @block.tensor
        def _(pe):
            norm.tensor(pe)
            pe.wait_ge(loaded_w, 16 * NW)
            for b in range(B):
                pe.wait_ge(norm.xnT_ready, b + 1)
                for i in range(3):
                    n = b * 3 + i
                    if n >= 4:
                        pe.wait_ge(in_copied, n - 3)
                    pe.matmul(k.bank[4 + n % 4][:], w3[:, i, :], k.xnT[:, b * T:(b + 1) * T], start=True, stop=True).then_inc(in_done, 1)
            pe.wait_ge(wbr_ready, 1)
            for b in range(B):
                pe.matmul(k.bank[b][:], wbr[:].rearrange("p h d -> p (h d)"), k.xnT[:, b * T:(b + 1) * T], start=True, stop=True).then_inc(beta_done, 1)
            pe.wait_ge(pool_order, 2 + 3 + 1 + B)
            pe.wait_ge(in_copied, 3 * B)
            pe.wait_ge(beta_ready, B)

            def lengths(bank, squares, done):
                for b in range(B):
                    last = pe.matmul(bank[HD * b:HD * (b + 1), :], of_head[:], squares[:, b, :], start=True, stop=True, tile_position=(0, HD * b))
                last.then_inc(done, 1)

            def spread_inverse(i, b, bank):
                r = slice(HD * b, HD * b + H)
                pe.matmul(bank[:], to_head[r, :], root[r, i, :], start=True, stop=True, tile_position=(HD * b, 0)).then_inc(inv_spread, 1)

            pe.wait_ge(sq_ready, 2 * B)
            lengths(k.bank[0], sq, norm_done)
            lengths(k.bank[1], sq_k, norm_done)
            for n in range(2 * B):
                pe.wait_ge(inv_ready, n // B + 1)
                if n >= 4:
                    pe.wait_ge(unit_ready, n - 3)
                spread_inverse(n // B, n % B, k.bank[4 + n % 4])
            for n in range(2 * B):
                i, b = n // B, n % B
                pe.wait_ge((kb_ready, vb_ready)[i], b + 1)
                if n >= 2:
                    pe.wait_ge(n_ready, n - 1)
                for j in range(TPB):
                    src = (kb[:, b, j * P:(j + 1) * P], s3[:, 2, b, j * P:(j + 1) * P])[i]
                    last = pe.transpose(k.bank[n % 2][:, j * P:(j + 1) * P], src, k.ident[:])
                last.then_inc(n_turned, 1)
            pe.wait_ge(unit_ready, 2 * B)
            for b in range(B):
                if b >= 2:
                    pe.wait_ge(aT_ready, b - 1)
                for j in range(TPB):
                    c = slice(j * P, (j + 1) * P)
                    last = pe.matmul(k.bank[4 + b % 2][:, c], s3[:, 1, b, c], kb[:, b, c], start=True, stop=True)
                last.then_inc(a_done, 1)
            pe.wait_ge(n_ready, 2 * B)
            pe.wait_ge(aT_ready, B)
            for b in range(B):
                pe.wait_ge(cT_ready, b + 1)
                if b >= 2:
                    pe.wait_ge(m_ready, b - 1)
                for j in range(TPB):
                    c = slice(j * P, (j + 1) * P)
                    last = pe.transpose(k.bank[b % 2][:, c], cT[:, b, c], k.ident[:])
                last.then_inc(x_done, 1)
            for l in range(1, LEVELS):
                def cross(b):
                    pe.wait_ge(cT_ready, l * B + b + 1)
                    pe.wait_ge(m_ready, l * B if l == 1 else (l - 1) * B + b + 1)
                    if (l - 1) * B + b >= 2:
                        pe.wait_ge(x_ready, (l - 1) * B + b - 1)
                    for j in range(TPB):
                        c = slice(j * P, (j + 1) * P)
                        last = pe.matmul(k.bank[b % 2][:, c], cT[:, b, c], m[:, b, c], start=True, stop=True)
                    last.then_inc(x_done, 1)

                def close(b):
                    n = (l - 1) * B + b
                    pe.wait_ge(x_ready, n + 1)
                    pe.wait_ge(mT_ready, B + n if n >= B else B)
                    if n >= 2:
                        pe.wait_ge(mT_ready, B + n - 1)
                    for j in range(TPB):
                        c = slice(j * P, (j + 1) * P)
                        pe.matmul(k.bank[4 + b % 2][:, c], mT[:, b, c], xx[:, b, c], start=True, stop=True)
                    for j in range(TPB):
                        c = slice(j * P, (j + 1) * P)
                        last = pe.matmul(k.bank[6 + b % 2][:, c], xx[:, b, c], mT[:, b, c], start=True, stop=True)
                    last.then_inc(yT_done, 1)

                cross(0)
                for b in range(B):
                    if b + 1 < B:
                        cross(b + 1)
                    close(b)
            pe.wait_ge(x_ready, (LEVELS - 1) * B)
            for b in range(B):
                pe.wait_ge(t_ready, b + 1)
                if b >= 2:
                    pe.wait_ge(w_copied, b - 1)
                    pe.wait_ge(u_copied, b - 1)
                for src, bank in ((kbn, k.bank[b % 2]), (vbn, k.bank[2 + b % 2])):
                    for j in range(TPB):
                        c = slice(j * P, (j + 1) * P)
                        last = pe.matmul(bank[:, c], src[:, b * TPB + j, :], mT[:, b, c], start=True, stop=True)
                last.then_inc(wu_done, 1)
            pe.wait_ge(qk_ready, 1)
            pe.matmul(k.bank[4][:, 0:B * NCH * B], ones[:], qk[:].rearrange("p b n c -> p (b n c)"), start=True, stop=True).then_inc(qk_done, 1)
            pe.wait_ge(o_ready, B)
            pe.wait_ge(osq_ready, B)
            lengths(k.bank[0], sq, on_done)
            pe.wait_ge(inv_ready, 3)
            for b in range(B):
                spread_inverse(0, b, k.bank[4 + b])
            for b in range(B):
                pe.wait_ge(on_ready, b + 1)
                for j in range(TPB):
                    c = slice(j * P, (j + 1) * P)
                    last = pe.matmul(k.bank[b][:, c], o[:, b, c], wo[:], start=True, stop=True)
                last.then_inc(out_done, 1)


def build(nc, a, out):
    with ExitStack() as ctx:
        k = Core(nc, ctx)
        x_loaded, made = k.sem("x_loaded"), k.sem("made")
        with nc.Block() as block:
            @block.sync
            def _(sp):
                sp.dma_start(k.x[:], a["L0_attn_a_x"].rearrange("b (j p) d -> p (b j) d", p=P)).then_inc(x_loaded, 16)
                sp.wait_ge(x_loaded, 16)

            @block.gpsimd
            def _(pool):
                link = Link(pool, made)
                link(pool.memset(k.eps[:], LN_EPS))
                pool.memset(k.ident16[:], 0.0)
                link(pool.memset(k.ident[:], 0.0))
                for m in (k.ident, k.ident16):
                    pool.affine_select(out=m[:], in_=m[:], compare_op=ALU.not_equal, fill=1.0,
                                       base=0, pattern=[[-1, P]], channel_multiplier=1)
        l0a = [a[f"L0_attn_a_{n}"] for n in ("w_qkv", "b_qkv", "w_out", "b_out", "w1_rpe", "b1_rpe", "w2_rpe", "b2_rpe")]
        l0f = [a[f"L0_ffn_{n}"] for n in ("gate_w", "w1", "w2")]
        l0b = [a[f"L0_attn_b_{n}"] for n in ("Wq", "Wk", "Wv", "Wo", "bo", "gamma", "beta")]
        l1a = [a[f"L1_attn_a_{n}"] for n in ("w_in", "conv_w", "conv_b", "w_xproj", "w_dt", "b_dt", "A_log", "D", "w_out",
                                             "ln_g", "ln_b")]
        l1b = [a[f"L1_attn_b_{n}"] for n in ("Wq", "Wk", "Wv", "Wb", "conv_q", "conv_k", "conv_v", "g", "Wo")]
        l1f = [a[f"L1_ffn_{n}"] for n in ("gate_weight", "gate_bias", "w_gate", "w_up", "w_down", "shared_w_gate", "shared_w_up",
                                          "shared_w_down", "anchor_w_gate", "anchor_w_up", "anchor_w_down")]
        layers = [("la", layer_attention, l0a), ("lb", layer_moe_experts, l0f), ("lc", layer_linear_attention, l0b),
                  ("ld", layer_moe_experts, l0f), ("le", layer_scan, l1a), ("lf", layer_moe_tokens, l1f),
                  ("lg", layer_delta, l1b), ("lh", layer_moe_tokens, l1f)]
        for n in PHASES:
            tag, layer, args = layers[n]
            k.next_layer()
            layer(k, tag, *args)
        k.next_layer()
        stored = k.sem("stored")
        with nc.Block() as block:
            @block.sync
            def _(sp):
                sp.dma_start(out.rearrange("b (j p) d -> p (b j) d", p=P), k.x[:]).then_inc(stored, 16)
                sp.wait_ge(stored, 16)


_INS = ['L0_attn_a_x', 'L0_attn_a_w_qkv', 'L0_attn_a_b_qkv', 'L0_attn_a_w_out', 'L0_attn_a_b_out', 'L0_attn_a_w1_rpe',
        'L0_attn_a_b1_rpe', 'L0_attn_a_w2_rpe', 'L0_attn_a_b2_rpe', 'L0_attn_b_Wq', 'L0_attn_b_Wk', 'L0_attn_b_Wv',
        'L0_attn_b_Wo', 'L0_attn_b_bo', 'L0_attn_b_gamma', 'L0_attn_b_beta', 'L0_ffn_gate_w', 'L0_ffn_w1', 'L0_ffn_w2',
        'L1_attn_a_w_in', 'L1_attn_a_conv_w', 'L1_attn_a_conv_b', 'L1_attn_a_w_xproj', 'L1_attn_a_w_dt', 'L1_attn_a_b_dt',
        'L1_attn_a_A_log', 'L1_attn_a_D', 'L1_attn_a_w_out', 'L1_attn_a_ln_g', 'L1_attn_a_ln_b', 'L1_attn_b_Wq',
        'L1_attn_b_Wk', 'L1_attn_b_Wv', 'L1_attn_b_Wb', 'L1_attn_b_conv_q', 'L1_attn_b_conv_k', 'L1_attn_b_conv_v',
        'L1_attn_b_g', 'L1_attn_b_Wo', 'L1_ffn_gate_weight', 'L1_ffn_gate_bias', 'L1_ffn_w_gate', 'L1_ffn_w_up',
        'L1_ffn_w_down', 'L1_ffn_shared_w_gate', 'L1_ffn_shared_w_up', 'L1_ffn_shared_w_down', 'L1_ffn_anchor_w_gate',
        'L1_ffn_anchor_w_up', 'L1_ffn_anchor_w_down']


def kernel(**inputs):
    import numpy as _np
    import concourse.bacc as _bacc
    from concourse import mybir as _mybir
    from concourse.bass_utils import run_bass_kernel_spmd as _run

    nc = _bacc.Bacc("TRN2", target_bir_lowering=False, num_devices=1)
    arrays, args = {}, {}
    for name in _INS:
        arr = _np.ascontiguousarray(inputs[name])
        arrays[f"in_{name}_dram"] = arr
        args[name] = nc.dram_tensor(f"in_{name}_dram", arr.shape, _mybir.dt.from_np(arr.dtype), kind="ExternalInput").ap()
    out = nc.dram_tensor("out_0_dram", (4, 512, 128), _mybir.dt.float32, kind="ExternalOutput").ap()
    build(nc, args, out)
    r = _run(nc, [arrays], core_ids=[0])
    return r.results[0]["out_0_dram"]
```
